# Optimizing a Trainium2 kernel written in Bass

```python
import numpy as np
import jax
import jax.numpy as jnp

def _softmax(x, axis=-1):
    return jax.nn.softmax(x, axis=axis)

def _gelu(x):
    return jax.nn.gelu(x, approximate=True)

def _silu(x):
    return jax.nn.silu(x)

def _sigmoid(x):
    return jax.nn.sigmoid(x)

def _layernorm(x, axis=-1, eps=1e-05):
    m = jnp.mean(x, axis=axis, keepdims=True)
    v = jnp.var(x, axis=axis, keepdims=True)
    return (x - m) / jnp.sqrt(v + eps)

def _scatter_add(tgt, idx, src, axis=0):
    return tgt.at[idx].add(src)

def _segment_sum(src, seg, n):
    return jax.ops.segment_sum(src, seg, n)
kernel_name = 'mk_flamingo_gated_d1_seqx_r4_f73c15'

def setup_inputs(seed: int=0):
    np.random.seed(seed)
    _w = jnp.asarray

    def _rec_inputs():
        import jax
        import jax.numpy as jnp
        _rk = jax.random.key(seed)
        x = -0.000125 + 0.9999 * jax.random.normal(jax.random.fold_in(_rk, 1), (64, 128, 256), jnp.float32)
        _lenS = 128 - jax.random.randint(jax.random.fold_in(_rk, 7), (64,), 0, max(1, 128 // 4) + 1, jnp.int32)
        _lenS2 = 128 - jax.random.randint(jax.random.fold_in(_rk, 8), (64,), 0, max(1, 128 // 4) + 1, jnp.int32)
        _ctx_768P = jax.random.normal(jax.random.fold_in(_rk, 11), (64, 16, 192), jnp.float32)
        _ctx_768c = jax.random.dirichlet(jax.random.fold_in(_rk, 511), 0.3 * jnp.ones((16,), jnp.float32), (64, 128))
        _ctx_768t = jnp.einsum('bsk,bkd->bsd', _ctx_768c, _ctx_768P)
        _ctx_768t = _ctx_768t * jax.lax.rsqrt(jnp.mean(jnp.square(_ctx_768t)) + 1e-12) * 0.953939
        ctx_768 = 0.00272024 + 0.999456 * (_ctx_768t + 0.3 * jax.random.normal(jax.random.fold_in(_rk, 611), (64, 128, 192), jnp.float32))
        _g = jax.random.normal(jax.random.fold_in(_rk, 9001), (2, 1), jnp.float32)
        _g = jnp.sign(_g) * jnp.maximum(jnp.abs(_g), 1.0) + (_g == 0) * 1.0
        g_xattn = _g[0]
        g_ffn = _g[1]
        return (x, ctx_768, g_xattn, g_ffn)
    x, ctx_768, g_xattn, g_ffn = _rec_inputs()

    def _L0_xattn_setup():
        import jax, jax.numpy as jnp
        import numpy as np
        N_HEADS = 16
        DIM_EMBED = 256
        DIM_CROSS = 192
        DIM_HEAD = DIM_EMBED // N_HEADS
        key = jax.random.key(seed)
        ks = jax.random.split(key, 10)
        B, Sq, Sk = (8, 1024, 77)
        s_e = 1.0 / np.sqrt(DIM_EMBED)
        s_c = 1.0 / np.sqrt(DIM_CROSS)
        return {'x': jax.random.normal(ks[0], (B, Sq, DIM_EMBED), jnp.float32), 'y': jax.random.normal(ks[1], (B, Sk, DIM_CROSS), jnp.float32), 'wq': jax.random.normal(ks[2], (DIM_EMBED, DIM_EMBED), jnp.float32) * s_e, 'bq': jax.random.normal(ks[3], (DIM_EMBED,), jnp.float32) * 0.01, 'wk': jax.random.normal(ks[4], (DIM_CROSS, DIM_EMBED), jnp.float32) * s_c, 'bk': jax.random.normal(ks[5], (DIM_EMBED,), jnp.float32) * 0.01, 'wv': jax.random.normal(ks[6], (DIM_CROSS, DIM_EMBED), jnp.float32) * s_c, 'bv': jax.random.normal(ks[7], (DIM_EMBED,), jnp.float32) * 0.01, 'wo': jax.random.normal(ks[8], (DIM_EMBED, DIM_EMBED), jnp.float32) * s_e, 'bo': jax.random.normal(ks[9], (DIM_EMBED,), jnp.float32) * 0.01}
    _L0_xattn_all = _L0_xattn_setup()
    _L0_xattn_in = {k: v for k, v in _L0_xattn_all.items() if k in ('wq', 'bq', 'wk', 'bk', 'wv', 'bv', 'wo', 'bo')}
    del _L0_xattn_all

    def _L0_ffn_setup():
        import jax, jax.numpy as jnp
        import numpy as np
        B, K, D = (128, 32, 256)
        E = 32
        H = int(D * 0.25)

        def _rsqrt_uniform(key, shape, d):
            bound = d ** (-0.5)
            return jax.random.uniform(key, shape, jnp.float32, -bound, bound)
        key = jax.random.key(seed)
        ks = jax.random.split(key, 7)
        return {'x': jax.random.normal(ks[0], (B, K, D), jnp.float32), 'router_w': _rsqrt_uniform(ks[1], (E, D), D), 'router_b': _rsqrt_uniform(ks[2], (E,), D), 'weights1': _rsqrt_uniform(ks[3], (E, D, H), H), 'bias1': _rsqrt_uniform(ks[4], (E, H), H), 'weights2': _rsqrt_uniform(ks[5], (E, H, D), D), 'bias2': _rsqrt_uniform(ks[6], (E, D), D)}
    _L0_ffn_all = _L0_ffn_setup()
    _L0_ffn_in = {k: v for k, v in _L0_ffn_all.items() if k in ('router_w', 'router_b', 'weights1', 'bias1', 'weights2', 'bias2')}
    del _L0_ffn_all
    return {'x': x, 'ctx_768': ctx_768, 'g_xattn': g_xattn, 'g_ffn': g_ffn, 'L0_xattn_wq': _L0_xattn_in['wq'], 'L0_xattn_bq': _L0_xattn_in['bq'], 'L0_xattn_wk': _L0_xattn_in['wk'], 'L0_xattn_bk': _L0_xattn_in['bk'], 'L0_xattn_wv': _L0_xattn_in['wv'], 'L0_xattn_bv': _L0_xattn_in['bv'], 'L0_xattn_wo': _L0_xattn_in['wo'], 'L0_xattn_bo': _L0_xattn_in['bo'], 'L0_ffn_router_w': _L0_ffn_in['router_w'], 'L0_ffn_router_b': _L0_ffn_in['router_b'], 'L0_ffn_weights1': _L0_ffn_in['weights1'], 'L0_ffn_bias1': _L0_ffn_in['bias1'], 'L0_ffn_weights2': _L0_ffn_in['weights2'], 'L0_ffn_bias2': _L0_ffn_in['bias2']}

def reference(x, ctx_768, g_xattn, g_ffn, L0_xattn_wq, L0_xattn_bq, L0_xattn_wk, L0_xattn_bk, L0_xattn_wv, L0_xattn_bv, L0_xattn_wo, L0_xattn_bo, L0_ffn_router_w, L0_ffn_router_b, L0_ffn_weights1, L0_ffn_bias1, L0_ffn_weights2, L0_ffn_bias2):
    import jax
    import jax.numpy as jnp

    def _L0_xattn_ref(x, y, wq, bq, wk, bk, wv, bv, wo, bo):
        import jax, jax.numpy as jnp
        import numpy as np
        N_HEADS = 16
        DIM_EMBED = 256
        DIM_CROSS = 192
        DIM_HEAD = DIM_EMBED // N_HEADS
        B, Sq, E = x.shape
        H, D = (N_HEADS, DIM_HEAD)
        q = (x @ wq + bq).reshape(B, Sq, H, D).transpose(0, 2, 1, 3)
        k = (y @ wk + bk).reshape(B, -1, H, D).transpose(0, 2, 1, 3)
        v = (y @ wv + bv).reshape(B, -1, H, D).transpose(0, 2, 1, 3)
        scores = jnp.einsum('bhqd,bhkd->bhqk', q, k) / jnp.sqrt(jnp.asarray(D, x.dtype))
        attn = jax.nn.softmax(scores, axis=-1)
        out = jnp.einsum('bhqk,bhkd->bhqd', attn, v)
        out = out.transpose(0, 2, 1, 3).reshape(B, Sq, E)
        return out @ wo + bo

    def _L0_ffn_ref(x, router_w, router_b, weights1, bias1, weights2, bias2):
        import jax, jax.numpy as jnp
        import numpy as np
        B, K, D = (128, 32, 256)
        E = 32
        H = int(D * 0.25)

        def _rsqrt_uniform(key, shape, d):
            bound = d ** (-0.5)
            return jax.random.uniform(key, shape, jnp.float32, -bound, bound)
        b, k, d = x.shape
        x_flat = x.reshape(-1, d)
        n = x_flat.shape[0]
        logits = x_flat @ router_w.T + router_b
        routed_idx = jnp.argmax(logits, axis=-1)

        def expert_mlp(w1, b1, w2, b2):
            h = jax.nn.relu(x_flat @ w1 + b1)
            return jax.nn.relu(h @ w2 + b2)
        y_all = jax.vmap(expert_mlp)(weights1, bias1, weights2, bias2)
        out_flat = y_all[routed_idx, jnp.arange(n)]
        return out_flat.reshape(b, k, d)
    x = x + jnp.tanh(g_xattn[0]) * _L0_xattn_ref(_layernorm(x, axis=-1), ctx_768, L0_xattn_wq, L0_xattn_bq, L0_xattn_wk, L0_xattn_bk, L0_xattn_wv, L0_xattn_bv, L0_xattn_wo, L0_xattn_bo)
    x = x + jnp.tanh(g_ffn[0]) * _L0_ffn_ref(_layernorm(x, axis=-1), L0_ffn_router_w, L0_ffn_router_b, L0_ffn_weights1, L0_ffn_bias1, L0_ffn_weights2, L0_ffn_bias2)
    return x

_drawn_inputs = setup_inputs


def setup_inputs(seed=0):
    import zlib

    import numpy as np

    out = dict(_drawn_inputs(seed))
    spreads = {}
    factors = {'L0_xattn_bq': 21.483,
     'L0_xattn_bk': 64.0,
     'L0_xattn_bv': 3.998,
     'L0_xattn_bo': 4.152,
     'L0_ffn_bias1': 6.562}
    for name, (base, spread) in spreads.items():
        noise = np.random.default_rng([zlib.crc32(name.encode()), seed]).standard_normal(out[name].shape)
        drawn = base * np.exp(spread * noise) if base else spread * noise
        out[name] = jnp.asarray(drawn.astype(out[name].dtype))
    for name, factor in factors.items():
        out[name] = (out[name] * factor).astype(out[name].dtype)
    return out
```

```python
import concourse.bass as bass
from concourse import mybir
from concourse.alu_op_type import AluOpType as ALU
from contextlib import ExitStack

F32, F16, BF16 = mybir.dt.float32, mybir.dt.float16, mybir.dt.bfloat16
U32, I32 = mybir.dt.uint32, mybir.dt.int32
ACT = mybir.ActivationFunctionType
X = mybir.AxisListType.X

P = 128
BATCHES, D, DC = 64, 256, 192
HEADS, DH = 16, 16
E, H = 32, 64
GB = 4
GROUPS = BATCHES // GB
GT = GB * P
TOKENS = BATCHES * P
KT = D // P
HP = HEADS // 2
STACK = 3 * DH
CHUNKS = 16
CH = 4
NPT = 3
WS = 8.0
MS = 64.0
EPS = 1e-5
ROW = D + 4
REGION = TOKENS + 2 * P
PADS = (E // 2) * REGION
ROWS = PADS + P
TILES = TOKENS // P + E
NG = 8
NOBODY = 1 << 20
LOOP_END = GROUPS - 4
SLICE = E // GROUPS


class Group:

    def __init__(self, base, off):
        self.base, self.off = base, off
        self.par = off % 2

    def plus(self, d):
        return Group(self.base, self.off + d)

    def real(self):
        return not isinstance(self.base, int) or 0 <= self.off < GROUPS

    def index(self, scale=1, add=0):
        return self.base * (2 * scale) + (self.off * scale + add)

    def count(self, per, k=0):
        return self.index(per, k)

    def halved(self, per, k=0):
        return self.base * per + ((self.off // 2) * per + k)


def wait(eng, sem, value):
    if isinstance(value, int) and value <= 0:
        return
    eng.wait_ge(sem, value)


def build(nc, x, ctx_t, g2, wq, bq, wk, bk, wv, bv, wo, bo, rw, rb, w1, b1, w2, b2, out):
    es = ExitStack()
    with es:
        def sb(name, shape, dt=F32):
            return es.enter_context(nc.sbuf_tensor(name, shape, dt))

        def pb(name):
            return es.enter_context(nc.psum_tensor(name, [P, 512], F32))

        def sem(name):
            return es.enter_context(nc.semaphore(name))

        q_bounce = nc.dram_tensor("q_bounce", [2, P, 2, KT, GT], F16, kind="Internal").ap()
        k_bounce = nc.dram_tensor("k_bounce", [2, P, 2, KT, GT], F16, kind="Internal").ap()
        rows = nc.dram_tensor("expert_rows", [ROWS, ROW], F32, kind="Internal").ap()

        ident = sb("ident", [P, P])
        tri = sb("tri", [P, P], BF16)
        ones = sb("ones", [P, P], BF16)
        ones16 = sb("ones16", [2, P], F16)
        half = sb("half", [P, GB])
        rank_e = sb("rank_e", [P, GB, E])
        sign_e = sb("sign_e", [P, GB, E])
        base_e = sb("base_e", [P, E])
        run = sb("run", [P, E])
        wq_s = sb("wq_s", [P, 2, KT, D], F16)
        wk_s = sb("wk_s", [P, 2, 2, D], F16)
        wv_s = sb("wv_s", [P, 2, 2, D], F16)
        wo_s = sb("wo_s", [P, 2, KT, D], F16)
        rw_s = sb("rw_s", [P, 2, KT, E], F16)
        rw_raw = sb("rw_raw", [P, KT, E])
        rb4 = sb("rb4", [P, GB, E])
        bqk = sb("bqk", [P, 2, KT])
        bqk8 = sb("bqk8", [P, 2, KT])
        bvc = sb("bvc", [P, KT])
        bvb = sb("bvb", [P, KT, P])
        gbias = sb("gbias", [P, D])
        bo_b = sb("bo_b", [P, D])
        gate = sb("gate", [P, 2])
        tg = sb("tg", [P, 2])
        b1c = sb("b1c", [P, E])
        b2raw = sb("b2raw", [E, D])
        b2hl = sb("b2hl", [E, 2, D], F16)
        w1s = sb("w1s", [P, 2, E * KT * P], F16)
        w2s = sb("w2s", [P, 2, E * D], F16)
        w1r = sb("w1r", [P, SLICE * KT * H])
        w2r = sb("w2r", [P, SLICE * D])
        pad = sb("pad", [P, ROW])

        xin = sb("xin", [P, GB, D])
        xres = sb("xres", [P, GB, D])
        yin = sb("yin", [P, 2, GT])
        ys = sb("ys", [P, 3, GT], F16)
        st1 = sb("st1", [P, GB, 6])
        mv1 = sb("mv1", [P, GB, 2])
        ve1 = sb("ve1", [P, GB])
        rs1 = sb("rs1", [P, GB])
        nm1 = sb("nm1", [P, GB])
        xn = sb("xn", [P, GB, D])
        xt = sb("xt", [P, 2, KT, GT], F16)
        qs = sb("qs", [P, 2, KT, GT], F16)
        ks = sb("ks", [P, 2, KT, GT], F16)
        qstk = sb("qstk", [P, 2, HP, GT], F16)
        kstk = sb("kstk", [P, 2, HP, GT], F16)
        v = sb("v", [P, 2, GB * HEADS * 32])
        mx = sb("mx", [P, GB, HEADS])
        mrow = sb("mrow", [HEADS, 2, 2 * P], F16)
        pt = sb("pt", [P, NPT, CH * P])
        ot = sb("ot", [P, GB, 512])
        rec = sb("rec", [P, GB, HEADS])
        an = sb("an", [P, GB, D])
        wraw = an
        at = xt
        x2 = sb("x2", [P, 2, GB, ROW])
        st2 = sb("st2", [P, GB, 6])
        mv2 = sb("mv2", [P, GB, 2])
        ve2 = sb("ve2", [P, GB])
        nm2 = sb("nm2", [P, GB])
        xn2 = sb("xn2", [P, GB, D])
        x2t = sb("x2t", [P, 2, KT, GT], F16)
        lg = sb("lg", [P, GB, E])
        lmax = sb("lmax", [P, GB])
        pick = sb("pick", [P, GB, E])
        first = sb("first", [P, GB])
        hot = sb("hot", [P, 2, GB, E])
        hots = sb("hots", [P, 2, GB, E], BF16)
        posn = sb("posn", [P, GB, E])
        pos = sb("pos", [P, GB])
        posi = sb("posi", [P, GB], U32)
        ids = sb("ids", [P, GB], I32)

        cnt = sb("cnt", [P, E])
        til = sb("til", [P, E])
        end = sb("end", [P, E])
        zero_e = sb("zero_e", [P, E])
        zero_ids = sb("zero_ids", [P, GB], I32)
        eps_c = sb("eps_c", [P, GB])
        minus = sb("minus", [P, GB])
        group_c = sb("group_c", [P, GB], I32)
        carry_p = sb("carry_p", [P, 8])
        carry_v = sb("carry_v", [P, 4])
        jcol = sb("jcol", [P, 1])
        iota_e = sb("iota_e", [P, E])
        ecmp = sb("ecmp", [P, E])
        eidx = sb("eidx", [P, 2])
        ehot = sb("ehot", [P, E])
        etmp = sb("etmp", [P, 4, E])
        ered = sb("ered", [P, 4])
        trow = sb("trow", [1, 2, P], U32)
        prow = sb("prow", [1, E], U32)

        yin_flat = yin[:].rearrange("p a n -> p (a n)")
        gt = x2[:].rearrange("p a b n -> p (a b) n")
        yr = xn2[:, 0:2, :]
        yo = [buf[:, b, :] for buf in (xin, xn) for b in range(GB)]
        gn = yin_flat[:, 0:2 * D].rearrange("p (g n) -> p g n", g=2)
        hr = yin_flat[:, 2 * D:2 * D + 2 * P].rearrange("p (g n) -> p g n", g=2)
        b2s = qstk[0:2, :, :, :].rearrange("p a b n -> p (a b n)")
        gx = qs[:].rearrange("p a k t -> p (a k t)")[:, 0:4 * KT * P].rearrange("p (g a k t) -> p g a k t", g=2, a=2, k=KT)
        hs = ks[:].rearrange("p a k t -> p (a k t)")[:, 0:2 * P].rearrange("p (g t) -> p g t", g=2)

        S = [pb("S0"), pb("S1")]
        ST = [pb("ST0"), pb("ST1")]
        AV = [pb("AV0"), pb("AV1")]
        M = [pb("M0"), pb("M1")]

        names = """consts w_in w_raw8 w_hi w_lo g_in tanh_done wo_g wo_hi wo_lo bias_in bv_wide bvwo_ready
        gb_a gb_done dve_set pool_set b2_hi b2_lo b2_rows
        ln1_st ln1_mv ln1_sm xn_done y_hi y_t xt_ready xt_hi xt_lo q_ready q_hi q_lo k_ready k_hi k_lo
        v_ready v_done
        s_ready s_max mt_ready m_done st_ready exp_done av_ready av_out o_ready nrm_r nrm_done at_ready
        at_hi at_lo xb_done y_ready x2_done ln2_st ln2_mv ln2_sm xn2_done x2t_ready x2t_hi x2t_lo
        lg_ready lg_done route hot_done rk_ready rk_read rk_link pos_done ids_done
        ew_r8 ew_hi ew_lo y_written
        t_link t_cols t_tr t_rows
        f_norm f_t f_hi f_lo f_h f_hs f_hr f_hlo f_y f_yr f_out f_carry""".split()
        s_ = {n: sem(n) for n in names}
        x_in = [sem("x_in0"), sem("x_in1")]
        y_in = [sem("y_in0"), sem("y_in1")]
        xr_in = [sem("xr_in0"), sem("xr_in1")]
        ew_in = sem("ew_in")
        q_out = sem("q_out")
        k_out = sem("k_out")
        stk = [sem("stk0"), sem("stk1")]
        m_in = [sem("m_in0"), sem("m_in1")]
        scat = [sem("scat0"), sem("scat1")]
        pad_out = sem("pad_out")
        pads_done = sem("pads_done")
        t_in = [sem(f"t_in{n}") for n in range(NG)]
        t_out = [sem(f"t_out{n}") for n in range(NG)]

        block = es.enter_context(nc.Block())

        def schedule(eng, step):
            for n in range(-2, 2):
                step(Group(0, n))
            with eng.Fori(1, LOOP_END // 2) as it:
                step(Group(it, 0))
                step(Group(it, 1))
            for n in range(LOOP_END, GROUPS + 2):
                step(Group(0, n))

        def tiles_schedule(eng, fstep, lead):
            def known(t):
                def at_(d):
                    j = t + d
                    return (j, j % NG, j // NG) if 0 <= j < TILES else None
                return at_

            def looped(it, u):
                def at_(d):
                    j = u + d
                    return (it * NG + j, j % NG, it + (j // NG))
                return at_

            for t in range(-lead, NG):
                fstep(known(t))
            with eng.Fori(1, TILES // NG - 1) as it:
                for u in range(NG):
                    fstep(looped(it, u))
            for t in range(TILES - NG, TILES + 2):
                fstep(known(t))

        @block.sync
        def _(sp):
            sp.dma_start(wraw[:, 0:2, :], wq.rearrange("(t p) n -> p t n", p=P)).then_inc(s_["w_in"], 16)
            sp.dma_start(wraw[:, 2:4, :], wk.rearrange("(t p) n -> p t n", p=P)).then_inc(s_["w_in"], 16)

            def load_x(a):
                if not a.real():
                    return
                wait(sp, s_["xn_done"], a.count(1))
                sp.dma_start(xin[:, :, :],
                             x[bass.ds(a.index(GB), GB), :, :].rearrange("b p n -> p b n")).then_inc(x_in[a.par], 16)
                wait(sp, s_["y_hi"], a.count(3))
                sp.dma_start(yin[:, :, :],
                             ctx_t[:, bass.ds(a.index(GT), GT)].rearrange("(t p) n -> p t n", p=P)).then_inc(y_in[a.par], 16)

            load_x(Group(0, 0))
            sp.dma_start(gate[:, :], g2.partition_broadcast(P)).then_inc(s_["g_in"], 16)
            sp.dma_start(bqk[:, 0, :], bq).then_inc(s_["bias_in"], 16)
            sp.dma_start(bqk[:, 1, :], bk).then_inc(s_["bias_in"], 16)
            sp.dma_start(bvc[:, :], bv).then_inc(s_["bias_in"], 16)
            sp.dma_start(bo_b[:, :], bo.partition_broadcast(P)).then_inc(s_["bias_in"], 16)
            sp.dma_start(b1c[:, :], b1).then_inc(s_["bias_in"], 16)
            sp.dma_start(b2raw[:, :], b2).then_inc(s_["bias_in"], 16)
            sp.dma_start(rw_raw[:, :, :], rw.rearrange("(t p) n -> p t n", p=P)).then_inc(s_["bias_in"], 16)
            for b in range(GB):
                sp.dma_start(rb4[:, b, :], rb.partition_broadcast(P)).then_inc(s_["bias_in"], 16)
            wait(sp, s_["w_raw8"], 4)
            wait(sp, s_["w_lo"], 2)
            sp.dma_start(wraw[:, 0:2, :], wv.rearrange("(t p) n -> p t n", p=P)).then_inc(s_["w_in"], 16)
            sp.dma_start(wraw[:, 2:4, :], wo.rearrange("(t p) n -> p t n", p=P)).then_inc(s_["w_in"], 16)
            sp.wait_ge(s_["pool_set"], 1)
            sp.dma_start(rows[PADS:PADS + P, :], pad[:, :]).then_inc(pad_out, 16)
            sp.wait_ge(s_["dve_set"], 1)

            def step(s):
                a, n1, g = s.plus(2), s.plus(1), s
                if a.real():
                    wait(sp, s_["ew_r8"], a.count(2))
                    wait(sp, s_["ew_lo"], a.count(2))
                    sp.dma_start(w1r[:, :], w1[:, bass.ds(a.index(SLICE * KT * H), SLICE * KT * H)]).then_inc(ew_in, 16)
                    sp.dma_start(w2r[:, :], w2[:, bass.ds(a.index(SLICE * D), SLICE * D)]).then_inc(ew_in, 16)
                if n1.real():
                    for u in range(2):
                        wait(sp, s_["m_done"], n1.count(4, 2 * u + 2))
                        for par in range(2):
                            sp.dma_start(qstk[64 * par + STACK:64 * par + STACK + 1, n1.par, :, u * 256:u * 256 + 256],
                                         mrow[HP * par:HP * par + HP, u, :]).then_inc(m_in[n1.par], 16)
                if a.real():
                    for lo, split, bounce, done, stack, order in (
                            ("q_lo", qs, q_bounce, q_out, qstk, (0, 1, 0)),
                            ("k_lo", ks, k_bounce, k_out, kstk, (0, 0, 1))):
                        wait(sp, s_[lo], a.count(2, 2))
                        sp.dma_start(bounce[a.par, :, :, :, :], split[:, :, :, :]).then_inc(done, 16)
                        wait(sp, done, a.count(16, 16))
                        for par in range(2):
                            for r, part in enumerate(order):
                                sp.dma_start(stack[64 * par + DH * r:64 * par + DH * r + DH, a.par, :, :],
                                             bounce[a.par, :, part, par, :].rearrange("(j d) t -> d j t", d=DH)
                                             ).then_inc(stk[a.par], 16)

                load_x(s.plus(3))
                if n1.real():
                    wait(sp, s_["x2_done"], n1.count(2))
                    sp.dma_start(xres[:, :, :],
                                 x[bass.ds(n1.index(GB), GB), :, :].rearrange("b p n -> p b n")).then_inc(xr_in[n1.par], 16)

            schedule(sp, step)

            sp.wait_ge(s_["b2_lo"], 1)
            sp.wait_ge(s_["st_ready"], CHUNKS * GROUPS)
            for n in range(2):
                sp.dma_start(b2s[n:n + 1, :], b2hl[:, n, :]).then_inc(s_["b2_rows"], 16)
            sp.wait_ge(s_["t_rows"], 1)
            for e in range(E):
                r = sp.value_load(prow[0:1, e:e + 1], min_val=0, max_val=PADS)
                sp.dma_start(rows[bass.ds(r, P - 1), :], pad[0:P - 1, :]).then_inc(pads_done, 16)
            sp.wait_ge(pads_done, 16 * E)
            sp.wait_ge(pad_out, 16)
            wait(sp, scat[0], 16 * GB * GROUPS // 2)
            wait(sp, scat[1], 16 * GB * GROUPS // 2)

            def tile(j, n, lap):
                wait(sp, t_out[n], 16 * lap if isinstance(lap, int) else lap * 16)
                r = sp.value_load(trow[0:1, 1, bass.ds(j, 1)], min_val=0, max_val=PADS)
                sp.dma_start(gt[:, n, :], rows[bass.ds(r, P), :]).then_inc(t_in[n], 16)

            for j in range(NG):
                tile(j, j, 0)
            with sp.Fori(1, TILES // NG) as it:
                for n in range(NG):
                    tile(it * NG + n, n, it)
            for n in range(NG):
                wait(sp, t_out[n], 16 * TILES // NG)

        @block.gpsimd
        def _(pool):
            g_ = nc.gpsimd

            def carry(site):
                return g_.tensor_tensor(carry_p[:, site:site + 1], zero_e[:, 0:1], zero_e[:, 0:1], ALU.add)

            g_.memset(ident[:], 0.0)
            g_.memset(tri[:], 1.0)
            g_.memset(ones[:], 1.0)
            g_.memset(ones16[:], 1.0)
            g_.memset(half[:], -0.5)
            g_.memset(zero_e[:], 0.0)
            g_.memset(eps_c[:], EPS)
            g_.memset(minus[:], -1.0)
            g_.memset(group_c[:], GT)
            g_.memset(zero_ids[:], 0)
            g_.memset(hots[:], 0.0)
            g_.iota(rank_e[:], pattern=[[0, GB], [-1, E]], base=E, channel_multiplier=0, allow_small_or_imprecise_dtypes=True)
            g_.iota(iota_e[:], pattern=[[1, E]], base=0, channel_multiplier=0, allow_small_or_imprecise_dtypes=True)
            g_.iota(jcol[:], pattern=[[0, 1]], base=0, channel_multiplier=1, allow_small_or_imprecise_dtypes=True)
            g_.iota(ids[:], pattern=[[P, GB]], base=-GT, channel_multiplier=1)
            g_.iota(base_e[:].rearrange("p (i o) -> p i o", o=2), pattern=[[REGION, E // 2], [REGION - 1, 2]],
                    base=0, channel_multiplier=0, allow_small_or_imprecise_dtypes=True)
            g_.iota(sign_e[:].rearrange("p b (i o) -> p b i o", o=2), pattern=[[0, GB], [0, E // 2], [-2, 2]],
                    base=1, channel_multiplier=0, allow_small_or_imprecise_dtypes=True)
            g_.memset(v[:], 1.0)
            g_.memset(x2[:], 0.0)
            g_.memset(pad[:], 0.0).then_inc(s_["consts"], 1)
            pool.wait_ge(s_["consts"], 1)
            g_.memset(pad[:, D + 2:D + 3].bitcast(U32), NOBODY)
            g_.tensor_copy(run[:], base_e[:])
            g_.affine_select(out=tri[:], in_=tri[:], compare_op=ALU.is_gt, fill=0.0, base=0,
                             pattern=[[1, P]], channel_multiplier=-1)
            g_.affine_select(out=ident[:], in_=ident[:], compare_op=ALU.not_equal, fill=1.0, base=0,
                             pattern=[[1, P]], channel_multiplier=-1).then_inc(s_["pool_set"], 1)
            pool.wait_ge(s_["pool_set"], 1)

            def norm_scale(mv, st, ve, rs, nm, shift, k0):
                link = s_[st]
                g_.tensor_tensor(ve, mv[:, :, 1], eps_c[:], ALU.add).then_inc(link, 1)
                wait(pool, link, k0(1))
                g_.tensor_tensor(rs, ve, half[:], ALU.pow).then_inc(link, 1)
                wait(pool, link, k0(2))
                g_.tensor_tensor(nm, mv[:, :, 0], rs, ALU.mult).then_inc(link, 1)
                wait(pool, link, k0(3))
                g_.tensor_tensor(shift, nm, minus[:], ALU.mult).then_inc(link, 1)
                wait(pool, link, k0(4))

            def step(s):
                a, g, r = s.plus(2), s, s.plus(-2)
                if a.real():
                    wait(pool, y_in[a.par], a.halved(16, 16))
                    wait(pool, s_["v_ready"], a.count(2))
                    wait(pool, s_["k_ready"], a.count(2))
                    zeros = zero_e[:, 0:1].to_broadcast([P, GT])
                    g_.tensor_tensor(ys[:, 0, :], yin[:, 0, :], zeros, ALU.add).then_inc(s_["y_t"], 1)
                    g_.tensor_tensor(ys[:, 2, :], yin[:, 1, :], zeros, ALU.add).then_inc(s_["y_t"], 1)
                    wait(pool, s_["y_t"], a.count(2, 2))
                    g_.tensor_tensor(ys[:, 1, :], yin[:, 0, :], ys[:, 0, :], ALU.subtract).then_inc(s_["y_hi"], 1)
                    wait(pool, s_["y_hi"], a.count(3, 1))
                    g_.tensor_tensor(ys[H:P, 2, :], yin[H:P, 1, :], ys[H:P, 2, :], ALU.subtract).then_inc(s_["y_hi"], 2)
                    wait(pool, s_["y_hi"], a.count(3, 3))
                    wait(pool, s_["ln1_mv"], a.count(GB, GB))
                    norm_scale(mv1, "ln1_sm", ve1[:], rs1[:], nm1[:], ve1[:], lambda k: a.count(4, k))
                    wait(pool, s_["xt_ready"], a.count(2))
                    carry(s.par)
                    for b in range(GB):
                        last = g_.tensor_scalar(xn[:, b, :], xin[:, b, :], rs1[:, b:b + 1], ve1[:, b:b + 1],
                                                ALU.mult, ALU.add)
                    last.then_inc(s_["xn_done"], 1)
                if r.real():
                    wait(pool, s_["pos_done"], r.count(1, 1))
                    carry(2 + s.par)
                    for b in range(GB):
                        g_.indirect_dma_start(out=rows[:, :], out_offset=bass.IndirectOffsetOnAxis(ap=posi[:, b:b + 1], axis=0),
                                              in_=x2[:, r.par, b, :], in_offset=None).then_inc(scat[r.par], 16)
                if g.real():
                    wait(pool, xr_in[g.par], g.halved(16, 16))
                    if isinstance(g.base, int) and g.off == 0:
                        pool.wait_ge(s_["gb_done"], 1)
                    g_.tensor_tensor(xres[:, :, :], xres[:, :, :],
                                     gbias[:].unsqueeze(1).to_broadcast([P, GB, D]), ALU.add).then_inc(s_["xb_done"], 1)
                if a.real():
                    wait(pool, s_["ew_hi"], a.count(2, 2))
                    o1, n1 = a.index(SLICE * KT * P), SLICE * KT * P
                    g_.tensor_tensor(w1s[:, 1, bass.ds(o1, n1)].rearrange("p (c u n) -> p c u n", u=2, n=H),
                                     w1r[:].rearrange("p (c n) -> p c n", n=H).unsqueeze(2).to_broadcast([P, SLICE * KT, 2, H]),
                                     w1s[:, 0, bass.ds(o1, n1)].rearrange("p (c u n) -> p c u n", u=2, n=H),
                                     ALU.subtract).then_inc(s_["ew_lo"], 1)
                    o2, n2 = a.index(SLICE * D), SLICE * D
                    g_.tensor_tensor(w2s[:, 1, bass.ds(o2, n2)], w2r[:], w2s[:, 0, bass.ds(o2, n2)],
                                     ALU.subtract).then_inc(s_["ew_lo"], 1)
                if g.real():
                    wait(pool, s_["ln2_mv"], g.count(GB, GB))
                    if g.off >= 1 or not isinstance(g.base, int):
                        wait(pool, s_["ids_done"], g.count(2))
                    g_.tensor_tensor(ids[:], ids[:], group_c[:], ALU.add).then_inc(s_["ids_done"], 1)
                    norm_scale(mv2, "ln2_sm", ve2[:], x2[:, g.par, :, D], nm2[:], x2[:, g.par, :, D + 1], lambda k: g.count(4, k))
                    wait(pool, s_["ids_done"], g.count(2, 1))
                    g_.tensor_tensor(x2[:, g.par, :, D + 2].bitcast(I32), ids[:], zero_ids[:], ALU.add).then_inc(s_["ids_done"], 1)
                    wait(pool, s_["x2t_ready"], g.count(2))
                    carry(4 + s.par)
                    for b in range(GB):
                        last = g_.tensor_scalar(xn2[:, b, :], x2[:, g.par, b, 0:D], x2[:, g.par, b, D:D + 1],
                                                x2[:, g.par, b, D + 1:D + 2], ALU.mult, ALU.add)
                    last.then_inc(s_["xn2_done"], 1)

            schedule(pool, step)

            def two_tiles(n, lap):
                wait(pool, s_["f_carry"], lap * (NG // 2) + (n // 2 + 1))
                wait(pool, s_["f_out"], lap * NG + (n + 2))
                carry(6).then_inc(s_["f_carry"], 1)
                for m in (n, n + 1):
                    g_.indirect_dma_start(out=out, out_offset=bass.IndirectOffsetOnAxis(ap=gt[:, m, D + 2:D + 3].bitcast(U32), axis=0),
                                          in_=yo[m], in_offset=None, bounds_check=TOKENS - 1, oob_is_err=False
                                          ).then_inc(t_out[m], 16)

            carry(7).then_inc(s_["f_carry"], 1)
            with pool.Fori(0, TILES // NG) as it:
                for n in range(0, NG, 2):
                    two_tiles(n, it)

        @block.scalar
        def _(act):
            a_ = nc.scalar

            def scaled_split(n, dst):
                for t in range(2):
                    a_.activation(wraw[:, 2 * n + t, :], wraw[:, 2 * n + t, :], ACT.Copy, scale=WS).then_inc(s_["w_raw8"], 1)

            act.wait_ge(s_["g_in"], 16)
            a_.activation(tg[:], gate[:], ACT.Tanh).then_inc(s_["tanh_done"], 1)
            act.wait_ge(s_["w_in"], 32)
            scaled_split(0, wq_s)
            scaled_split(1, wk_s)
            act.wait_ge(s_["w_raw8"], 4)
            a_.copy(wq_s[:, 0, :, :], wraw[:, 0:2, :]).then_inc(s_["w_hi"], 1)
            a_.copy(wk_s[:, 0, :, :], wraw[:, 2:4, :]).then_inc(s_["w_hi"], 1)
            act.wait_ge(s_["bias_in"], 16 * 11)
            a_.activation(bqk8[:], bqk[:], ACT.Copy, scale=WS).then_inc(s_["w_hi"], 1)
            a_.activation(b2raw[:], b2raw[:], ACT.Copy, scale=WS).then_inc(s_["w_hi"], 1)
            a_.activation(rw_raw[:], rw_raw[:], ACT.Copy, scale=WS).then_inc(s_["w_hi"], 1)
            act.wait_ge(s_["w_hi"], 5)
            a_.copy(b2hl[:, 0, :], b2raw[:]).then_inc(s_["b2_hi"], 1)
            a_.copy(rw_s[:, 0, :, :], rw_raw[:]).then_inc(s_["b2_hi"], 1)
            a_.copy(bvb[:], bvc[:].unsqueeze(2).to_broadcast([P, KT, P])).then_inc(s_["bv_wide"], 1)
            act.wait_ge(s_["w_in"], 64)
            scaled_split(0, wv_s)
            act.wait_ge(s_["w_raw8"], 6)
            a_.copy(wv_s[:, 0, :, :], wraw[:, 0:2, :]).then_inc(s_["w_hi"], 1)
            act.wait_ge(s_["bvwo_ready"], 1)
            act.wait_ge(s_["tanh_done"], 1)
            a_.activation(wraw[:, 2:4, :], wraw[:, 2:4, :], ACT.Copy, scale=WS).then_inc(s_["w_raw8"], 1)
            act.wait_ge(s_["w_raw8"], 7)
            a_.activation(wraw[:, 2:4, :], wraw[:, 2:4, :], ACT.Identity, scale=tg[:, 0:1]).then_inc(s_["w_raw8"], 1)
            act.wait_ge(s_["w_raw8"], 8)
            a_.copy(wo_s[:, 0, :, :], wraw[:, 2:4, :]).then_inc(s_["w_hi"], 1)

            def exp_chunk(g, c):
                act.wait_ge(s_["st_ready"], g.count(CHUNKS, c + 1))
                wait(act, s_["av_ready"], g.count(CHUNKS, c + 1 - NPT))
                a_.activation(pt[:, c % NPT, :], ST[c % 2][:], ACT.Exp,
                              scale=0.25 / (WS * WS)).then_inc(s_["exp_done"], 1)

            def attn_out(g, b):
                act.wait_ge(s_["av_ready"], g.count(CHUNKS, 4 * b + 4))
                wait(act, s_["o_ready"], g.count(4))
                a_.copy(ot[:, b, :], AV[b % 2][:]).then_inc(s_["av_out"], 1)

            def max_row(n1, b):
                act.wait_ge(s_["mt_ready"], n1.count(4, b + 1))
                if b % 2 == 0:
                    prev = n1.plus(-1)
                    if prev.real():
                        wait(act, m_in[prev.par], prev.halved(64, 32 * (b // 2) + 32))
                a_.activation(mrow[:, b // 2, (b % 2) * P:(b % 2) * P + P], M[b % 2][0:HEADS, 0:P], ACT.Copy,
                              scale=-1.0 / MS).then_inc(s_["m_done"], 1)

            def step(s):
                a, n1, g, f = s.plus(2), s.plus(1), s, s.plus(-1)
                for c in range(CHUNKS):
                    if g.real():
                        exp_chunk(g, c)
                    if c % 4 == 2 and c > 4:
                        if g.real():
                            attn_out(g, c // 4 - 1)
                        if n1.real():
                            max_row(n1, c // 4 - 1)
                if g.real():
                    attn_out(g, 3)
                if n1.real():
                    max_row(n1, 3)
                if a.real():
                    act.wait_ge(ew_in, a.count(32, 32))
                    a_.activation(w1r[:], w1r[:], ACT.Copy, scale=WS).then_inc(s_["ew_r8"], 1)
                    a_.activation(w2r[:], w2r[:], ACT.Copy, scale=WS).then_inc(s_["ew_r8"], 1)
                    act.wait_ge(s_["ew_r8"], a.count(2, 2))
                    a_.copy(w1s[:, 0, bass.ds(a.index(SLICE * KT * P), SLICE * KT * P)].rearrange("p (c u n) -> p c u n", u=2, n=H),
                            w1r[:].rearrange("p (c n) -> p c n", n=H).unsqueeze(2).to_broadcast([P, SLICE * KT, 2, H])
                            ).then_inc(s_["ew_hi"], 1)
                    a_.copy(w2s[:, 0, bass.ds(a.index(SLICE * D), SLICE * D)], w2r[:]).then_inc(s_["ew_hi"], 1)
                    for t in range(KT):
                        act.wait_ge(s_["xt_ready"], a.count(2, t + 1))
                        wait(act, s_["y_ready"], a.count(2, -4))
                        a_.copy(xt[:, 0, t, :], M[t][:]).then_inc(s_["xt_hi"], 1)
                    for t in range(KT):
                        act.wait_ge(s_["q_ready"], a.count(2, t + 1))
                        wait(act, q_out, a.count(16))
                        a_.activation(qs[:, 0, t, :], ST[t][:], ACT.Identity, bias=bqk8[:, 0, t:t + 1]).then_inc(s_["q_hi"], 1)
                if f.real():
                    for t in range(KT):
                        act.wait_ge(s_["x2t_ready"], f.count(2, t + 1))
                        wait(act, s_["lg_ready"], f.count(1))
                        a_.copy(x2t[:, 0, t, :], AV[t][:]).then_inc(s_["x2t_hi"], 1)
                if a.real():
                    for t in range(KT):
                        act.wait_ge(s_["k_ready"], a.count(2, t + 1))
                        wait(act, k_out, a.count(16))
                        a_.activation(ks[:, 0, t, :], M[t][:], ACT.Identity, bias=bqk8[:, 1, t:t + 1]).then_inc(s_["k_hi"], 1)
                if g.real():
                    for t in range(KT):
                        act.wait_ge(s_["at_ready"], g.count(2, t + 1))
                        if a.real():
                            act.wait_ge(s_["q_ready"], a.count(2, 2))
                        a_.copy(at[:, 0, t, :], S[t][:]).then_inc(s_["at_hi"], 1)
                if a.real():
                    for t in range(2):
                        act.wait_ge(s_["v_ready"], a.count(2, t + 1))
                        wait(act, s_["av_ready"], a.count(CHUNKS, -CHUNKS))
                        vv = v[:, a.par, t * 1024:t * 1024 + 1024].rearrange("p (h d) -> p h d", d=32)[:, :, 0:DH]
                        a_.activation(vv, ST[t][:].rearrange("p (h d) -> p h d", d=DH), ACT.Copy,
                                      scale=1.0 / WS).then_inc(s_["v_done"], 1)

            schedule(act, step)

            act.wait_ge(s_["t_rows"], 1)

            def normed(t):
                j, n, lap = t
                act.wait_ge(t_in[n], lap * 16 + 16)
                wait(act, s_["f_t"], j + (-1))
                a_.activation(gn[:, n % 2, :], gt[:, n, 0:D], ACT.Identity, bias=gt[:, n, D + 1:D + 2],
                              scale=gt[:, n, D:D + 1]).then_inc(s_["f_norm"], 1)

            def moved_hi(t):
                j, n, lap = t
                act.wait_ge(s_["f_t"], j + 1)
                wait(act, s_["f_h"], j + (-1))
                a_.copy(gx[:, n % 2, 0, :, :], S[n % 2][:, 0:D].rearrange("p (k t) -> p k t", k=KT)).then_inc(s_["f_hi"], 1)

            def hidden(t):
                j, n, lap = t
                act.wait_ge(s_["f_h"], j + 1)
                wait(act, s_["f_y"], j + (-1))
                e = act.value_load(trow[0:1, 0, bass.ds(j, 1)], min_val=0, max_val=E - 1)
                a_.activation(hs[:, n % 2, :], ST[n % 2][:, 0:P], ACT.Relu, bias=b1c[:, bass.ds(e, 1)],
                              scale=1.0 / WS).then_inc(s_["f_hs"], 1)
                a_.activation(hr[H:P, n % 2, :], ST[n % 2][H:P, 0:P], ACT.Relu, bias=b1c[H:P, bass.ds(e, 1)],
                              scale=1.0 / WS).then_inc(s_["f_hr"], 1)

            def relu_out(t):
                j, n, lap = t
                act.wait_ge(s_["f_y"], j + 1)
                wait(act, s_["f_out"], j + (-1))
                a_.activation(yr[:, n % 2, :], AV[n % 2][:, 0:D], ACT.Relu, scale=1.0 / WS).then_inc(s_["f_yr"], 1)

            def fstep(at_):
                for d, stage in ((1, normed), (0, moved_hi), (-1, hidden), (-2, relu_out)):
                    t = at_(d)
                    if t is not None:
                        stage(t)

            tiles_schedule(act, fstep, lead=1)

        @block.vector
        def _(dve):
            v_ = nc.vector

            def carry(site):
                v_.tensor_copy(carry_v[:, site:site + 1], tg[:, 0:1])

            v_.memset(kstk[:], MS).then_inc(s_["dve_set"], 1)
            dve.wait_ge(s_["w_hi"], 2)
            v_.tensor_tensor(wq_s[:, 1, :, :], wraw[:, 0:2, :], wq_s[:, 0, :, :], ALU.subtract).then_inc(s_["w_lo"], 1)
            v_.tensor_tensor(wk_s[:, 1, :, :], wraw[:, 2:4, :], wk_s[:, 0, :, :], ALU.subtract).then_inc(s_["w_lo"], 1)
            dve.wait_ge(s_["b2_hi"], 2)
            v_.tensor_tensor(b2hl[:, 1, :], b2raw[:], b2hl[:, 0, :], ALU.subtract).then_inc(s_["b2_lo"], 1)
            v_.tensor_tensor(rw_s[:, 1, :, :], rw_raw[:], rw_s[:, 0, :, :], ALU.subtract).then_inc(s_["w_lo"], 1)
            dve.wait_ge(s_["w_hi"], 6)
            v_.tensor_tensor(wv_s[:, 1, :, :], wraw[:, 0:2, :], wv_s[:, 0, :, :], ALU.subtract).then_inc(s_["w_lo"], 1)
            dve.wait_ge(s_["bvwo_ready"], 1)
            v_.tensor_tensor(gbias[:], AV[0][:, 0:D], bo_b[:], ALU.add).then_inc(s_["gb_a"], 1)
            dve.wait_ge(s_["gb_a"], 1)
            dve.wait_ge(s_["tanh_done"], 1)
            v_.tensor_scalar(gbias[:], gbias[:], tg[:, 0:1], None, ALU.mult).then_inc(s_["gb_done"], 1)
            dve.wait_ge(s_["w_hi"], 7)
            v_.tensor_tensor(wo_s[:, 1, :, :], wraw[:, 2:4, :], wo_s[:, 0, :, :], ALU.subtract).then_inc(s_["w_lo"], 1)
            dve.wait_ge(s_["pool_set"], 1)

            def stats(src, st, mv, st_sem, mv_sem, g, k):
                for b in range(GB):
                    v_.bn_stats(st[:, b, :], src(b)).then_inc(s_[st_sem], 1)
                wait(dve, s_[st_sem], g.count(GB, GB))
                carry(2 * k + g.par)
                for b in range(GB):
                    v_.bn_aggr(mv[:, b, :], st[:, b, :]).then_inc(s_[mv_sem], 1)

            def max_chunk(n1, c):
                dve.wait_ge(s_["s_ready"], n1.count(CHUNKS, c + 1))
                if c % 4 == 0:
                    wait(dve, s_["mt_ready"], n1.count(4, c // 4 - 3))
                b, cc = c // 4, c % 4
                v_.reduce_max(mx[:, b, CH * cc:CH * cc + CH], S[c % 2][:].rearrange("p (h t) -> p h t", h=CH), X
                              ).then_inc(s_["s_max"], 1)

            def rank_post(r):
                link = s_["rk_link"]
                dve.wait_ge(s_["rk_ready"], r.count(1, 1))
                v_.tensor_tensor(posn[:], M[1][:, 0:GB * E].rearrange("p (b e) -> p b e", b=GB),
                                 run[:].unsqueeze(1).to_broadcast([P, GB, E]), ALU.add).then_inc(link, 1)
                dve.wait_ge(link, r.count(3, 1))
                v_.tensor_tensor(run[:], M[1][:, GB * E:GB * E + E], run[:], ALU.add).then_inc(s_["rk_read"], 1)
                v_.tensor_tensor(posn[:], posn[:], hot[:, r.par, :, :], ALU.mult).then_inc(link, 1)
                dve.wait_ge(link, r.count(3, 2))
                v_.reduce_sum(pos[:], posn[:], X).then_inc(link, 1)
                dve.wait_ge(link, r.count(3, 3))
                pr = r.plus(-1)
                if pr.real():
                    wait(dve, scat[pr.par], pr.halved(16 * GB, 16 * GB))
                v_.tensor_copy(posi[:], pos[:]).then_inc(s_["pos_done"], 1)
                dve.wait_ge(s_["rk_read"], r.count(1, 1))

            def lo_part(dst, src, hi, ready, n, done, bias=None):
                dve.wait_ge(s_[ready], n)
                if bias is None:
                    v_.tensor_tensor(dst, src, hi, ALU.subtract).then_inc(s_[done], 1)
                else:
                    v_.scalar_tensor_tensor(out=dst, in0=src, scalar=bias, in1=hi, op0=ALU.add,
                                            op1=ALU.subtract).then_inc(s_[done], 1)

            def route(f):
                link = s_["route"]
                dve.wait_ge(s_["lg_ready"], f.count(1, 1))
                v_.scalar_tensor_tensor(out=lg[:].rearrange("p b e -> p (b e)"), in0=S[0][:, 0:GB * E], scalar=1.0 / WS,
                                        in1=rb4[:].rearrange("p b e -> p (b e)"), op0=ALU.mult, op1=ALU.add
                                        ).then_inc(s_["lg_done"], 1)
                dve.wait_ge(s_["lg_done"], f.count(1, 1))
                v_.reduce_max(lmax[:], lg[:], X).then_inc(link, 1)
                dve.wait_ge(link, f.count(5, 1))
                v_.tensor_tensor(pick[:], lg[:], lmax[:].unsqueeze(2).to_broadcast([P, GB, E]), ALU.is_ge).then_inc(link, 1)
                dve.wait_ge(link, f.count(5, 2))
                v_.tensor_tensor(pick[:], pick[:], rank_e[:], ALU.mult).then_inc(link, 1)
                dve.wait_ge(link, f.count(5, 3))
                v_.reduce_max(first[:], pick[:], X).then_inc(link, 1)
                dve.wait_ge(link, f.count(5, 4))
                v_.tensor_tensor(hot[:, f.par, :, :], rank_e[:], first[:].unsqueeze(2).to_broadcast([P, GB, E]),
                                 ALU.is_equal).then_inc(link, 1)
                dve.wait_ge(link, f.count(5, 5))
                v_.tensor_tensor(hots[:, f.par, :, :], hot[:, f.par, :, :], sign_e[:], ALU.mult).then_inc(s_["hot_done"], 1)

            def step(s):
                a, n1, g, f, r = s.plus(2), s.plus(1), s, s.plus(-1), s.plus(-2)
                if a.real():
                    dve.wait_ge(x_in[a.par], a.halved(16, 16))
                    wait(dve, s_["xn_done"], a.count(1))
                    stats(lambda b: xin[:, b, :], st1, mv1, "ln1_st", "ln1_mv", a, 0)
                for c in range(CHUNKS):
                    if n1.real():
                        max_chunk(n1, c)
                    if c == 6 and r.real():
                        rank_post(r)
                if a.real():
                    for t in range(KT):
                        lo_part(xt[:, 1, t, :], M[t][:], xt[:, 0, t, :], "xt_hi", a.count(2, t + 1), "xt_lo")
                if g.real():
                    banks = [S[0], S[1], AV[0], AV[1]]
                    for b in range(GB):
                        bank = banks[b][:].rearrange("p (h d) -> p h d", d=32)
                        dve.wait_ge(s_["o_ready"], g.count(4, b + 1))
                        v_.reciprocal(rec[:, b, :], bank[:, :, DH]).then_inc(s_["nrm_r"], 1)
                        dve.wait_ge(s_["nrm_r"], g.count(4, b + 1))
                        if b == 0:
                            wait(dve, s_["at_ready"], g.count(2))
                        v_.tensor_tensor(an[:, b, :].rearrange("p (h d) -> p h d", d=DH), bank[:, :, 0:DH],
                                         rec[:, b, :].unsqueeze(2).to_broadcast([P, HEADS, DH]), ALU.mult
                                         ).then_inc(s_["nrm_done"], 1)
                if a.real():
                    for t in range(KT):
                        lo_part(qs[:, 1, t, :], ST[t][:], qs[:, 0, t, :], "q_hi", a.count(2, t + 1), "q_lo", bqk8[:, 0, t:t + 1])
                if f.real():
                    for t in range(KT):
                        lo_part(x2t[:, 1, t, :], AV[t][:], x2t[:, 0, t, :], "x2t_hi", f.count(2, t + 1), "x2t_lo")
                if a.real():
                    for t in range(KT):
                        lo_part(ks[:, 1, t, :], M[t][:], ks[:, 0, t, :], "k_hi", a.count(2, t + 1), "k_lo", bqk8[:, 1, t:t + 1])
                if g.real():
                    for t in range(KT):
                        lo_part(at[:, 1, t, :], S[t][:], at[:, 0, t, :], "at_hi", g.count(2, t + 1), "at_lo")
                    dve.wait_ge(s_["xb_done"], g.count(1, 1))
                    pg = g.plus(-2)
                    if pg.real():
                        wait(dve, scat[pg.par], pg.halved(16 * GB, 16 * GB))
                    for t in range(2):
                        dve.wait_ge(s_["y_ready"], g.count(2, t + 1))
                        v_.scalar_tensor_tensor(out=x2[:, g.par, 2 * t:2 * t + 2, 0:D],
                                                in0=M[t][:].rearrange("p (b n) -> p b n", b=2), scalar=1.0 / WS,
                                                in1=xres[:, 2 * t:2 * t + 2, :], op0=ALU.mult, op1=ALU.add
                                                ).then_inc(s_["x2_done"], 1)
                    dve.wait_ge(s_["x2_done"], g.count(2, 2))
                    wait(dve, s_["xn2_done"], g.count(1))
                    stats(lambda b: x2[:, g.par, b, 0:D], st2, mv2, "ln2_st", "ln2_mv", g, 1)
                if f.real():
                    route(f)

            schedule(dve, step)

            link, n = s_["t_link"], [0]

            def then(ins):
                n[0] += 1
                ins.then_inc(link, 1)
                dve.wait_ge(link, n[0])

            def floored(dst, src, add):
                then(v_.tensor_scalar(dst, src, float(add), 1.0 / P, ALU.add, ALU.mult))
                then(v_.tensor_scalar(dst, dst, -0.498, 8388608.0, ALU.add, ALU.add))
                then(v_.tensor_scalar(dst, dst, 8388608.0, None, ALU.subtract))

            dve.wait_ge(s_["rk_read"], GROUPS)
            then(v_.tensor_tensor(cnt[:], run[:], base_e[:], ALU.subtract))
            then(v_.tensor_tensor(cnt[:], cnt[:], sign_e[:, 0, :], ALU.mult))
            floored(til[:], cnt[:], P - 1)
            then(v_.tensor_tensor_scan(end[:], til[:], zero_e[:], 0.0, ALU.add, ALU.add))
            then(v_.tensor_scalar(ecmp[:], end[:], jcol[:, 0:1], None, ALU.is_le))
            then(v_.reduce_sum(eidx[:, 0:1], ecmp[:], X))
            then(v_.tensor_scalar(ehot[:], iota_e[:], eidx[:, 0:1], None, ALU.is_equal))
            then(v_.tensor_tensor(etmp[:, 3, :], end[:], til[:], ALU.subtract))
            then(v_.tensor_tensor(etmp[:, 0, :], etmp[:, 3, :], ehot[:], ALU.mult))
            then(v_.tensor_scalar(etmp[:, 3, :], sign_e[:, 0, :], -1.0, (P - 1) / 2.0, ALU.add, ALU.mult))
            then(v_.tensor_tensor(etmp[:, 3, :], etmp[:, 3, :], base_e[:], ALU.add))
            then(v_.tensor_tensor(etmp[:, 1, :], etmp[:, 3, :], ehot[:], ALU.mult))
            then(v_.tensor_tensor(etmp[:, 2, :], sign_e[:, 0, :], ehot[:], ALU.mult))
            then(v_.tensor_copy(etmp[:, 3, :], ehot[:]))
            then(v_.reduce_sum(ered[:], etmp[:], X))
            then(v_.tensor_scalar(eidx[:, 1:2], jcol[:], ered[:, 0:1], float(P), ALU.subtract, ALU.mult))
            then(v_.tensor_scalar(eidx[:, 1:2], eidx[:, 1:2], ered[:, 2:3], ered[:, 1:2], ALU.mult, ALU.add))
            then(v_.tensor_scalar(ered[:, 3:4], ered[:, 3:4], -float(PADS), float(PADS), ALU.mult, ALU.add))
            then(v_.tensor_tensor(eidx[:, 1:2], eidx[:, 1:2], ered[:, 3:4], ALU.add))
            v_.tensor_scalar(eidx[:, 0:1], eidx[:, 0:1], float(E - 1), None, ALU.min).then_inc(s_["t_cols"], 1)
            then(v_.tensor_scalar(etmp[:, 0, :], sign_e[:, 0, :], -1.0, (P - 2) / 2.0, ALU.add, ALU.mult))
            then(v_.tensor_tensor(etmp[:, 1, :], etmp[:, 0, :], run[:], ALU.add))
            then(v_.tensor_copy(prow[:], etmp[0:1, 1, :]))
            dve.wait_ge(s_["t_tr"], 1)
            v_.tensor_copy(trow[:].rearrange("p a b -> p (a b)"), M[0][0:1, 0:2 * P]).then_inc(s_["t_rows"], 1)

            def moved_lo(t):
                j, n, lap = t
                dve.wait_ge(s_["f_hi"], j + 1)
                v_.tensor_tensor(gx[:, n % 2, 1, :, :], S[n % 2][:, 0:D].rearrange("p (k t) -> p k t", k=KT),
                                 gx[:, n % 2, 0, :, :], ALU.subtract).then_inc(s_["f_lo"], 1)

            def hidden_lo(t):
                j, n, lap = t
                dve.wait_ge(s_["f_hr"], j + 1)
                v_.tensor_tensor(hs[H:P, n % 2, :], hr[H:P, n % 2, :], hs[H:P, n % 2, :], ALU.subtract
                                 ).then_inc(s_["f_hlo"], 1)

            def finish(t):
                j, n, lap = t
                dve.wait_ge(s_["f_yr"], j + 1)
                wait(dve, t_out[n], lap * 16)
                v_.scalar_tensor_tensor(out=yo[n], in0=yr[:, n % 2, :], scalar=tg[:, 1:2], in1=gt[:, n, 0:D],
                                        op0=ALU.mult, op1=ALU.add).then_inc(s_["f_out"], 1)

            def fstep(at_):
                for d, stage in ((0, moved_lo), (-1, hidden_lo), (-2, finish)):
                    t = at_(d)
                    if t is not None:
                        stage(t)

            tiles_schedule(dve, fstep, lead=0)

        @block.tensor
        def _(pe):
            t_ = nc.tensor
            pe.wait_ge(s_["bv_wide"], 1)
            pe.wait_ge(s_["w_in"], 64)
            for t in range(KT):
                last = t_.matmul(AV[0][:, 0:D], bvb[:, t, :], wraw[:, 2 + t, :], start=(t == 0), stop=(t == KT - 1))
            last.then_inc(s_["bvwo_ready"], 1)
            pe.wait_ge(s_["pool_set"], 1)
            pe.wait_ge(s_["w_lo"], 5)

            def scores(n1, c):
                b, cc = c // 4, c % 4
                if c == 0:
                    pe.wait_ge(stk[n1.par], n1.halved(16 * 12, 16 * 12))
                    wait(pe, s_["lg_done"], n1.count(1, -2))
                if c == 1:
                    wait(pe, s_["at_lo"], n1.count(2, -2))
                if c >= 2:
                    pe.wait_ge(s_["s_max"], n1.count(CHUNKS, c - 1))
                r0 = 64 * (cc // 2)
                for i in range(CH):
                    hp = CH * (cc % 2) + i
                    last = t_.matmul(S[c % 2][:, i * P:(i + 1) * P], qstk[r0:r0 + STACK, n1.par, hp, b * P:(b + 1) * P],
                                     kstk[r0:r0 + STACK, n1.par, hp, b * P:(b + 1) * P], start=True, stop=True)
                last.then_inc(s_["s_ready"], 1)

            def scores_t(g, c):
                b, cc = c // 4, c % 4
                if c == 0:
                    pe.wait_ge(m_in[g.par], g.halved(64, 64))
                    nv = g.plus(1)
                    pe.wait_ge(s_["v_done"], nv.count(2, 2) if nv.real() else 2 * GROUPS)
                if c >= 2:
                    pe.wait_ge(s_["exp_done"], g.count(CHUNKS, c - 1))
                r0 = 64 * (cc // 2)
                for i in range(CH):
                    hp = CH * (cc % 2) + i
                    last = t_.matmul(ST[c % 2][:, i * P:(i + 1) * P], kstk[r0:r0 + STACK + 1, g.par, hp, b * P:(b + 1) * P],
                                     qstk[r0:r0 + STACK + 1, g.par, hp, b * P:(b + 1) * P], start=True, stop=True)
                last.then_inc(s_["st_ready"], 1)

            def times_v(g, c):
                b, cc = c // 4, c % 4
                pe.wait_ge(s_["exp_done"], g.count(CHUNKS, c + 1))
                if cc == 0:
                    if b >= 2:
                        pe.wait_ge(s_["av_out"], g.count(4, b - 1))
                    else:
                        wait(pe, s_["x2t_lo"], g.count(2, -4 + b + 1))
                        wait(pe, s_["nrm_done"], g.count(4))
                for i in range(CH):
                    h = (b * HEADS + CH * cc + i) * 32
                    last = t_.matmul(AV[b % 2][32 * i:32 * i + 32, cc * P:(cc + 1) * P], v[:, g.par, h:h + 32],
                                     pt[:, c % NPT, i * P:(i + 1) * P], start=True, stop=True)
                last.then_inc(s_["av_ready"], 1)

            def max_t(n1, b):
                pe.wait_ge(s_["s_max"], n1.count(CHUNKS, 4 * b + 4))
                if b < 2:
                    wait(pe, s_["x2_done"], n1.count(2, -4 + b + 1))
                    if b == 1:
                        r = n1.plus(-3)
                        if r.real():
                            wait(pe, s_["pos_done"], r.count(1, 1))
                    kk = n1.plus(1)
                    pe.wait_ge(s_["k_lo"], n1.count(2, 2))
                else:
                    pe.wait_ge(s_["m_done"], n1.count(4, b - 1))
                t_.transpose(M[b % 2][0:HEADS, 0:P], mx[:, b, :], ident[:]).then_inc(s_["mt_ready"], 1)

            def ranks(r):
                pe.wait_ge(s_["hot_done"], r.count(1, 1))
                pe.wait_ge(s_["x2_done"], min_groups(r.plus(1), 2))
                nk = r.plus(3)
                pe.wait_ge(s_["k_lo"], nk.count(2, 2) if nk.real() else 2 * GROUPS)
                oh = hots[:, r.par, :, :].rearrange("p b e -> p (b e)")
                t_.matmul(M[1][:, 0:GB * E], tri[:], oh, start=True, stop=False)
                for b in range(1, GB):
                    last_b = b == GB - 1
                    t_.matmul(M[1][:, b * E:GB * E], ones[:], oh[:, 0:(GB - b) * E], start=False, stop=last_b)
                for b in range(GB):
                    last = t_.matmul(M[1][:, GB * E:GB * E + E], ones[:], oh[:, b * E:(b + 1) * E],
                                     start=(b == 0), stop=(b == GB - 1))
                last.then_inc(s_["rk_ready"], 1)

            def min_groups(g, per):
                return g.count(per, per) if g.real() else per * GROUPS

            def split_matmul(bank, pairs):
                for n, (w, m) in enumerate(pairs):
                    last = t_.matmul(bank, w, m, start=(n == 0), stop=(n == len(pairs) - 1))
                return last

            THREE = ((0, 0), (1, 0), (0, 1))

            def step(s):
                a, n1, g, f, r = s.plus(2), s.plus(1), s, s.plus(-1), s.plus(-2)
                for c in range(CHUNKS + 2):
                    if n1.real() and c < CHUNKS:
                        scores(n1, c)
                    if c == 2 and r.real():
                        ranks(r)
                    if g.real() and c < CHUNKS:
                        scores_t(g, c)
                    if g.real() and 1 <= c <= CHUNKS:
                        times_v(g, c - 1)
                    if n1.real() and c >= 5 and c % 4 == 1:
                        max_t(n1, c // 4 - 1)
                if a.real():
                    pe.wait_ge(s_["xn_done"], a.count(1, 1))
                    if n1.real():
                        pe.wait_ge(s_["m_done"], n1.count(4, 4))
                    for t in range(KT):
                        for b in range(GB):
                            last = t_.transpose(M[t][:, b * P:(b + 1) * P], xn[:, b, t * P:(t + 1) * P], ident[:])
                        last.then_inc(s_["xt_ready"], 1)
                if g.real():
                    banks = [S[0], S[1], AV[0], AV[1]]
                    wait(pe, s_["s_max"], CHUNKS * GROUPS if not n1.real() else n1.count(CHUNKS, CHUNKS))
                    pe.wait_ge(s_["av_out"], g.count(4, 4))
                    for b in range(GB):
                        for cc in range(4):
                            last = t_.transpose(banks[b][:, cc * P:(cc + 1) * P], ot[:, b, cc * P:(cc + 1) * P], ident[:])
                        last.then_inc(s_["o_ready"], 1)
                if a.real():
                    pe.wait_ge(s_["xt_lo"], a.count(2, 2))
                    if g.real():
                        pe.wait_ge(s_["exp_done"], g.count(CHUNKS, CHUNKS))
                    elif n1.real():
                        pe.wait_ge(s_["v_done"], n1.count(2, 2))
                    for m in range(2):
                        split_matmul(ST[m][:], [(wq_s[:, i, t, m * P:(m + 1) * P], xt[:, j, t, :])
                                                for t in range(KT) for i, j in THREE]).then_inc(s_["q_ready"], 1)
                if f.real():
                    pe.wait_ge(s_["xn2_done"], f.count(1, 1))
                    if g.real():
                        pe.wait_ge(s_["nrm_done"], g.count(4, 4))
                    for t in range(KT):
                        for b in range(GB):
                            last = t_.transpose(AV[t][:, b * P:(b + 1) * P], xn2[:, b, t * P:(t + 1) * P], ident[:])
                        last.then_inc(s_["x2t_ready"], 1)
                if a.real():
                    pe.wait_ge(s_["y_hi"], a.count(3, 3))
                    for m in range(2):
                        col = slice(m * P, (m + 1) * P)
                        split_matmul(M[m][:], [(wk_s[:, i, t, col], ys[:, j, :]) for i, t, j in
                                               ((0, 0, 0), (1, 0, 0), (0, 0, 1), (0, 1, 2), (1, 1, 2))]
                                     ).then_inc(s_["k_ready"], 1)
                if g.real():
                    pe.wait_ge(s_["nrm_done"], g.count(4, 4))
                    for t in range(KT):
                        for b in range(GB):
                            last = t_.transpose(S[t][:, b * P:(b + 1) * P], an[:, b, t * P:(t + 1) * P], ident[:])
                        last.then_inc(s_["at_ready"], 1)
                if a.real():
                    pe.wait_ge(s_["q_lo"], a.count(2, 2))
                    for b in range(GB):
                        tok = slice(b * P, (b + 1) * P)
                        last = split_matmul(ST[b // 2][:, (b % 2) * D:(b % 2) * D + D],
                                            [(ys[:, j, tok], wv_s[:, i, t, :]) for i, t, j in
                                             ((0, 0, 0), (1, 0, 0), (0, 0, 1), (0, 1, 2), (1, 1, 2))])
                        if b % 2:
                            last.then_inc(s_["v_ready"], 1)
                if g.real():
                    pe.wait_ge(s_["at_lo"], g.count(2, 2))
                    if a.real():
                        pe.wait_ge(s_["k_lo"], a.count(2, 2))
                    elif n1.real():
                        pe.wait_ge(s_["m_done"], n1.count(4, 4))
                    for b in range(GB):
                        tok = slice(b * P, (b + 1) * P)
                        last = split_matmul(M[b // 2][:, (b % 2) * D:(b % 2) * D + D],
                                            [(at[:, i, t, tok], wo_s[:, j, t, :]) for t in range(KT) for i, j in THREE])
                        if b % 2:
                            last.then_inc(s_["y_ready"], 1)
                if f.real():
                    pe.wait_ge(s_["x2t_lo"], f.count(2, 2))
                    for b in range(GB):
                        tok = slice(b * P, (b + 1) * P)
                        last = split_matmul(S[0][:, b * E:(b + 1) * E],
                                            [(x2t[:, i, t, tok], rw_s[:, j, t, :]) for t in range(KT) for i, j in THREE])
                    last.then_inc(s_["lg_ready"], 1)

            schedule(pe, step)

            pe.wait_ge(s_["t_cols"], 1)
            for n in range(2):
                last = t_.transpose(M[0][0:1, n * P:(n + 1) * P], eidx[:, n:n + 1], ident[:])
            last.then_inc(s_["t_tr"], 1)
            pe.wait_ge(s_["t_rows"], 1)
            pe.wait_ge(s_["ew_lo"], 2 * GROUPS)
            pe.wait_ge(s_["ew_hi"], 2 * GROUPS)
            pe.wait_ge(s_["b2_rows"], 32)

            def moved(t):
                j, n, lap = t
                pe.wait_ge(s_["f_norm"], j + 1)
                wait(pe, s_["f_lo"], j + (-1))
                for k in range(KT):
                    last = t_.transpose(S[n % 2][:, k * P:(k + 1) * P], gn[:, n % 2, k * P:(k + 1) * P], ident[:])
                last.then_inc(s_["f_t"], 1)

            def hidden(t, e):
                j, n, lap = t
                pe.wait_ge(s_["f_lo"], j + 1)
                wait(pe, s_["f_hr"], j + (-1))
                split_matmul(ST[n % 2][:, 0:P],
                             [(w1s[:, i, bass.ds(e * (KT * P) + k * P, P)], gx[:, n % 2, m, k, :])
                              for k in range(KT) for i, m in THREE]).then_inc(s_["f_h"], 1)

            def output(t, e):
                j, n, lap = t
                pe.wait_ge(s_["f_hlo"], j + 1)
                wait(pe, s_["f_yr"], j + (-1))
                cols = bass.ds(e * D, D)
                bank = AV[n % 2][:, 0:D]
                t_.matmul(bank, ones16[:], b2s[:, cols], start=True, stop=False)
                t_.matmul(bank, hs[:, n % 2, :], w2s[:, 0, cols], start=False, stop=False)
                t_.matmul(bank, hs[:, n % 2, :], w2s[:, 1, cols], start=False, stop=True).then_inc(s_["f_y"], 1)

            def fstep(at_):
                t0, t1, t2 = at_(0), at_(-1), at_(-2)
                if t0 is not None:
                    moved(t0)
                if t1 is not None:
                    hidden(t1, pe.value_load(trow[0:1, 0, bass.ds(t1[0], 1)], min_val=0, max_val=E - 1))
                if t2 is not None:
                    output(t2, pe.value_load(trow[0:1, 0, bass.ds(t2[0], 1)], min_val=0, max_val=E - 1))

            tiles_schedule(pe, fstep, lead=0)


def kernel(x, ctx_768, g_xattn, g_ffn, L0_xattn_wq, L0_xattn_bq, L0_xattn_wk, L0_xattn_bk, L0_xattn_wv, L0_xattn_bv,
           L0_xattn_wo, L0_xattn_bo, L0_ffn_router_w, L0_ffn_router_b, L0_ffn_weights1, L0_ffn_bias1,
           L0_ffn_weights2, L0_ffn_bias2):
    import numpy as np
    import concourse.bacc as bacc
    from concourse.bass_utils import run_bass_kernel_spmd

    def arr(a):
        return np.ascontiguousarray(np.asarray(a))

    def tail_twice(a):
        a = np.asarray(a)
        return np.ascontiguousarray(np.concatenate([a, a[P:DC]], axis=0))

    def twice(a):
        return np.concatenate([a, a], axis=0)

    w1 = np.asarray(L0_ffn_weights1)
    w2 = np.asarray(L0_ffn_weights2)
    arrays = {
        "x": arr(x),
        "ctx_t": tail_twice(np.asarray(ctx_768).reshape(TOKENS, DC).T),
        "g2": arr(np.concatenate([np.asarray(g_xattn), np.asarray(g_ffn)])),
        "wq": arr(L0_xattn_wq),
        "bq": arr(np.asarray(L0_xattn_bq).reshape(KT, P).T),
        "wk": tail_twice(L0_xattn_wk),
        "bk": arr(np.asarray(L0_xattn_bk).reshape(KT, P).T),
        "wv": tail_twice(L0_xattn_wv),
        "bv": arr(np.asarray(L0_xattn_bv).reshape(KT, P).T),
        "wo": arr(L0_xattn_wo),
        "bo": arr(L0_xattn_bo),
        "rw": arr(np.asarray(L0_ffn_router_w).T),
        "rb": arr(L0_ffn_router_b),
        "w1": arr(w1.reshape(E, KT, P, H).transpose(2, 0, 1, 3).reshape(P, E * KT * H)),
        "b1": arr(twice(np.asarray(L0_ffn_bias1).T)),
        "w2": arr(twice(w2.transpose(1, 0, 2).reshape(H, E * D))),
        "b2": arr(L0_ffn_bias2),
    }
    nc = bacc.Bacc("TRN2", target_bir_lowering=False, num_devices=1)
    args = [nc.dram_tensor(name, a.shape, mybir.dt.from_np(a.dtype), kind="ExternalInput").ap() for name, a in arrays.items()]
    out = nc.dram_tensor("out", (TOKENS, D), F32, kind="ExternalOutput").ap()
    build(nc, *args, out)
    r = run_bass_kernel_spmd(nc, [arrays], core_ids=[0])
    return r.results[0]["out"].reshape(BATCHES, P, D)
```

```python
import concourse.bass as bass
from concourse import mybir
from concourse.alu_op_type import AluOpType as ALU
from contextlib import ExitStack

F32, F16, BF16 = mybir.dt.float32, mybir.dt.float16, mybir.dt.bfloat16
U32, I32 = mybir.dt.uint32, mybir.dt.int32
ACT = mybir.ActivationFunctionType
X = mybir.AxisListType.X

P = 128
BATCHES, D, DC = 64, 256, 192
HEADS, DH = 16, 16
E, H = 32, 64
GB = 4
GROUPS = BATCHES // GB
GT = GB * P
TOKENS = BATCHES * P
KT = D // P
HP = HEADS // 2
STACK = 2 * 3 * DH
CHUNKS = 16
CH = 4
NPT = 2
WS = 8.0
MS = 64.0
EPS = 1e-5
ROW = D + 4
REGION = TOKENS + 2 * P
PADS = (E // 2) * REGION
ROWS = PADS + P
TILES = TOKENS // P + E
NG = 8
NOBODY = 1 << 20
LOOP_END = GROUPS - 4
SLICE = E // GROUPS


class Group:

    def __init__(self, base, off):
        self.base, self.off = base, off
        self.par = off % 2

    def plus(self, d):
        return Group(self.base, self.off + d)

    def real(self):
        return not isinstance(self.base, int) or 0 <= self.off < GROUPS

    def index(self, scale=1, add=0):
        return self.base * (2 * scale) + (self.off * scale + add)

    def count(self, per, k=0):
        return self.index(per, k)

    def halved(self, per, k=0):
        return self.base * per + ((self.off // 2) * per + k)


def wait(eng, sem, value):
    if isinstance(value, int) and value <= 0:
        return
    eng.wait_ge(sem, value)


def build(nc, x, ctx_t, g2, wq, bq, wk, bk, wv, bv, wo, bo, rw, rb, w1, b1, w2, b2, out):
    es = ExitStack()
    with es:
        def sb(name, shape, dt=F32):
            return es.enter_context(nc.sbuf_tensor(name, shape, dt))

        def pb(name):
            return es.enter_context(nc.psum_tensor(name, [P, 512], F32))

        def sem(name):
            return es.enter_context(nc.semaphore(name))

        q_image = nc.dram_tensor("q_image", [2, KT, 2, DH, HP, GT], F16, kind="Internal").ap()
        k_image = nc.dram_tensor("k_image", [2, KT, 2, DH, HP, GT], F16, kind="Internal").ap()
        rows = nc.dram_tensor("expert_rows", [ROWS, ROW], F32, kind="Internal").ap()

        ident = sb("ident", [P, P])
        tri = sb("tri", [P, P], BF16)
        ones = sb("ones", [P, P], BF16)
        ones16 = sb("ones16", [2, P], F16)
        half = sb("half", [P, GB])
        rank_e = sb("rank_e", [P, E])
        sign_e = sb("sign_e", [P, E])
        base_e = sb("base_e", [P, E])
        run = sb("run", [P, E])
        wq_s = sb("wq_s", [P, 2, KT, D], F16)
        wk_s = sb("wk_s", [P, 2, 2, D], F16)
        wv_s = sb("wv_s", [P, 2, 2, D], F16)
        wo_s = sb("wo_s", [P, 2, KT, D], F16)
        rw_s = sb("rw_s", [P, 2, KT, E], F16)
        rb_b = sb("rb_b", [P, E])
        bqk = sb("bqk", [P, 2, KT])
        bqk8 = sb("bqk8", [P, 2, KT])
        bvc = sb("bvc", [P, KT])
        gbias = sb("gbias", [P, D])
        gate = sb("gate", [P, 2])
        tg = sb("tg", [P, 2])
        b1c = sb("b1c", [P, E])
        b2hl = sb("b2hl", [E, 2, D], F16)
        w1s = sb("w1s", [P, 2, E * KT * P], F16)
        w2s = sb("w2s", [P, 2, E * D], F16)
        w1r = sb("w1r", [P, SLICE * KT * H])
        w2r = sb("w2r", [P, SLICE * D])
        pad = sb("pad", [P, ROW])

        xin = sb("xin", [P, GB, D])
        xres = sb("xres", [P, GB, D])
        yin = sb("yin", [P, 2, GT])
        ys = sb("ys", [P, 3, GT], F16)
        st1 = sb("st1", [P, GB, 6])
        mv1 = sb("mv1", [P, GB, 2])
        ve1 = sb("ve1", [P, GB])
        rs1 = sb("rs1", [P, GB])
        nm1 = sb("nm1", [P, GB])
        xn = sb("xn", [P, GB, D])
        xt = sb("xt", [P, 2, KT, GT], F16)
        qs = sb("qs", [P, 2, KT, GT], F16)
        ks = sb("ks", [P, 2, KT, GT], F16)
        qstk = sb("qstk", [P, 2, HP, GT], F16)
        kstk = sb("kstk", [P, 2, 2, HP, GT], F16)
        v = sb("v", [P, 2, GB * HEADS * 32])
        mx = sb("mx", [P, GB, HEADS])
        mrow = sb("mrow", [HEADS, GT], F16)
        pt = sb("pt", [P, NPT, CH * P])
        ot = sb("ot", [P, GB, 512])
        rec = sb("rec", [P, GB, HEADS])
        an = ot[:, :, 0:D]
        at = xt
        x2 = sb("x2", [P, 2, GB, ROW])
        st2 = sb("st2", [P, GB, 6])
        mv2 = sb("mv2", [P, GB, 2])
        ve2 = sb("ve2", [P, GB])
        nm2 = sb("nm2", [P, GB])
        xn2 = sb("xn2", [P, GB, D])
        wraw = xn2
        ot_flat = ot[:].rearrange("p a n -> p (a n)")
        bvb = ot_flat[:, 0:KT * P].rearrange("p (k n) -> p k n", k=KT)
        bo_b = ot_flat[:, 2 * P:2 * P + D]
        b2raw = ot_flat[0:E, 4 * P:4 * P + D]
        rw_raw = ot_flat[:, 6 * P:6 * P + KT * E].rearrange("p (k e) -> p k e", k=KT)
        x2t = ot[:, :, D:2 * D].bitcast(F16)
        lg = sb("lg", [P, GB, E])
        lmax = sb("lmax", [P, GB])
        pick = sb("pick", [P, GB, E])
        first = sb("first", [P, GB])
        hot = sb("hot", [P, GB, E])
        hots = sb("hots", [P, GB, E], BF16)
        posn = sb("posn", [P, GB, E])
        pos = sb("pos", [P, GB])
        posi = sb("posi", [P, GB], U32)
        ids = sb("ids", [P, GB], I32)

        cnt = sb("cnt", [P, E])
        til = sb("til", [P, E])
        end = sb("end", [P, E])
        zero_e = sb("zero_e", [P, E])
        zero_ids = sb("zero_ids", [P, GB], I32)
        eps_c = sb("eps_c", [P, GB])
        minus = sb("minus", [P, GB])
        group_c = sb("group_c", [P, GB], I32)
        carry_p = sb("carry_p", [P, 8])
        carry_v = sb("carry_v", [P, 4])
        jcol = sb("jcol", [P, 1])
        iota_e = sb("iota_e", [P, E])
        ecmp = sb("ecmp", [P, E])
        eidx = sb("eidx", [P, 2])
        ehot = sb("ehot", [P, E])
        etmp = sb("etmp", [P, 4, E])
        ered = sb("ered", [P, 4])
        trow = w1r[0:1, 0:2 * P].bitcast(U32).rearrange("p (a b) -> p a b", a=2)
        prow = sb("prow", [1, E], U32)

        yin_flat = yin[:].rearrange("p a n -> p (a n)")
        gt = x2[:].rearrange("p a b n -> p (a b) n")
        yr = xn2[:, 0:2, :]
        ido = posn[:].rearrange("p b e -> p (b e)")[:, 0:NG].bitcast(U32)
        yo = [buf[:, b, :] for buf in (xin, xn) for b in range(GB)]
        gn = yin_flat[:, 0:2 * D].rearrange("p (g n) -> p g n", g=2)
        hr = yin_flat[:, 2 * D:2 * D + 2 * P].rearrange("p (g n) -> p g n", g=2)
        b2s = qstk[0:2, :, :, :].rearrange("p a b n -> p (a b n)")
        gx = qs[:].rearrange("p a k t -> p (a k t)")[:, 0:4 * KT * P].rearrange("p (g a k t) -> p g a k t", g=2, a=2, k=KT)
        hs = ks[:].rearrange("p a k t -> p (a k t)")[:, 0:2 * P].rearrange("p (g t) -> p g t", g=2)

        S = [pb("S0"), pb("S1")]
        ST = [pb("ST0"), pb("ST1")]
        AV = [pb("AV0"), pb("AV1")]
        M = [pb("M0"), pb("M1")]

        names = """consts w_in w_raw8 w_hi w_lo g_in tanh_done wo_g wo_hi wo_lo bias_in bv_wide bvwo_ready
        gb_a gb_done row_in dve_set pool_set b2_hi b2_lo b2_rows
        ln1_st ln1_mv ln1_sm xn_done y_hi y_t xt_ready xt_hi xt_lo q_ready q_hi q_lo k_ready k_hi k_lo
        v_ready v_done
        s_ready s_max mt_ready m_done st_ready exp_done av_ready av_out o_ready nrm_r nrm_done at_ready
        at_hi at_lo xb_done y_ready x2_done ln2_st ln2_mv ln2_sm xn2_done x2t_ready x2t_hi x2t_lo
        lg_ready lg_done route hot_done rk_ready rk_read rk_link pos_done ids_done
        ew_r8 ew_hi ew_lo y_written
        t_link t_cols t_tr t_rows
        f_norm f_t f_hi f_lo f_h f_hs f_hr f_hlo f_y f_yr f_out f_carry""".split()
        s_ = {n: sem(n) for n in names}
        x_in = [sem("x_in0"), sem("x_in1")]
        y_in = [sem("y_in0"), sem("y_in1")]
        xr_in = [sem("xr_in0"), sem("xr_in1")]
        ew_in = sem("ew_in")
        q_out = sem("q_out")
        k_out = sem("k_out")
        stk = [sem("stk0"), sem("stk1")]
        m_in = [sem("m_in0"), sem("m_in1")]
        scat = [sem("scat0"), sem("scat1")]
        pad_out = sem("pad_out")
        pads_done = sem("pads_done")
        t_in = [sem(f"t_in{n}") for n in range(NG)]
        t_out = [sem(f"t_out{n}") for n in range(NG)]

        MAX_T = {5: 0, 12: 1, 13: 2, 17: 3}
        MAX_ROW = {6: 0, 13: 1, 14: 2}

        block = es.enter_context(nc.Block())

        def schedule(eng, step):
            for n in range(-3, 2):
                step(Group(0, n))
            with eng.Fori(1, LOOP_END // 2) as it:
                step(Group(it, 0))
                step(Group(it, 1))
            for n in range(LOOP_END, GROUPS + 2):
                step(Group(0, n))

        def load_row(eng, row, first, n, top):
            return nc.values_load_multi_w_load_instructions(trow[0:1, row, bass.ds(first, n)], engines=[eng.engine],
                                                            min_val=0, max_val=top)[1]

        def tiles_schedule(eng, fstep, lead, experts=False):
            def known(t, first, row):
                def at_(d):
                    j = t + d
                    e = row[j - first] if row and 0 <= j - first < len(row) else None
                    return (j, j % NG, j // NG, e) if 0 <= j < TILES else None
                return at_

            def looped(it, u, row):
                def at_(d):
                    j = u + d
                    e = row[j + NG] if row and j < NG else None
                    return (it * NG + j, j % NG, it + (j // NG), e)
                return at_

            row = load_row(eng, 0, 0, NG, E - 1) if experts else None
            for t in range(-lead, NG):
                fstep(known(t, 0, row))
            with eng.Fori(1, TILES // NG - 1) as it:
                row = load_row(eng, 0, it * NG + (-NG), 2 * NG, E - 1) if experts else None
                for u in range(NG):
                    fstep(looped(it, u, row))
            row = load_row(eng, 0, TILES - 2 * NG, 2 * NG, E - 1) if experts else None
            for t in range(TILES - NG, TILES + 2):
                fstep(known(t, TILES - 2 * NG, row))

        @block.sync
        def _(sp):
            sp.dma_start(wraw[:, 0:2, :], wq.rearrange("(t p) n -> p t n", p=P)).then_inc(s_["w_in"], 16)
            sp.dma_start(wraw[:, 2:4, :], wk.rearrange("(t p) n -> p t n", p=P)).then_inc(s_["w_in"], 16)

            def load_x(a):
                if not a.real():
                    return
                wait(sp, s_["xn_done"], a.count(1))
                sp.dma_start(xin[:, :, :],
                             x[bass.ds(a.index(GB), GB), :, :].rearrange("b p n -> p b n")).then_inc(x_in[a.par], 16)
                wait(sp, s_["y_hi"], a.count(3))
                sp.dma_start(yin[:, :, :],
                             ctx_t[:, bass.ds(a.index(GT), GT)].rearrange("(t p) n -> p t n", p=P)).then_inc(y_in[a.par], 16)

            sp.dma_start(gate[:, :], g2.partition_broadcast(P)).then_inc(s_["g_in"], 16)
            sp.dma_start(bqk[:, 0, :], bq).then_inc(s_["bias_in"], 16)
            sp.dma_start(bqk[:, 1, :], bk).then_inc(s_["bias_in"], 16)
            sp.dma_start(bvc[:, :], bv).then_inc(s_["bias_in"], 16)
            sp.dma_start(bo_b[:, :], bo.partition_broadcast(P)).then_inc(s_["bias_in"], 16)
            sp.dma_start(b1c[:, :], b1).then_inc(s_["bias_in"], 16)
            sp.dma_start(b2raw[:, :], b2).then_inc(s_["bias_in"], 16)
            sp.dma_start(rw_raw[:, :, :], rw.rearrange("(t p) n -> p t n", p=P)).then_inc(s_["bias_in"], 16)
            sp.dma_start(rb_b[:, :], rb.partition_broadcast(P)).then_inc(s_["bias_in"], 16)
            wait(sp, s_["w_raw8"], 4)
            wait(sp, s_["w_lo"], 2)
            sp.dma_start(wraw[:, 0:2, :], wv.rearrange("(t p) n -> p t n", p=P)).then_inc(s_["w_in"], 16)
            sp.dma_start(wraw[:, 2:4, :], wo.rearrange("(t p) n -> p t n", p=P)).then_inc(s_["w_in"], 16)
            sp.wait_ge(s_["pool_set"], 1)
            sp.dma_start(rows[PADS:PADS + P, :], pad[:, :]).then_inc(pad_out, 16)
            sp.wait_ge(s_["dve_set"], 2)
            for par in range(2):
                sp.dma_start(kstk[STACK + 1:STACK + 2, par, 1, :, :], kstk[STACK:STACK + 1, par, 0, :, :]
                             ).then_inc(s_["row_in"], 16)
            sp.wait_ge(s_["row_in"], 16 * 2)

            def step(s):
                a, n1, g = s.plus(2), s.plus(1), s
                if a.real():
                    wait(sp, s_["ew_r8"], a.count(2))
                    wait(sp, s_["ew_lo"], a.count(2))
                    sp.dma_start(w1r[:, :], w1[:, bass.ds(a.index(SLICE * KT * H), SLICE * KT * H)]).then_inc(ew_in, 16)
                    sp.dma_start(w2r[:, :], w2[:, bass.ds(a.index(SLICE * D), SLICE * D)]).then_inc(ew_in, 16)
                load_x(s.plus(3))
                if n1.real():
                    wait(sp, s_["m_done"], n1.count(4, 4))
                    for half in range(2):
                        sp.dma_start(qstk[STACK + half:STACK + half + 1, n1.par, :, :],
                                     mrow[HP * half:HP * half + HP, :]).then_inc(m_in[n1.par], 16)
                if a.real():
                    for t in range(KT):
                        wait(sp, s_["k_hi"], a.count(2, t + 1))
                        sp.dma_start(k_image[a.par, t, 0].rearrange("d j n -> j d n"), ks[:, 0, t, :]
                                     ).then_inc(k_out, 16)
                    for t in range(KT):
                        wait(sp, s_["k_lo"], a.count(2, t + 1))
                        sp.dma_start(k_image[a.par, t, 1].rearrange("d j n -> j d n"), ks[:, 1, t, :]
                                     ).then_inc(k_out, 16)
                    for t in range(KT):
                        wait(sp, s_["q_hi"], a.count(2, t + 1))
                        sp.dma_start(q_image[a.par, t, 1].rearrange("d j n -> j d n"), qs[:, 0, t, :]
                                     ).then_inc(q_out, 16)
                    for t in range(KT):
                        wait(sp, s_["q_lo"], a.count(2, t + 1))
                        sp.dma_start(q_image[a.par, t, 0].rearrange("d j n -> j d n"), qs[:, 1, t, :]
                                     ).then_inc(q_out, 16)
                    def stack(dst, src, first):
                        for t in range(KT):
                            rows_of = STACK // 2 * t
                            sp.dma_start(dst(t)[rows_of:rows_of + DH], src[t, first]).then_inc(stk[a.par], 16)
                            sp.dma_start(dst(t)[rows_of + DH:rows_of + 3 * DH], src[t].rearrange("a d j n -> (a d) j n")
                                         ).then_inc(stk[a.par], 16)

                    wait(sp, k_out, a.count(64, 64))
                    stack(lambda t: kstk[:, a.par, t, :, :], k_image[a.par], 0)
                    wait(sp, q_out, a.count(64, 64))
                    stack(lambda t: qstk[:, a.par, :, :], q_image[a.par], 1)
                if n1.real():
                    wait(sp, s_["x2_done"], n1.count(2))
                    sp.dma_start(xres[:, :, :],
                                 x[bass.ds(n1.index(GB), GB), :, :].rearrange("b p n -> p b n")).then_inc(xr_in[n1.par], 16)

            schedule(sp, step)

            sp.wait_ge(s_["b2_lo"], 1)
            sp.wait_ge(s_["st_ready"], CHUNKS * GROUPS)
            for n in range(2):
                sp.dma_start(b2s[n:n + 1, :], b2hl[:, n, :]).then_inc(s_["b2_rows"], 16)
            sp.wait_ge(s_["t_rows"], 1)
            for e in range(0, E, NG):
                pads = nc.values_load_multi_w_load_instructions(prow[0:1, e:e + NG], engines=[sp.engine],
                                                                min_val=0, max_val=PADS)[1]
                for r in pads:
                    sp.dma_start(rows[bass.ds(r, P - 1), :], pad[0:P - 1, :]).then_inc(pads_done, 16)
            sp.wait_ge(pads_done, 16 * E)
            sp.wait_ge(pad_out, 16)
            wait(sp, scat[0], 16 * GB * GROUPS // 2)
            wait(sp, scat[1], 16 * GB * GROUPS // 2)

            def tile(n, lap, r):
                wait(sp, s_["f_out"], lap * NG + (n + 1 - NG))
                sp.dma_start(gt[:, n, :], rows[bass.ds(r, P), :]).then_inc(t_in[n], 16)

            first = load_row(sp, 1, 0, NG, PADS)
            for n in range(NG):
                tile(n, 0, first[n])
            with sp.Fori(1, TILES // NG) as it:
                first = load_row(sp, 1, it * NG, NG, PADS)
                for n in range(NG):
                    tile(n, it, first[n])
            for n in range(NG):
                wait(sp, t_out[n], 16 * TILES // NG)

        @block.gpsimd
        def _(pool):
            g_ = nc.gpsimd

            def carry(site):
                return g_.tensor_tensor(carry_p[:, site:site + 1], zero_e[:, 0:1], zero_e[:, 0:1], ALU.add)

            g_.memset(ident[:], 0.0)
            g_.memset(tri[:], 1.0)
            g_.memset(ones[:], 1.0)
            g_.memset(ones16[:], 1.0)
            g_.memset(half[:], -0.5)
            g_.memset(zero_e[:], 0.0)
            g_.memset(eps_c[:], EPS)
            g_.memset(minus[:], -1.0)
            g_.memset(group_c[:], GT)
            g_.memset(zero_ids[:], 0)
            g_.memset(hots[:], 0.0)
            g_.iota(rank_e[:], pattern=[[-1, E]], base=E, channel_multiplier=0, allow_small_or_imprecise_dtypes=True)
            g_.iota(iota_e[:], pattern=[[1, E]], base=0, channel_multiplier=0, allow_small_or_imprecise_dtypes=True)
            g_.iota(jcol[:], pattern=[[0, 1]], base=0, channel_multiplier=1, allow_small_or_imprecise_dtypes=True)
            g_.iota(ids[:], pattern=[[P, GB]], base=-GT, channel_multiplier=1)
            g_.iota(base_e[:].rearrange("p (i o) -> p i o", o=2), pattern=[[REGION, E // 2], [REGION - 1, 2]],
                    base=0, channel_multiplier=0, allow_small_or_imprecise_dtypes=True)
            g_.iota(sign_e[:].rearrange("p (i o) -> p i o", o=2), pattern=[[0, E // 2], [-2, 2]],
                    base=1, channel_multiplier=0, allow_small_or_imprecise_dtypes=True)
            g_.memset(v[:], 1.0)
            g_.memset(x2[:], 0.0)
            g_.memset(pad[:], 0.0).then_inc(s_["consts"], 1)
            pool.wait_ge(s_["consts"], 1)
            g_.memset(pad[:, D + 2:D + 3].bitcast(U32), NOBODY)
            g_.tensor_copy(run[:], base_e[:])
            g_.affine_select(out=tri[:], in_=tri[:], compare_op=ALU.is_gt, fill=0.0, base=0,
                             pattern=[[1, P]], channel_multiplier=-1)
            g_.affine_select(out=ident[:], in_=ident[:], compare_op=ALU.not_equal, fill=1.0, base=0,
                             pattern=[[1, P]], channel_multiplier=-1).then_inc(s_["pool_set"], 1)
            pool.wait_ge(s_["pool_set"], 1)

            def norm_scale(mv, st, ve, rs, nm, shift, k0):
                link = s_[st]
                g_.tensor_tensor(ve, mv[:, :, 1], eps_c[:], ALU.add).then_inc(link, 1)
                wait(pool, link, k0(1))
                g_.tensor_tensor(rs, ve, half[:], ALU.pow).then_inc(link, 1)
                wait(pool, link, k0(2))
                g_.tensor_tensor(nm, mv[:, :, 0], rs, ALU.mult).then_inc(link, 1)
                wait(pool, link, k0(3))
                g_.tensor_tensor(shift, nm, minus[:], ALU.mult).then_inc(link, 1)
                wait(pool, link, k0(4))

            def step(s):
                a, g, f, r = s.plus(2), s, s.plus(-1), s.plus(-2)
                if a.real():
                    wait(pool, y_in[a.par], a.halved(16, 16))
                    wait(pool, s_["v_ready"], a.count(2))
                    wait(pool, s_["k_ready"], a.count(2))
                    zeros = zero_e[:, 0:1].to_broadcast([P, GT])
                    g_.tensor_tensor(ys[:, 0, :], yin[:, 0, :], zeros, ALU.add).then_inc(s_["y_t"], 1)
                    g_.tensor_tensor(ys[:, 2, :], yin[:, 1, :], zeros, ALU.add).then_inc(s_["y_t"], 1)
                    wait(pool, s_["y_t"], a.count(2, 2))
                    g_.tensor_tensor(ys[:, 1, :], yin[:, 0, :], ys[:, 0, :], ALU.subtract).then_inc(s_["y_hi"], 1)
                    wait(pool, s_["y_hi"], a.count(3, 1))
                    sent = a.plus(-5)
                    if sent.real():
                        wait(pool, scat[sent.par], sent.halved(16 * GB, 16 * GB))
                    g_.tensor_tensor(ys[H:P, 2, :], yin[H:P, 1, :], ys[H:P, 2, :], ALU.subtract).then_inc(s_["y_hi"], 2)
                    wait(pool, s_["y_hi"], a.count(3, 3))
                    wait(pool, s_["ln1_mv"], a.count(GB, GB))
                    norm_scale(mv1, "ln1_sm", ve1[:], rs1[:], nm1[:], ve1[:], lambda k: a.count(4, k))
                    wait(pool, s_["xt_ready"], a.count(2))
                    carry(s.par)
                    for b in range(GB):
                        last = g_.tensor_scalar(xn[:, b, :], xin[:, b, :], rs1[:, b:b + 1], ve1[:, b:b + 1],
                                                ALU.mult, ALU.add)
                    last.then_inc(s_["xn_done"], 1)
                if f.real():
                    wait(pool, s_["ln2_mv"], f.count(GB, GB))
                    wait(pool, s_["ids_done"], f.count(2))
                    g_.tensor_tensor(ids[:], ids[:], group_c[:], ALU.add).then_inc(s_["ids_done"], 1)
                    norm_scale(mv2, "ln2_sm", ve2[:], x2[:, f.par, :, D], nm2[:], x2[:, f.par, :, D + 1], lambda k: f.count(4, k))
                    wait(pool, s_["ids_done"], f.count(2, 1))
                    g_.tensor_tensor(x2[:, f.par, :, D + 2].bitcast(I32), ids[:], zero_ids[:], ALU.add).then_inc(s_["ids_done"], 1)
                    wait(pool, s_["x2t_ready"], f.count(2))
                    carry(4 + s.par)
                    for b in range(GB):
                        last = g_.tensor_scalar(xn2[:, b, :], x2[:, f.par, b, 0:D], x2[:, f.par, b, D:D + 1],
                                                x2[:, f.par, b, D + 1:D + 2], ALU.mult, ALU.add)
                    last.then_inc(s_["xn2_done"], 1)
                if g.real():
                    wait(pool, xr_in[g.par], g.halved(16, 16))
                    if isinstance(g.base, int) and g.off == 0:
                        pool.wait_ge(s_["gb_done"], 1)
                    g_.tensor_tensor(xres[:, :, :], xres[:, :, :],
                                     gbias[:].unsqueeze(1).to_broadcast([P, GB, D]), ALU.add).then_inc(s_["xb_done"], 1)
                if r.real():
                    wait(pool, s_["pos_done"], r.count(1, 1))
                    carry(2 + s.par)
                    for b in range(GB):
                        g_.indirect_dma_start(out=rows[:, :], out_offset=bass.IndirectOffsetOnAxis(ap=posi[:, b:b + 1], axis=0),
                                              in_=x2[:, r.par, b, :], in_offset=None).then_inc(scat[r.par], 16)
                if a.real():
                    wait(pool, s_["ew_hi"], a.count(2, 2))
                    o1, n1 = a.index(SLICE * KT * P), SLICE * KT * P
                    g_.tensor_tensor(w1s[:, 1, bass.ds(o1, n1)].rearrange("p (c u n) -> p c u n", u=2, n=H),
                                     w1r[:].rearrange("p (c n) -> p c n", n=H).unsqueeze(2).to_broadcast([P, SLICE * KT, 2, H]),
                                     w1s[:, 0, bass.ds(o1, n1)].rearrange("p (c u n) -> p c u n", u=2, n=H),
                                     ALU.subtract).then_inc(s_["ew_lo"], 1)
                    o2, n2 = a.index(SLICE * D), SLICE * D
                    g_.tensor_tensor(w2s[:, 1, bass.ds(o2, n2)], w2r[:], w2s[:, 0, bass.ds(o2, n2)],
                                     ALU.subtract).then_inc(s_["ew_lo"], 1)

            schedule(pool, step)

            def two_tiles(n, lap):
                wait(pool, s_["f_carry"], lap * (NG // 2) + (n // 2 + 1))
                wait(pool, s_["f_out"], lap * NG + (n + 2))
                carry(6).then_inc(s_["f_carry"], 1)
                for m in (n, n + 1):
                    g_.indirect_dma_start(out=out, out_offset=bass.IndirectOffsetOnAxis(ap=ido[:, m:m + 1], axis=0),
                                          in_=yo[m], in_offset=None, bounds_check=TOKENS - 1, oob_is_err=False
                                          ).then_inc(t_out[m], 16)

            carry(7).then_inc(s_["f_carry"], 1)
            with pool.Fori(0, TILES // NG) as it:
                for n in range(0, NG, 2):
                    two_tiles(n, it)

        @block.scalar
        def _(act):
            a_ = nc.scalar

            def scaled_split(n, dst):
                for t in range(2):
                    a_.activation(wraw[:, 2 * n + t, :], wraw[:, 2 * n + t, :], ACT.Copy, scale=WS).then_inc(s_["w_raw8"], 1)

            act.wait_ge(s_["g_in"], 16)
            a_.activation(tg[:], gate[:], ACT.Tanh).then_inc(s_["tanh_done"], 1)
            act.wait_ge(s_["w_in"], 32)
            scaled_split(0, wq_s)
            scaled_split(1, wk_s)
            act.wait_ge(s_["w_raw8"], 4)
            a_.copy(wq_s[:, 0, :, :], wraw[:, 0:2, :]).then_inc(s_["w_hi"], 1)
            a_.copy(wk_s[:, 0, :, :], wraw[:, 2:4, :]).then_inc(s_["w_hi"], 1)
            act.wait_ge(s_["bias_in"], 16 * 8)
            a_.activation(bqk8[:], bqk[:], ACT.Copy, scale=WS).then_inc(s_["w_hi"], 1)
            a_.activation(b2raw[:], b2raw[:], ACT.Copy, scale=WS).then_inc(s_["w_hi"], 1)
            a_.activation(rw_raw[:], rw_raw[:], ACT.Copy, scale=WS).then_inc(s_["w_hi"], 1)
            act.wait_ge(s_["w_hi"], 5)
            a_.copy(b2hl[:, 0, :], b2raw[:]).then_inc(s_["b2_hi"], 1)
            a_.copy(rw_s[:, 0, :, :], rw_raw[:]).then_inc(s_["b2_hi"], 1)
            a_.copy(bvb[:], bvc[:].unsqueeze(2).to_broadcast([P, KT, P])).then_inc(s_["bv_wide"], 1)
            act.wait_ge(s_["w_in"], 64)
            scaled_split(0, wv_s)
            act.wait_ge(s_["w_raw8"], 6)
            a_.copy(wv_s[:, 0, :, :], wraw[:, 0:2, :]).then_inc(s_["w_hi"], 1)
            act.wait_ge(s_["bvwo_ready"], 1)
            act.wait_ge(s_["tanh_done"], 1)
            a_.activation(wraw[:, 2:4, :], wraw[:, 2:4, :], ACT.Copy, scale=WS).then_inc(s_["w_raw8"], 1)
            act.wait_ge(s_["w_raw8"], 7)
            a_.activation(wraw[:, 2:4, :], wraw[:, 2:4, :], ACT.Identity, scale=tg[:, 0:1]).then_inc(s_["w_raw8"], 1)
            act.wait_ge(s_["w_raw8"], 8)
            a_.copy(wo_s[:, 0, :, :], wraw[:, 2:4, :]).then_inc(s_["w_hi"], 1)

            def exp_chunk(g, c):
                act.wait_ge(s_["st_ready"], g.count(CHUNKS, c + 1))
                wait(act, s_["av_ready"], g.count(CHUNKS, c + 1 - NPT))
                a_.activation(pt[:, c % NPT, :], ST[c % 2][:], ACT.Exp,
                              scale=0.25 / (WS * WS)).then_inc(s_["exp_done"], 1)

            def attn_out(g, b):
                act.wait_ge(s_["av_ready"], g.count(CHUNKS, 4 * b + 4))
                wait(act, s_["lg_ready"], g.count(1, -1))
                a_.copy(ot[:, b, :], AV[b % 2][:]).then_inc(s_["av_out"], 1)

            def max_row(n1, b):
                act.wait_ge(s_["mt_ready"], n1.count(4, b + 1))
                prev = n1.plus(-1)
                if prev.real():
                    wait(act, m_in[prev.par], prev.halved(32, 32))
                a_.activation(mrow[:, b * P:(b + 1) * P], M[(b + 1) % 2][0:HEADS, 0:P], ACT.Copy,
                              scale=-1.0 / MS).then_inc(s_["m_done"], 1)

            def expert_raw(a):
                act.wait_ge(ew_in, a.count(32, 32))
                a_.activation(w1r[:], w1r[:], ACT.Copy, scale=WS).then_inc(s_["ew_r8"], 1)
                a_.activation(w2r[:], w2r[:], ACT.Copy, scale=WS).then_inc(s_["ew_r8"], 1)

            def expert_hi(a):
                act.wait_ge(s_["ew_r8"], a.count(2, 2))
                a_.copy(w1s[:, 0, bass.ds(a.index(SLICE * KT * P), SLICE * KT * P)].rearrange("p (c u n) -> p c u n", u=2, n=H),
                        w1r[:].rearrange("p (c n) -> p c n", n=H).unsqueeze(2).to_broadcast([P, SLICE * KT, 2, H])
                        ).then_inc(s_["ew_hi"], 1)
                a_.copy(w2s[:, 0, bass.ds(a.index(SLICE * D), SLICE * D)], w2r[:]).then_inc(s_["ew_hi"], 1)

            def step(s):
                a, n1, g, f = s.plus(2), s.plus(1), s, s.plus(-1)
                for c in range(CHUNKS):
                    if g.real():
                        exp_chunk(g, c)
                        if c % 4 == 2 and c > 4:
                            attn_out(g, c // 4 - 1)
                    if n1.real() and c in MAX_ROW:
                        max_row(n1, MAX_ROW[c])
                    if a.real() and c == 8:
                        expert_raw(a)
                    if a.real() and c == 11:
                        expert_hi(a)
                if g.real():
                    attn_out(g, 3)
                if n1.real():
                    max_row(n1, 3)
                if a.real():
                    for t in range(KT):
                        act.wait_ge(s_["xt_ready"], a.count(2, t + 1))
                        wait(act, s_["y_ready"], a.count(2, -4))
                        a_.copy(xt[:, 0, t, :], M[t][:]).then_inc(s_["xt_hi"], 1)
                    for t in range(KT):
                        act.wait_ge(s_["k_ready"], a.count(2, t + 1))
                        wait(act, k_out, a.count(64))
                        a_.activation(ks[:, 0, t, :], ST[t][:], ACT.Identity, bias=bqk8[:, 1, t:t + 1]).then_inc(s_["k_hi"], 1)
                    for t in range(KT):
                        act.wait_ge(s_["q_ready"], a.count(2, t + 1))
                        wait(act, q_out, a.count(64))
                        a_.activation(qs[:, 0, t, :], M[t][:], ACT.Identity, bias=bqk8[:, 0, t:t + 1]).then_inc(s_["q_hi"], 1)
                    for t in range(2):
                        act.wait_ge(s_["v_ready"], a.count(2, t + 1))
                        wait(act, s_["av_ready"], a.count(CHUNKS, -CHUNKS))
                        vv = v[:, a.par, t * 1024:t * 1024 + 1024].rearrange("p (h d) -> p h d", d=32)[:, :, 0:DH]
                        a_.activation(vv, ST[t][:].rearrange("p (h d) -> p h d", d=DH), ACT.Copy,
                                      scale=1.0 / WS).then_inc(s_["v_done"], 1)
                if g.real():
                    for t in range(KT):
                        act.wait_ge(s_["at_ready"], g.count(2, t + 1))
                        if a.real():
                            act.wait_ge(s_["q_ready"], a.count(2, 2))
                        a_.copy(at[:, 0, t, :], S[t][:]).then_inc(s_["at_hi"], 1)
                if f.real():
                    for t in range(KT):
                        act.wait_ge(s_["x2t_ready"], f.count(2, t + 1))
                        a_.copy(x2t[:, t, :], AV[t][:]).then_inc(s_["x2t_hi"], 1)

            schedule(act, step)

            act.wait_ge(s_["t_rows"], 1)

            def moved_hi(t):
                j, n, lap, e = t
                act.wait_ge(s_["f_t"], j + 1)
                wait(act, s_["f_h"], j + (-1))
                a_.copy(gx[:, n % 2, 0, :, :], S[n % 2][:, 0:D].rearrange("p (k t) -> p k t", k=KT)).then_inc(s_["f_hi"], 1)

            def hidden(t):
                j, n, lap, e = t
                act.wait_ge(s_["f_h"], j + 1)
                wait(act, s_["f_y"], j + (-1))
                a_.activation(hs[:, n % 2, :], ST[n % 2][:, 0:P], ACT.Relu, bias=b1c[:, bass.ds(e, 1)],
                              scale=1.0 / WS).then_inc(s_["f_hs"], 1)
                a_.activation(hr[H:P, n % 2, :], ST[n % 2][H:P, 0:P], ACT.Relu, bias=b1c[H:P, bass.ds(e, 1)],
                              scale=1.0 / WS).then_inc(s_["f_hr"], 1)

            def relu_out(t):
                j, n, lap, e = t
                act.wait_ge(s_["f_y"], j + 1)
                wait(act, s_["f_out"], j + (-1))
                a_.activation(yr[:, n % 2, :], AV[n % 2][:, 0:D], ACT.Relu, scale=1.0 / WS).then_inc(s_["f_yr"], 1)

            def fstep(at_):
                for d, stage in ((0, moved_hi), (-1, hidden), (-2, relu_out)):
                    t = at_(d)
                    if t is not None:
                        stage(t)

            tiles_schedule(act, fstep, lead=0, experts=True)

        @block.vector
        def _(dve):
            v_ = nc.vector

            def carry(site):
                v_.tensor_copy(carry_v[:, site:site + 1], tg[:, 0:1])

            v_.memset(kstk[:], 0.0).then_inc(s_["dve_set"], 1)
            dve.wait_ge(s_["dve_set"], 1)
            v_.memset(kstk[STACK:STACK + 1, :, 0, :, :], MS).then_inc(s_["dve_set"], 1)
            dve.wait_ge(s_["w_hi"], 2)
            v_.tensor_tensor(wq_s[:, 1, :, :], wraw[:, 0:2, :], wq_s[:, 0, :, :], ALU.subtract).then_inc(s_["w_lo"], 1)
            v_.tensor_tensor(wk_s[:, 1, :, :], wraw[:, 2:4, :], wk_s[:, 0, :, :], ALU.subtract).then_inc(s_["w_lo"], 1)
            dve.wait_ge(s_["b2_hi"], 2)
            v_.tensor_tensor(b2hl[:, 1, :], b2raw[:], b2hl[:, 0, :], ALU.subtract).then_inc(s_["b2_lo"], 1)
            v_.tensor_tensor(rw_s[:, 1, :, :], rw_raw[:], rw_s[:, 0, :, :], ALU.subtract).then_inc(s_["w_lo"], 1)
            dve.wait_ge(s_["w_hi"], 6)
            v_.tensor_tensor(wv_s[:, 1, :, :], wraw[:, 0:2, :], wv_s[:, 0, :, :], ALU.subtract).then_inc(s_["w_lo"], 1)
            dve.wait_ge(s_["bvwo_ready"], 1)
            v_.tensor_tensor(gbias[:], AV[0][:, 0:D], bo_b[:], ALU.add).then_inc(s_["gb_a"], 1)
            dve.wait_ge(s_["gb_a"], 1)
            dve.wait_ge(s_["tanh_done"], 1)
            v_.tensor_scalar(gbias[:], gbias[:], tg[:, 0:1], None, ALU.mult).then_inc(s_["gb_done"], 1)
            dve.wait_ge(s_["w_hi"], 7)
            v_.tensor_tensor(wo_s[:, 1, :, :], wraw[:, 2:4, :], wo_s[:, 0, :, :], ALU.subtract).then_inc(s_["w_lo"], 1)
            dve.wait_ge(s_["pool_set"], 1)

            def stats_1(src, st, st_sem):
                for b in range(GB):
                    v_.bn_stats(st[:, b, :], src(b)).then_inc(s_[st_sem], 1)

            def stats_2(st, mv, st_sem, mv_sem, g, k):
                wait(dve, s_[st_sem], g.count(GB, GB))
                carry(2 * k + g.par)
                for b in range(GB):
                    v_.bn_aggr(mv[:, b, :], st[:, b, :]).then_inc(s_[mv_sem], 1)

            def max_chunk(n1, c):
                dve.wait_ge(s_["s_ready"], n1.count(CHUNKS, c + 1))
                if c % 4 == 0:
                    wait(dve, s_["mt_ready"], n1.count(4, c // 4 - 3))
                b, cc = c // 4, c % 4
                v_.reduce_max(mx[:, b, CH * cc:CH * cc + CH], S[c % 2][:].rearrange("p (h t) -> p h t", h=CH), X
                              ).then_inc(s_["s_max"], 1)

            def rank_post(r, n):
                link = s_["rk_link"]
                if n == 0:
                    dve.wait_ge(s_["rk_ready"], r.count(1, 1))
                    v_.tensor_tensor(posn[:], M[0][:, 0:GB * E].rearrange("p (b e) -> p b e", b=GB),
                                     run[:].unsqueeze(1).to_broadcast([P, GB, E]), ALU.add).then_inc(link, 1)
                    dve.wait_ge(link, r.count(3, 1))
                    v_.tensor_tensor(run[:], M[0][:, GB * E:GB * E + E], run[:], ALU.add).then_inc(s_["rk_read"], 1)
                    v_.tensor_tensor(posn[:], posn[:], hot[:], ALU.mult).then_inc(link, 1)
                if n == 1:
                    dve.wait_ge(link, r.count(3, 2))
                    v_.reduce_sum(pos[:], posn[:], X).then_inc(link, 1)
                if n == 2:
                    dve.wait_ge(link, r.count(3, 3))
                    pr = r.plus(-1)
                    if pr.real():
                        wait(dve, scat[pr.par], pr.halved(16 * GB, 16 * GB))
                    v_.tensor_copy(posi[:], pos[:]).then_inc(s_["pos_done"], 1)
                    dve.wait_ge(s_["rk_read"], r.count(1, 1))

            def lo_part(dst, src, hi, ready, n, done, bias=None):
                dve.wait_ge(s_[ready], n)
                if bias is None:
                    v_.tensor_tensor(dst, src, hi, ALU.subtract).then_inc(s_[done], 1)
                else:
                    v_.scalar_tensor_tensor(out=dst, in0=src, scalar=bias, in1=hi, op0=ALU.add,
                                            op1=ALU.subtract).then_inc(s_[done], 1)

            def logits(f):
                dve.wait_ge(s_["lg_ready"], f.count(1, 1))
                v_.scalar_tensor_tensor(out=lg[:], in0=S[0][:, 0:GB * E].rearrange("p (b e) -> p b e", b=GB), scalar=1.0 / WS,
                                        in1=rb_b[:].unsqueeze(1).to_broadcast([P, GB, E]), op0=ALU.mult, op1=ALU.add
                                        ).then_inc(s_["lg_done"], 1)

            def route(r, n):
                link = s_["route"]
                ranks_e = rank_e[:].unsqueeze(1).to_broadcast([P, GB, E])
                if n == 0:
                    dve.wait_ge(s_["lg_done"], r.count(1, 1))
                    v_.reduce_max(lmax[:], lg[:], X).then_inc(link, 1)
                if n == 1:
                    dve.wait_ge(link, r.count(5, 1))
                    v_.tensor_tensor(pick[:], lg[:], lmax[:].unsqueeze(2).to_broadcast([P, GB, E]), ALU.is_ge).then_inc(link, 1)
                if n == 2:
                    dve.wait_ge(link, r.count(5, 2))
                    v_.tensor_tensor(pick[:], pick[:], ranks_e, ALU.mult).then_inc(link, 1)
                if n == 3:
                    dve.wait_ge(link, r.count(5, 3))
                    v_.reduce_max(first[:], pick[:], X).then_inc(link, 1)
                if n == 4:
                    dve.wait_ge(link, r.count(5, 4))
                    v_.tensor_tensor(hot[:], ranks_e, first[:].unsqueeze(2).to_broadcast([P, GB, E]),
                                     ALU.is_equal).then_inc(link, 1)
                if n == 5:
                    dve.wait_ge(link, r.count(5, 5))
                    v_.tensor_tensor(hots[:], hot[:], sign_e[:].unsqueeze(1).to_broadcast([P, GB, E]), ALU.mult
                                     ).then_inc(s_["hot_done"], 1)

            def step(s):
                nxt, a, n1, g, f, r = s.plus(3), s.plus(2), s.plus(1), s, s.plus(-1), s.plus(-2)
                for c in range(CHUNKS):
                    if n1.real():
                        max_chunk(n1, c)
                    if f.real() and c < GB:
                        v_.bn_stats(st2[:, c, :], x2[:, f.par, c, 0:D]).then_inc(s_["ln2_st"], 1)
                    if f.real() and c == GB:
                        wait(dve, s_["xn2_done"], f.count(1))
                        stats_2(st2, mv2, "ln2_st", "ln2_mv", f, 1)
                    if r.real() and c < 6:
                        route(r, c)
                    if r.real() and 8 <= c < 11:
                        rank_post(r, c - 8)
                if a.real():
                    for t in range(KT):
                        lo_part(xt[:, 1, t, :], M[t][:], xt[:, 0, t, :], "xt_hi", a.count(2, t + 1), "xt_lo")
                    for t in range(KT):
                        lo_part(ks[:, 1, t, :], ST[t][:], ks[:, 0, t, :], "k_hi", a.count(2, t + 1), "k_lo", bqk8[:, 1, t:t + 1])
                    for t in range(KT):
                        lo_part(qs[:, 1, t, :], M[t][:], qs[:, 0, t, :], "q_hi", a.count(2, t + 1), "q_lo", bqk8[:, 0, t:t + 1])
                if g.real():
                    banks = [bank[:].rearrange("p (h d) -> p h d", d=32) for bank in (S[0], S[1], AV[0], AV[1])]
                    for b in range(GB):
                        dve.wait_ge(s_["o_ready"], g.count(4, b + 1))
                        v_.reciprocal(rec[:, b, :], banks[b][:, :, DH]).then_inc(s_["nrm_r"], 1)
                    for b in range(GB):
                        dve.wait_ge(s_["nrm_r"], g.count(4, b + 1))
                        v_.tensor_tensor(an[:, b, :].rearrange("p (h d) -> p h d", d=DH), banks[b][:, :, 0:DH],
                                         rec[:, b, :].unsqueeze(2).to_broadcast([P, HEADS, DH]), ALU.mult
                                         ).then_inc(s_["nrm_done"], 1)
                if nxt.real():
                    dve.wait_ge(x_in[nxt.par], nxt.halved(16, 16))
                    wait(dve, s_["xn_done"], nxt.count(1))
                    stats_1(lambda b: xin[:, b, :], st1, "ln1_st")
                if g.real():
                    for t in range(KT):
                        lo_part(at[:, 1, t, :], S[t][:], at[:, 0, t, :], "at_hi", g.count(2, t + 1), "at_lo")
                if nxt.real():
                    stats_2(st1, mv1, "ln1_st", "ln1_mv", nxt, 0)
                if f.real():
                    for t in range(KT):
                        lo_part(x2t[:, KT + t, :], AV[t][:], x2t[:, t, :], "x2t_hi", f.count(2, t + 1), "x2t_lo")
                if g.real():
                    dve.wait_ge(s_["xb_done"], g.count(1, 1))
                    pg = g.plus(-2)
                    if pg.real():
                        wait(dve, scat[pg.par], pg.halved(16 * GB, 16 * GB))
                    for t in range(2):
                        dve.wait_ge(s_["y_ready"], g.count(2, t + 1))
                        v_.scalar_tensor_tensor(out=x2[:, g.par, 2 * t:2 * t + 2, 0:D],
                                                in0=M[t][:].rearrange("p (b n) -> p b n", b=2), scalar=1.0 / WS,
                                                in1=xres[:, 2 * t:2 * t + 2, :], op0=ALU.mult, op1=ALU.add
                                                ).then_inc(s_["x2_done"], 1)
                if f.real():
                    logits(f)
                if g.real():
                    dve.wait_ge(s_["x2_done"], g.count(2, 2))

            schedule(dve, step)

            link, n = s_["t_link"], [0]

            def then(ins):
                n[0] += 1
                ins.then_inc(link, 1)
                dve.wait_ge(link, n[0])

            def floored(dst, src, add):
                then(v_.tensor_scalar(dst, src, float(add), 1.0 / P, ALU.add, ALU.mult))
                then(v_.tensor_scalar(dst, dst, -0.498, 8388608.0, ALU.add, ALU.add))
                then(v_.tensor_scalar(dst, dst, 8388608.0, None, ALU.subtract))

            dve.wait_ge(s_["rk_read"], GROUPS)
            then(v_.tensor_tensor(cnt[:], run[:], base_e[:], ALU.subtract))
            then(v_.tensor_tensor(cnt[:], cnt[:], sign_e[:], ALU.mult))
            floored(til[:], cnt[:], P - 1)
            then(v_.tensor_tensor_scan(end[:], til[:], zero_e[:], 0.0, ALU.add, ALU.add))
            then(v_.tensor_scalar(ecmp[:], end[:], jcol[:, 0:1], None, ALU.is_le))
            then(v_.reduce_sum(eidx[:, 0:1], ecmp[:], X))
            then(v_.tensor_scalar(ehot[:], iota_e[:], eidx[:, 0:1], None, ALU.is_equal))
            then(v_.tensor_tensor(etmp[:, 3, :], end[:], til[:], ALU.subtract))
            then(v_.tensor_tensor(etmp[:, 0, :], etmp[:, 3, :], ehot[:], ALU.mult))
            then(v_.tensor_scalar(etmp[:, 3, :], sign_e[:], -1.0, (P - 1) / 2.0, ALU.add, ALU.mult))
            then(v_.tensor_tensor(etmp[:, 3, :], etmp[:, 3, :], base_e[:], ALU.add))
            then(v_.tensor_tensor(etmp[:, 1, :], etmp[:, 3, :], ehot[:], ALU.mult))
            then(v_.tensor_tensor(etmp[:, 2, :], sign_e[:], ehot[:], ALU.mult))
            then(v_.tensor_copy(etmp[:, 3, :], ehot[:]))
            then(v_.reduce_sum(ered[:], etmp[:], X))
            then(v_.tensor_scalar(eidx[:, 1:2], jcol[:], ered[:, 0:1], float(P), ALU.subtract, ALU.mult))
            then(v_.tensor_scalar(eidx[:, 1:2], eidx[:, 1:2], ered[:, 2:3], ered[:, 1:2], ALU.mult, ALU.add))
            then(v_.tensor_scalar(ered[:, 3:4], ered[:, 3:4], -float(PADS), float(PADS), ALU.mult, ALU.add))
            then(v_.tensor_tensor(eidx[:, 1:2], eidx[:, 1:2], ered[:, 3:4], ALU.add))
            v_.tensor_scalar(eidx[:, 0:1], eidx[:, 0:1], float(E - 1), None, ALU.min).then_inc(s_["t_cols"], 1)
            then(v_.tensor_scalar(etmp[:, 0, :], sign_e[:], -1.0, (P - 2) / 2.0, ALU.add, ALU.mult))
            then(v_.tensor_tensor(etmp[:, 1, :], etmp[:, 0, :], run[:], ALU.add))
            then(v_.tensor_copy(prow[:], etmp[0:1, 1, :]))
            dve.wait_ge(s_["t_tr"], 1)
            v_.tensor_copy(trow[:].rearrange("p a b -> p (a b)"), M[0][0:1, 0:2 * P]).then_inc(s_["t_rows"], 1)

            def normed(t):
                j, n, lap, e = t
                dve.wait_ge(t_in[n], lap * 16 + 16)
                wait(dve, s_["f_t"], j + (-1))
                v_.tensor_scalar(gn[:, n % 2, :], gt[:, n, 0:D], gt[:, n, D:D + 1], gt[:, n, D + 1:D + 2],
                                 ALU.mult, ALU.add).then_inc(s_["f_norm"], 1)

            def moved_lo(t):
                j, n, lap, e = t
                dve.wait_ge(s_["f_hi"], j + 1)
                v_.tensor_tensor(gx[:, n % 2, 1, :, :], S[n % 2][:, 0:D].rearrange("p (k t) -> p k t", k=KT),
                                 gx[:, n % 2, 0, :, :], ALU.subtract).then_inc(s_["f_lo"], 1)

            def hidden_lo(t):
                j, n, lap, e = t
                dve.wait_ge(s_["f_hr"], j + 1)
                v_.tensor_tensor(hs[H:P, n % 2, :], hr[H:P, n % 2, :], hs[H:P, n % 2, :], ALU.subtract
                                 ).then_inc(s_["f_hlo"], 1)

            def finish(t):
                j, n, lap, e = t
                dve.wait_ge(s_["f_yr"], j + 1)
                wait(dve, t_out[n], lap * 16)
                v_.scalar_tensor_tensor(out=yo[n], in0=yr[:, n % 2, :], scalar=tg[:, 1:2], in1=gt[:, n, 0:D],
                                        op0=ALU.mult, op1=ALU.add)
                v_.tensor_copy(ido[:, n:n + 1], gt[:, n, D + 2:D + 3].bitcast(U32)).then_inc(s_["f_out"], 1)

            def fstep(at_):
                for d, stage in ((1, normed), (0, moved_lo), (-1, hidden_lo), (-2, finish)):
                    t = at_(d)
                    if t is not None:
                        stage(t)

            tiles_schedule(dve, fstep, lead=1)

        @block.tensor
        def _(pe):
            t_ = nc.tensor
            pe.wait_ge(s_["bv_wide"], 1)
            pe.wait_ge(s_["w_in"], 64)
            for t in range(KT):
                last = t_.matmul(AV[0][:, 0:D], bvb[:, t, :], wraw[:, 2 + t, :], start=(t == 0), stop=(t == KT - 1))
            last.then_inc(s_["bvwo_ready"], 1)
            pe.wait_ge(s_["pool_set"], 1)
            pe.wait_ge(s_["w_lo"], 5)

            def scores(n1, c):
                b, cc = c // 4, c % 4
                if c == 0:
                    pe.wait_ge(stk[n1.par], n1.halved(128, 128))
                    wait(pe, s_["lg_done"], n1.count(1, -2))
                if c == 1:
                    wait(pe, s_["at_lo"], n1.count(2, -2))
                if c >= 2:
                    pe.wait_ge(s_["s_max"], n1.count(CHUNKS, c - 1))
                for i in range(CH):
                    hp = CH * (cc % 2) + i
                    last = t_.matmul(S[c % 2][:, i * P:(i + 1) * P], qstk[0:STACK, n1.par, hp, b * P:(b + 1) * P],
                                     kstk[0:STACK, n1.par, cc // 2, hp, b * P:(b + 1) * P], start=True, stop=True)
                last.then_inc(s_["s_ready"], 1)

            def scores_t(g, c):
                b, cc = c // 4, c % 4
                if c == 0:
                    pe.wait_ge(m_in[g.par], g.halved(32, 32))
                    nv = g.plus(1)
                    pe.wait_ge(s_["v_done"], nv.count(2, 2) if nv.real() else 2 * GROUPS)
                if c >= 2:
                    pe.wait_ge(s_["exp_done"], g.count(CHUNKS, c - 1))
                for i in range(CH):
                    hp = CH * (cc % 2) + i
                    last = t_.matmul(ST[c % 2][:, i * P:(i + 1) * P],
                                     kstk[0:STACK + 2, g.par, cc // 2, hp, b * P:(b + 1) * P],
                                     qstk[0:STACK + 2, g.par, hp, b * P:(b + 1) * P], start=True, stop=True)
                last.then_inc(s_["st_ready"], 1)

            def times_v(g, c):
                b, cc = c // 4, c % 4
                pe.wait_ge(s_["exp_done"], g.count(CHUNKS, c + 1))
                if cc == 0:
                    if b >= 2:
                        pe.wait_ge(s_["av_out"], g.count(4, b - 1))
                    else:
                        wait(pe, s_["x2t_lo"], g.count(2, -4 + b + 1))
                        wait(pe, s_["nrm_done"], g.count(4))
                for i in range(CH):
                    h = (b * HEADS + CH * cc + i) * 32
                    last = t_.matmul(AV[b % 2][32 * i:32 * i + 32, cc * P:(cc + 1) * P], v[:, g.par, h:h + 32],
                                     pt[:, c % NPT, i * P:(i + 1) * P], start=True, stop=True)
                last.then_inc(s_["av_ready"], 1)

            def max_t(n1, b):
                pe.wait_ge(s_["s_max"], n1.count(CHUNKS, 4 * b + 4))
                if b < 2:
                    wait(pe, s_["x2_done"], n1.count(2, -2))
                    r = n1.plus(-3)
                    if b == 1 and r.real():
                        wait(pe, s_["rk_read"], r.count(1, 1))
                else:
                    pe.wait_ge(s_["m_done"], n1.count(4, b - 1))
                t_.transpose(M[(b + 1) % 2][0:HEADS, 0:P], mx[:, b, :], ident[:]).then_inc(s_["mt_ready"], 1)

            def ranks(r):
                pe.wait_ge(s_["hot_done"], r.count(1, 1))
                pe.wait_ge(s_["x2_done"], min_groups(r.plus(1), 2))
                oh = hots[:].rearrange("p b e -> p (b e)")
                t_.matmul(M[0][:, 0:GB * E], tri[:], oh, start=True, stop=False)
                for b in range(1, GB):
                    last_b = b == GB - 1
                    t_.matmul(M[0][:, b * E:GB * E], ones[:], oh[:, 0:(GB - b) * E], start=False, stop=last_b)
                for b in range(GB):
                    last = t_.matmul(M[0][:, GB * E:GB * E + E], ones[:], oh[:, b * E:(b + 1) * E],
                                     start=(b == 0), stop=(b == GB - 1))
                last.then_inc(s_["rk_ready"], 1)

            def min_groups(g, per):
                return g.count(per, per) if g.real() else per * GROUPS

            def split_matmul(bank, pairs):
                for n, (w, m) in enumerate(pairs):
                    last = t_.matmul(bank, w, m, start=(n == 0), stop=(n == len(pairs) - 1))
                return last

            THREE = ((0, 0), (1, 0), (0, 1))

            def step(s):
                a, n1, g, f, r = s.plus(2), s.plus(1), s, s.plus(-1), s.plus(-2)
                for c in range(CHUNKS + 2):
                    if n1.real() and c < CHUNKS:
                        scores(n1, c)
                    if c == 7 and r.real():
                        ranks(r)
                    if g.real() and c < CHUNKS:
                        scores_t(g, c)
                    if g.real() and 1 <= c <= CHUNKS:
                        times_v(g, c - 1)
                    if n1.real() and c in MAX_T:
                        max_t(n1, MAX_T[c])
                if a.real():
                    pe.wait_ge(s_["xn_done"], a.count(1, 1))
                    if n1.real():
                        pe.wait_ge(s_["m_done"], n1.count(4, 4))
                    for t in range(KT):
                        for b in range(GB):
                            last = t_.transpose(M[t][:, b * P:(b + 1) * P], xn[:, b, t * P:(t + 1) * P], ident[:])
                        last.then_inc(s_["xt_ready"], 1)
                if a.real():
                    pe.wait_ge(s_["y_hi"], a.count(3, 3))
                    if g.real():
                        pe.wait_ge(s_["exp_done"], g.count(CHUNKS, CHUNKS))
                    elif n1.real():
                        pe.wait_ge(s_["v_done"], n1.count(2, 2))
                    for m in range(2):
                        col = slice(m * P, (m + 1) * P)
                        split_matmul(ST[m][:], [(wk_s[:, i, t, col], ys[:, j, :]) for i, t, j in
                                                ((0, 0, 0), (1, 0, 0), (0, 0, 1), (0, 1, 2), (1, 1, 2))]
                                     ).then_inc(s_["k_ready"], 1)
                    pe.wait_ge(s_["xt_lo"], a.count(2, 2))
                    for m in range(2):
                        split_matmul(M[m][:], [(wq_s[:, i, t, m * P:(m + 1) * P], xt[:, j, t, :])
                                               for t in range(KT) for i, j in THREE]).then_inc(s_["q_ready"], 1)
                if g.real():
                    banks = [S[0], S[1], AV[0], AV[1]]
                    wait(pe, s_["s_max"], CHUNKS * GROUPS if not n1.real() else n1.count(CHUNKS, CHUNKS))
                    pe.wait_ge(s_["av_out"], g.count(4, 4))
                    for b in range(GB):
                        for cc in range(4):
                            last = t_.transpose(banks[b][:, cc * P:(cc + 1) * P], ot[:, b, cc * P:(cc + 1) * P], ident[:])
                        last.then_inc(s_["o_ready"], 1)
                if a.real():
                    pe.wait_ge(s_["k_lo"], a.count(2, 2))
                    for b in range(GB):
                        tok = slice(b * P, (b + 1) * P)
                        last = split_matmul(ST[b // 2][:, (b % 2) * D:(b % 2) * D + D],
                                            [(ys[:, j, tok], wv_s[:, i, t, :]) for i, t, j in
                                             ((0, 0, 0), (1, 0, 0), (0, 0, 1), (0, 1, 2), (1, 1, 2))])
                        if b % 2:
                            last.then_inc(s_["v_ready"], 1)
                if g.real():
                    pe.wait_ge(s_["nrm_done"], g.count(4, 4))
                    for t in range(KT):
                        for b in range(GB):
                            last = t_.transpose(S[t][:, b * P:(b + 1) * P], an[:, b, t * P:(t + 1) * P], ident[:])
                        last.then_inc(s_["at_ready"], 1)
                if f.real():
                    pe.wait_ge(s_["xn2_done"], f.count(1, 1))
                    for t in range(KT):
                        for b in range(GB):
                            last = t_.transpose(AV[t][:, b * P:(b + 1) * P], xn2[:, b, t * P:(t + 1) * P], ident[:])
                        last.then_inc(s_["x2t_ready"], 1)
                if g.real():
                    pe.wait_ge(s_["at_lo"], g.count(2, 2))
                    if a.real():
                        pe.wait_ge(s_["q_lo"], a.count(2, 2))
                    elif n1.real():
                        pe.wait_ge(s_["m_done"], n1.count(4, 4))
                    elif r.real():
                        pe.wait_ge(s_["rk_read"], r.count(1, 1))
                    for b in range(GB):
                        tok = slice(b * P, (b + 1) * P)
                        last = split_matmul(M[b // 2][:, (b % 2) * D:(b % 2) * D + D],
                                            [(at[:, i, t, tok], wo_s[:, j, t, :]) for t in range(KT) for i, j in THREE])
                        if b % 2:
                            last.then_inc(s_["y_ready"], 1)
                if f.real():
                    pe.wait_ge(s_["x2t_lo"], f.count(2, 2))
                    for b in range(GB):
                        tok = slice(b * P, (b + 1) * P)
                        last = split_matmul(S[0][:, b * E:(b + 1) * E],
                                            [(x2t[:, i * KT + t, tok], rw_s[:, j, t, :]) for t in range(KT) for i, j in THREE])
                    last.then_inc(s_["lg_ready"], 1)

            schedule(pe, step)

            pe.wait_ge(s_["t_cols"], 1)
            for n in range(2):
                last = t_.transpose(M[0][0:1, n * P:(n + 1) * P], eidx[:, n:n + 1], ident[:])
            last.then_inc(s_["t_tr"], 1)
            pe.wait_ge(s_["t_rows"], 1)
            pe.wait_ge(s_["ew_lo"], 2 * GROUPS)
            pe.wait_ge(s_["ew_hi"], 2 * GROUPS)
            pe.wait_ge(s_["b2_rows"], 32)

            def moved(t):
                j, n, lap, e = t
                pe.wait_ge(s_["f_norm"], j + 1)
                wait(pe, s_["f_lo"], j + (-1))
                for k in range(KT):
                    last = t_.transpose(S[n % 2][:, k * P:(k + 1) * P], gn[:, n % 2, k * P:(k + 1) * P], ident[:])
                last.then_inc(s_["f_t"], 1)

            def hidden(t):
                j, n, lap, e = t
                pe.wait_ge(s_["f_lo"], j + 1)
                wait(pe, s_["f_hr"], j + (-1))
                split_matmul(ST[n % 2][:, 0:P],
                             [(w1s[:, i, bass.ds(e * (KT * P) + k * P, P)], gx[:, n % 2, m, k, :])
                              for k in range(KT) for i, m in THREE]).then_inc(s_["f_h"], 1)

            def output(t):
                j, n, lap, e = t
                pe.wait_ge(s_["f_hlo"], j + 1)
                wait(pe, s_["f_yr"], j + (-1))
                cols = bass.ds(e * D, D)
                bank = AV[n % 2][:, 0:D]
                t_.matmul(bank, ones16[:], b2s[:, cols], start=True, stop=False)
                t_.matmul(bank, hs[:, n % 2, :], w2s[:, 0, cols], start=False, stop=False)
                t_.matmul(bank, hs[:, n % 2, :], w2s[:, 1, cols], start=False, stop=True).then_inc(s_["f_y"], 1)

            def fstep(at_):
                t0, t1, t2 = at_(0), at_(-1), at_(-2)
                if t0 is not None:
                    moved(t0)
                if t1 is not None:
                    hidden(t1)
                if t2 is not None:
                    output(t2)

            tiles_schedule(pe, fstep, lead=0, experts=True)


def kernel(x, ctx_768, g_xattn, g_ffn, L0_xattn_wq, L0_xattn_bq, L0_xattn_wk, L0_xattn_bk, L0_xattn_wv, L0_xattn_bv,
           L0_xattn_wo, L0_xattn_bo, L0_ffn_router_w, L0_ffn_router_b, L0_ffn_weights1, L0_ffn_bias1,
           L0_ffn_weights2, L0_ffn_bias2):
    import numpy as np
    import concourse.bacc as bacc
    from concourse.bass_utils import run_bass_kernel_spmd

    def arr(a):
        return np.ascontiguousarray(np.asarray(a))

    def tail_twice(a):
        a = np.asarray(a)
        return np.ascontiguousarray(np.concatenate([a, a[P:DC]], axis=0))

    def twice(a):
        return np.concatenate([a, a], axis=0)

    w1 = np.asarray(L0_ffn_weights1)
    w2 = np.asarray(L0_ffn_weights2)
    arrays = {
        "x": arr(x),
        "ctx_t": tail_twice(np.asarray(ctx_768).reshape(TOKENS, DC).T),
        "g2": arr(np.concatenate([np.asarray(g_xattn), np.asarray(g_ffn)])),
        "wq": arr(L0_xattn_wq),
        "bq": arr(np.asarray(L0_xattn_bq).reshape(KT, P).T),
        "wk": tail_twice(L0_xattn_wk),
        "bk": arr(np.asarray(L0_xattn_bk).reshape(KT, P).T),
        "wv": tail_twice(L0_xattn_wv),
        "bv": arr(np.asarray(L0_xattn_bv).reshape(KT, P).T),
        "wo": arr(L0_xattn_wo),
        "bo": arr(L0_xattn_bo),
        "rw": arr(np.asarray(L0_ffn_router_w).T),
        "rb": arr(L0_ffn_router_b),
        "w1": arr(w1.reshape(E, KT, P, H).transpose(2, 0, 1, 3).reshape(P, E * KT * H)),
        "b1": arr(twice(np.asarray(L0_ffn_bias1).T)),
        "w2": arr(twice(w2.transpose(1, 0, 2).reshape(H, E * D))),
        "b2": arr(L0_ffn_bias2),
    }
    nc = bacc.Bacc("TRN2", target_bir_lowering=False, num_devices=1)
    args = [nc.dram_tensor(name, a.shape, mybir.dt.from_np(a.dtype), kind="ExternalInput").ap() for name, a in arrays.items()]
    out = nc.dram_tensor("out", (TOKENS, D), F32, kind="ExternalOutput").ap()
    build(nc, *args, out)
    r = run_bass_kernel_spmd(nc, [arrays], core_ids=[0])
    return r.results[0]["out"].reshape(BATCHES, P, D)
```

```python
import concourse.bass as bass
from concourse import mybir
from concourse.alu_op_type import AluOpType as ALU
from contextlib import ExitStack

F32, F16, BF16 = mybir.dt.float32, mybir.dt.float16, mybir.dt.bfloat16
U32, I32 = mybir.dt.uint32, mybir.dt.int32
ACT = mybir.ActivationFunctionType
X = mybir.AxisListType.X

P = 128
BATCHES, D, DC = 64, 256, 192
HEADS, DH = 16, 16
E, H = 32, 64
GB = 4
GROUPS = BATCHES // GB
GT = GB * P
TOKENS = BATCHES * P
KT = D // P
HP = HEADS // 2
STACK = 2 * 3 * DH
CHUNKS = 16
CH = 4
NPT = 2
WS = 8.0
MS = 64.0
EPS = 1e-5
ROW = D + 4
REGION = TOKENS + 2 * P
PADS = (E // 2) * REGION
ROWS = PADS + P
TILES_PAD = P
TILES = TOKENS // P + E
PACK = 4
NG = 8
BODY = 24
NOBODY = 1 << 20
LOOP_END = GROUPS - 4
PADS_SP = 20
SLICE = E // GROUPS


class Group:

    def __init__(self, base, off):
        self.base, self.off = base, off
        self.par = off % 2

    def plus(self, d):
        return Group(self.base, self.off + d)

    def real(self):
        return not isinstance(self.base, int) or 0 <= self.off < GROUPS

    def index(self, scale=1, add=0):
        return self.base * (2 * scale) + (self.off * scale + add)

    def count(self, per, k=0):
        return self.index(per, k)

    def halved(self, per, k=0):
        return self.base * per + ((self.off // 2) * per + k)


def wait(eng, sem, value):
    if isinstance(value, int) and value <= 0:
        return
    eng.wait_ge(sem, value)


def build(nc, x, ctx_t, g2, wq, bq, wk, bk, wv, bv, wo, bo, rw, rb, w1, b1, w2, b2, out):
    es = ExitStack()
    with es:
        def sb(name, shape, dt=F32):
            return es.enter_context(nc.sbuf_tensor(name, shape, dt))

        def pb(name):
            return es.enter_context(nc.psum_tensor(name, [P, 512], F32))

        def sem(name):
            return es.enter_context(nc.semaphore(name))

        q_image = nc.dram_tensor("q_image", [2, KT, 2, DH, HP, GT], F16, kind="Internal").ap()
        k_image = nc.dram_tensor("k_image", [2, KT, 2, DH, HP, GT], F16, kind="Internal").ap()
        rows = nc.dram_tensor("expert_rows", [ROWS, ROW], F32, kind="Internal").ap()

        ident = sb("ident", [P, P])
        tri = sb("tri", [P, P], BF16)
        ones = sb("ones", [P, P], BF16)
        ones16 = sb("ones16", [2, P], F16)
        ms_row = sb("ms_row", [1, GT], F16)
        half = sb("half", [P, GB])
        rank_e = sb("rank_e", [P, E])
        sign_e = sb("sign_e", [P, E])
        base_e = sb("base_e", [P, E])
        run = sb("run", [P, E])
        wq_s = sb("wq_s", [P, 2, KT, D], F16)
        wk_s = sb("wk_s", [P, 2, 2, D], F16)
        wv_s = sb("wv_s", [P, 2, 2, D], F16)
        wo_s = sb("wo_s", [P, 2, KT, D], F16)
        rw_s = sb("rw_s", [P, 2, KT, E], F16)
        rb_b = sb("rb_b", [P, E])
        bqk = sb("bqk", [P, 2, KT])
        bqk8 = sb("bqk8", [P, 2, KT])
        bvc = sb("bvc", [P, KT])
        gbias = sb("gbias", [P, D])
        gate = sb("gate", [P, 2])
        tg = sb("tg", [P, 2])
        b1c = sb("b1c", [P, E])
        b2hl = sb("b2hl", [E, 2, D], F16)
        w1s = sb("w1s", [P, 2, E * KT * P], F16)
        w2s = sb("w2s", [P, 2, E * D], F16)
        w1r = sb("w1r", [P, SLICE * KT * H])
        w2r = sb("w2r", [P, SLICE * D])
        pad = sb("pad", [P, ROW])

        xin = sb("xin", [P, GB, D])
        xres = sb("xres", [P, GB, D])
        yin = sb("yin", [P, 2, GT])
        ys = sb("ys", [P, 3, GT], F16)
        st1 = sb("st1", [P, GB, 6])
        mv1 = sb("mv1", [P, GB, 2])
        ve1 = sb("ve1", [P, GB])
        rs1 = sb("rs1", [P, GB])
        nm1 = sb("nm1", [P, GB])
        xn = sb("xn", [P, GB, D])
        xt = sb("xt", [P, 2, KT, GT], F16)
        qs = sb("qs", [P, 2, KT, GT], F16)
        ks = sb("ks", [P, 2, KT, GT], F16)
        qstk = sb("qstk", [P, 2, HP, GT], F16)
        kstk = sb("kstk", [P, 2, 2, HP, GT], F16)
        v = sb("v", [P, 2, GB * HEADS * 32])
        mx = sb("mx", [P, GB, HEADS])
        mrow = sb("mrow", [HEADS, GT], F16)
        pt = sb("pt", [P, NPT, CH * P])
        ot = sb("ot", [P, GB, 512])
        rec = sb("rec", [P, GB, HEADS])
        an = ot[:, :, 0:D]
        at = xt
        x2 = sb("x2", [P, 2, GB, ROW])
        st2 = sb("st2", [P, GB, 6])
        mv2 = sb("mv2", [P, GB, 2])
        ve2 = sb("ve2", [P, GB])
        nm2 = sb("nm2", [P, GB])
        xn2 = sb("xn2", [P, GB, D])
        wraw = xn2
        wraw2 = xres
        ot_flat = ot[:].rearrange("p a n -> p (a n)")
        bvb = ot_flat[:, 0:KT * P].rearrange("p (k n) -> p k n", k=KT)
        bo_b = ot_flat[:, 2 * P:2 * P + D]
        b2raw = ot_flat[0:E, 4 * P:4 * P + D]
        rw_raw = ot_flat[:, 6 * P:6 * P + KT * E].rearrange("p (k e) -> p k e", k=KT)
        x2t = ot[:, :, D:2 * D].bitcast(F16)
        lg = sb("lg", [P, GB, E])
        lmax = sb("lmax", [P, GB])
        pick = sb("pick", [P, GB, E])
        first = sb("first", [P, GB])
        hot = sb("hot", [P, GB, E])
        hots = sb("hots", [P, GB, E], BF16)
        posn = sb("posn", [P, GB, E])
        pos = sb("pos", [P, GB])
        posi = sb("posi", [P, GB], U32)
        ids = sb("ids", [P, GB], I32)

        cnt = sb("cnt", [P, E])
        til = sb("til", [P, E])
        end = sb("end", [P, E])
        zero_e = sb("zero_e", [P, E])
        zero_ids = sb("zero_ids", [P, GB], I32)
        eps_c = sb("eps_c", [P, GB])
        minus = sb("minus", [P, GB])
        group_c = sb("group_c", [P, GB], I32)
        carry_p = sb("carry_p", [P, 8])
        carry_v = sb("carry_v", [P, 4])
        jcol = sb("jcol", [P, 1])
        iota_e = sb("iota_e", [P, E])
        ecmp = sb("ecmp", [P, E])
        eidx = sb("eidx", [P, 2])
        ehot = sb("ehot", [P, E])
        etmp = sb("etmp", [P, 4, E])
        ered = sb("ered", [P, 4])
        places = sb("places", [1, TILES_PAD // PACK, PACK])
        trow = w1r[0:1, 0:2 * P].bitcast(U32).rearrange("p (a b) -> p a b", a=2)
        pidx = sb("pidx", [P, E], U32)
        prow = sb("prow", [1, E], U32)

        yin_flat = yin[:].rearrange("p a n -> p (a n)")
        gt = x2[:].rearrange("p a b n -> p (a b) n")
        yr = xn2[:, 0:2, :]
        ido = posn[:].rearrange("p b e -> p (b e)")[:, 0:NG].bitcast(U32)
        yo = [buf[:, b, :] for buf in (xin, xn) for b in range(GB)]
        gn = yin_flat[:, 0:2 * D].rearrange("p (g n) -> p g n", g=2)
        hr = yin_flat[:, 2 * D:2 * D + 2 * P].rearrange("p (g n) -> p g n", g=2)
        b2s = qstk[0:2, :, :, :].rearrange("p a b n -> p (a b n)")
        gx = qs[:].rearrange("p a k t -> p (a k t)")[:, 0:4 * KT * P].rearrange("p (g a k t) -> p g a k t", g=2, a=2, k=KT)
        hs = ks[:].rearrange("p a k t -> p (a k t)")[:, 0:2 * P].rearrange("p (g t) -> p g t", g=2)

        S = [pb("S0"), pb("S1")]
        ST = [pb("ST0"), pb("ST1")]
        AV = [pb("AV0"), pb("AV1")]
        M = [pb("M0"), pb("M1")]

        names = """consts w_in w_in2 w_raw8 w_hi w_lo g_in tanh_done bias_in bv_wide bvwo_ready
        gb_a gb_done row_in dve_set pool_set b2_hi b2_lo b2_rows
        ln1_st ln1_mv ln1_sm xn_done y_hi y_t xt_ready xt_hi xt_lo q_ready q_hi q_lo k_ready k_hi k_lo
        v_ready v_done
        s_ready s_max mt_ready m_done st_ready exp_done av_ready av_out o_ready nrm_r nrm_done at_ready
        at_hi at_lo xb_done y_ready x2_done ln2_st ln2_mv ln2_sm xn2_done x2t_ready x2t_hi x2t_lo
        lg_ready lg_done route hot_done rk_ready rk_read rk_link pos_done ids_done
        ew_r8 ew_hi ew_lo
        t_link p_rows t_cols t_tr t_rows
        f_norm f_t f_hi f_lo f_h f_hs f_hr f_hlo f_y f_yr f_out f_carry""".split()
        s_ = {n: sem(n) for n in names}
        x_in = [sem("x_in0"), sem("x_in1")]
        y_in = [sem("y_in0"), sem("y_in1")]
        xr_in = [sem("xr_in0"), sem("xr_in1")]
        ew_in = sem("ew_in")
        q_out = sem("q_out")
        k_out = sem("k_out")
        stk = [sem("stk0"), sem("stk1")]
        m_in = [sem("m_in0"), sem("m_in1")]
        scat = [sem("scat0"), sem("scat1")]
        pad_out = sem("pad_out")
        pads_done = sem("pads_done")
        pads_pool = sem("pads_pool")
        t_in = [sem(f"t_in{n}") for n in range(NG)]
        t_out = [sem(f"t_out{n}") for n in range(NG)]

        MAX_T = {5: 0, 12: 1, 13: 2}
        MAX_ROW = {6: 0, 13: 1, 14: 2}

        block = es.enter_context(nc.Block())

        def schedule(eng, step):
            for n in range(-3, 2):
                step(Group(0, n))
            with eng.Fori(1, LOOP_END // 2) as it:
                step(Group(it, 0))
                step(Group(it, 1))
            for n in range(LOOP_END, GROUPS + 2):
                step(Group(0, n))

        def load_row(eng, row, first, n, top):
            return nc.values_load_multi_w_load_instructions(trow[0:1, row, bass.ds(first, n)], engines=[eng.engine],
                                                            min_val=0, max_val=top)[1]

        def tiles_schedule(eng, fstep, lead, experts=(), scale=1):
            def tiles(at_, words, first, held):
                def get(d):
                    t = at_(d)
                    if t is None:
                        return None
                    j = t[3]
                    if d in experts and j not in held:
                        word = words[j // PACK - first]
                        held[j] = eng.snap(((word >> (5 * (j % PACK))) & (E - 1)) * scale)
                    return (t[0], t[1], t[2], held.get(j))
                return get

            def load_words(first, n):
                return load_row(eng, 0, first, n, E ** PACK - 1) if experts else None

            def known(t):
                def at_(d):
                    j = t + d
                    return (j, j % NG, j // NG, j) if 0 <= j < TILES else None
                return at_

            def looped(it, u):
                def at_(d):
                    j = u + d
                    return (it * BODY + j, j % NG, it * (BODY // NG) + (j // NG), j)
                return at_

            words, held = load_words(0, BODY // PACK), {}
            for t in range(-lead, BODY):
                fstep(tiles(known(t), words, 0, held))
            with eng.Fori(1, TILES // BODY - 1) as it:
                words, held = load_words(it * (BODY // PACK) + (-1), BODY // PACK + 1), {}
                for u in range(BODY):
                    fstep(tiles(looped(it, u), words, -1, held))
            first = (TILES - BODY) // PACK - 1
            words, held = load_words(first, BODY // PACK + 1), {}
            for t in range(TILES - BODY, TILES + 4):
                fstep(tiles(known(t), words, first, held))

        @block.sync
        def _(sp):
            sp.dma_start(wraw[:, 0:2, :], wq.rearrange("(t p) n -> p t n", p=P)).then_inc(s_["w_in"], 16)
            sp.dma_start(wraw[:, 2:4, :], wk.rearrange("(t p) n -> p t n", p=P)).then_inc(s_["w_in"], 16)

            def load_x(a):
                if not a.real():
                    return
                wait(sp, s_["xn_done"], a.count(1))
                sp.dma_start(xin[:, :, :],
                             x[bass.ds(a.index(GB), GB), :, :].rearrange("b p n -> p b n")).then_inc(x_in[a.par], 16)
                wait(sp, s_["y_hi"], a.count(3))
                sp.dma_start(yin[:, :, :],
                             ctx_t[:, bass.ds(a.index(GT), GT)].rearrange("(t p) n -> p t n", p=P)).then_inc(y_in[a.par], 16)

            load_x(Group(0, 0))
            sp.dma_start(gate[:, :], g2.partition_broadcast(P)).then_inc(s_["g_in"], 16)
            sp.dma_start(bqk[:, 0, :], bq).then_inc(s_["bias_in"], 16)
            sp.dma_start(bqk[:, 1, :], bk).then_inc(s_["bias_in"], 16)
            sp.dma_start(bvc[:, :], bv).then_inc(s_["bias_in"], 16)
            sp.dma_start(bo_b[:, :], bo.partition_broadcast(P)).then_inc(s_["bias_in"], 16)
            sp.dma_start(b1c[:, :], b1).then_inc(s_["bias_in"], 16)
            sp.dma_start(b2raw[:, :], b2).then_inc(s_["bias_in"], 16)
            sp.dma_start(rw_raw[:, :, :], rw.rearrange("(t p) n -> p t n", p=P)).then_inc(s_["bias_in"], 16)
            sp.dma_start(rb_b[:, :], rb.partition_broadcast(P)).then_inc(s_["bias_in"], 16)
            sp.dma_start(wraw2[:, 0:2, :], wv.rearrange("(t p) n -> p t n", p=P)).then_inc(s_["w_in2"], 16)
            sp.dma_start(wraw2[:, 2:4, :], wo.rearrange("(t p) n -> p t n", p=P)).then_inc(s_["w_in2"], 16)
            sp.wait_ge(s_["pool_set"], 1)
            sp.dma_start(rows[PADS:PADS + P, :], pad[:, :]).then_inc(pad_out, 16)
            sp.wait_ge(s_["dve_set"], 1)
            for par in range(2):
                for half in range(KT):
                    sp.dma_start(kstk[STACK + half:STACK + half + 1, par, half, :, :],
                                 ms_row[:].unsqueeze(1).to_broadcast([1, HP, GT])).then_inc(s_["row_in"], 16)
            sp.wait_ge(s_["row_in"], 16 * 4)

            def step(s):
                a, n1, g = s.plus(2), s.plus(1), s
                if not (isinstance(s.base, int) and s.off == -3):
                    load_x(s.plus(3))
                if a.real():
                    wait(sp, s_["ew_r8"], a.count(2))
                    wait(sp, s_["ew_lo"], a.count(2))
                    sp.dma_start(w1r[:, :], w1[:, bass.ds(a.index(SLICE * KT * H), SLICE * KT * H)]).then_inc(ew_in, 16)
                    sp.dma_start(w2r[:, :], w2[:, bass.ds(a.index(SLICE * D), SLICE * D)]).then_inc(ew_in, 16)
                    for t in range(KT):
                        wait(sp, s_["k_hi"], a.count(2, t + 1))
                        sp.dma_start(k_image[a.par, t, 0].rearrange("d j n -> j d n"), ks[:, 0, t, :]
                                     ).then_inc(k_out, 16)
                    for t in range(KT):
                        wait(sp, s_["k_lo"], a.count(2, t + 1))
                        sp.dma_start(k_image[a.par, t, 1].rearrange("d j n -> j d n"), ks[:, 1, t, :]
                                     ).then_inc(k_out, 16)
                    for t in range(KT):
                        wait(sp, s_["q_hi"], a.count(2, t + 1))
                        sp.dma_start(q_image[a.par, t, 1].rearrange("d j n -> j d n"), qs[:, 0, t, :]
                                     ).then_inc(q_out, 16)
                    for t in range(KT):
                        wait(sp, s_["q_lo"], a.count(2, t + 1))
                        sp.dma_start(q_image[a.par, t, 0].rearrange("d j n -> j d n"), qs[:, 1, t, :]
                                     ).then_inc(q_out, 16)

                    def stack(dst, src, first):
                        for t in range(KT):
                            rows_of = STACK // 2 * t
                            sp.dma_start(dst(t)[rows_of:rows_of + DH], src[t, first]).then_inc(stk[a.par], 16)
                            sp.dma_start(dst(t)[rows_of + DH:rows_of + 3 * DH], src[t].rearrange("a d j n -> (a d) j n")
                                         ).then_inc(stk[a.par], 16)

                    wait(sp, k_out, a.count(64, 64))
                    stack(lambda t: kstk[:, a.par, t, :, :], k_image[a.par], 0)
                    wait(sp, q_out, a.count(64, 64))
                    stack(lambda t: qstk[:, a.par, :, :], q_image[a.par], 1)
                if n1.real():
                    wait(sp, s_["m_done"], n1.count(4, 4))
                    for half in range(2):
                        sp.dma_start(qstk[STACK + half:STACK + half + 1, n1.par, :, :],
                                     mrow[HP * half:HP * half + HP, :]).then_inc(m_in[n1.par], 16)
                if n1.real():
                    wait(sp, s_["x2_done"], n1.count(2))
                    sp.dma_start(xres[:, :, :],
                                 x[bass.ds(n1.index(GB), GB), :, :].rearrange("b p n -> p b n")).then_inc(xr_in[n1.par], 16)

            schedule(sp, step)

            sp.wait_ge(s_["b2_lo"], 1)
            sp.wait_ge(s_["st_ready"], CHUNKS * GROUPS)
            for n in range(2):
                sp.dma_start(b2s[n:n + 1, :], b2hl[:, n, :]).then_inc(s_["b2_rows"], 16)
            sp.wait_ge(s_["p_rows"], 2)
            for e in range(0, PADS_SP, NG // 2):
                pads = nc.values_load_multi_w_load_instructions(prow[0:1, e:e + NG // 2], engines=[sp.engine],
                                                                min_val=0, max_val=PADS)[1]
                for r in pads:
                    sp.dma_start(rows[bass.ds(r, P), :], pad[:, :]).then_inc(pads_done, 16)
            sp.wait_ge(pads_done, 16 * PADS_SP)
            sp.wait_ge(pads_pool, 16 * (E - PADS_SP))
            sp.wait_ge(pad_out, 16)
            sp.wait_ge(s_["t_rows"], 1)
            wait(sp, scat[0], 16 * GB * GROUPS // 2)
            wait(sp, scat[1], 16 * GB * GROUPS // 2)

            def tile(n, lap, r):
                wait(sp, s_["f_out"], lap * NG + (n + 1 - NG))
                sp.dma_start(gt[:, n, :], rows[bass.ds(r, P), :]).then_inc(t_in[n], 16)

            first = load_row(sp, 1, 0, NG, PADS)
            for n in range(NG):
                tile(n, 0, first[n])
            with sp.Fori(1, TILES // NG) as it:
                for m in range(0, NG, NG // 2):
                    first = load_row(sp, 1, it * NG + m, NG // 2, PADS)
                    for n in range(NG // 2):
                        tile(m + n, it, first[n])
            for n in range(NG):
                wait(sp, t_out[n], 16 * TILES // NG)

        @block.gpsimd
        def _(pool):
            g_ = nc.gpsimd

            def carry(site):
                return g_.tensor_tensor(carry_p[:, site:site + 1], zero_e[:, 0:1], zero_e[:, 0:1], ALU.add)

            g_.memset(ident[:], 0.0)
            g_.memset(tri[:], 1.0)
            g_.memset(ones[:], 1.0)
            g_.memset(ones16[:], 1.0)
            g_.memset(half[:], -0.5)
            g_.memset(zero_e[:], 0.0)
            g_.memset(eps_c[:], EPS)
            g_.memset(minus[:], -1.0)
            g_.memset(group_c[:], GT)
            g_.memset(zero_ids[:], 0)
            g_.memset(hots[:], 0.0)
            g_.iota(rank_e[:], pattern=[[-1, E]], base=E, channel_multiplier=0, allow_small_or_imprecise_dtypes=True)
            g_.iota(iota_e[:], pattern=[[1, E]], base=0, channel_multiplier=0, allow_small_or_imprecise_dtypes=True)
            g_.iota(jcol[:], pattern=[[0, 1]], base=0, channel_multiplier=1, allow_small_or_imprecise_dtypes=True)
            g_.iota(ids[:], pattern=[[P, GB]], base=-GT, channel_multiplier=1)
            g_.iota(base_e[:].rearrange("p (i o) -> p i o", o=2), pattern=[[REGION, E // 2], [REGION - 1, 2]],
                    base=0, channel_multiplier=0, allow_small_or_imprecise_dtypes=True)
            g_.iota(sign_e[:].rearrange("p (i o) -> p i o", o=2), pattern=[[0, E // 2], [-2, 2]],
                    base=1, channel_multiplier=0, allow_small_or_imprecise_dtypes=True)
            g_.memset(ms_row[:], MS)
            for n in range(PACK):
                g_.memset(places[:, :, n:n + 1], float(E ** n))
            g_.memset(kstk[:, :, 1, :, :], 0.0)
            g_.memset(v[:], 1.0)
            g_.memset(x2[:, :, :, D + 3:D + 4], 0.0)
            g_.memset(pad[:], 0.0).then_inc(s_["consts"], 1)
            pool.wait_ge(s_["consts"], 1)
            g_.memset(pad[:, D + 2:D + 3].bitcast(U32), NOBODY)
            g_.tensor_copy(run[:], base_e[:])
            g_.affine_select(out=tri[:], in_=tri[:], compare_op=ALU.is_gt, fill=0.0, base=0,
                             pattern=[[1, P]], channel_multiplier=-1)
            g_.affine_select(out=ident[:], in_=ident[:], compare_op=ALU.not_equal, fill=1.0, base=0,
                             pattern=[[1, P]], channel_multiplier=-1).then_inc(s_["pool_set"], 1)
            pool.wait_ge(s_["pool_set"], 1)

            def norm_scale(mv, st, ve, rs, nm, shift, k0):
                link = s_[st]
                g_.tensor_tensor(ve, mv[:, :, 1], eps_c[:], ALU.add).then_inc(link, 1)
                wait(pool, link, k0(1))
                g_.tensor_tensor(rs, ve, half[:], ALU.pow).then_inc(link, 1)
                wait(pool, link, k0(2))
                g_.tensor_tensor(nm, mv[:, :, 0], rs, ALU.mult).then_inc(link, 1)
                wait(pool, link, k0(3))
                g_.tensor_tensor(shift, nm, minus[:], ALU.mult).then_inc(link, 1)
                wait(pool, link, k0(4))

            def step(s):
                a, n1, g, f, r = s.plus(2), s.plus(1), s, s.plus(-1), s.plus(-2)
                if n1.real():
                    wait(pool, s_["ew_hi"], n1.count(2, 2))
                    o1, c1 = n1.index(SLICE * KT * P), SLICE * KT * P
                    g_.tensor_tensor(w1s[:, 1, bass.ds(o1, c1)].rearrange("p (c u n) -> p c u n", u=2, n=H),
                                     w1r[:].rearrange("p (c n) -> p c n", n=H).unsqueeze(2).to_broadcast([P, SLICE * KT, 2, H]),
                                     w1s[:, 0, bass.ds(o1, c1)].rearrange("p (c u n) -> p c u n", u=2, n=H),
                                     ALU.subtract).then_inc(s_["ew_lo"], 1)
                    o2, c2 = n1.index(SLICE * D), SLICE * D
                    g_.tensor_tensor(w2s[:, 1, bass.ds(o2, c2)], w2r[:], w2s[:, 0, bass.ds(o2, c2)],
                                     ALU.subtract).then_inc(s_["ew_lo"], 1)
                if a.real():
                    wait(pool, y_in[a.par], a.halved(16, 16))
                    wait(pool, s_["v_ready"], a.count(2))
                    wait(pool, s_["k_ready"], a.count(2))
                    zeros = zero_e[:, 0:1].to_broadcast([P, GT])
                    g_.tensor_tensor(ys[:, 0, :], yin[:, 0, :], zeros, ALU.add).then_inc(s_["y_t"], 1)
                    g_.tensor_tensor(ys[:, 2, :], yin[:, 1, :], zeros, ALU.add).then_inc(s_["y_t"], 1)
                    wait(pool, s_["y_t"], a.count(2, 2))
                    g_.tensor_tensor(ys[:, 1, :], yin[:, 0, :], ys[:, 0, :], ALU.subtract).then_inc(s_["y_hi"], 1)
                    wait(pool, s_["y_hi"], a.count(3, 1))
                    sent = a.plus(-5)
                    if sent.real():
                        wait(pool, scat[sent.par], sent.halved(16 * GB, 16 * GB))
                    g_.tensor_tensor(ys[H:P, 2, :], yin[H:P, 1, :], ys[H:P, 2, :], ALU.subtract).then_inc(s_["y_hi"], 2)
                    wait(pool, s_["y_hi"], a.count(3, 3))
                    wait(pool, s_["ln1_mv"], a.count(GB, GB))
                    norm_scale(mv1, "ln1_sm", ve1[:], rs1[:], nm1[:], ve1[:], lambda k: a.count(4, k))
                    wait(pool, s_["xt_ready"], a.count(2))
                    carry(s.par)
                    for b in range(GB):
                        last = g_.tensor_scalar(xn[:, b, :], xin[:, b, :], rs1[:, b:b + 1], ve1[:, b:b + 1],
                                                ALU.mult, ALU.add)
                    last.then_inc(s_["xn_done"], 1)
                if f.real():
                    wait(pool, s_["ln2_mv"], f.count(GB, GB))
                    wait(pool, s_["ids_done"], f.count(2))
                    g_.tensor_tensor(ids[:], ids[:], group_c[:], ALU.add).then_inc(s_["ids_done"], 1)
                    norm_scale(mv2, "ln2_sm", ve2[:], x2[:, f.par, :, D], nm2[:], x2[:, f.par, :, D + 1], lambda k: f.count(4, k))
                    wait(pool, s_["ids_done"], f.count(2, 1))
                    g_.tensor_tensor(x2[:, f.par, :, D + 2].bitcast(I32), ids[:], zero_ids[:], ALU.add).then_inc(s_["ids_done"], 1)
                    wait(pool, s_["x2t_ready"], f.count(2))
                    carry(4 + s.par)
                    for b in range(GB):
                        last = g_.tensor_scalar(xn2[:, b, :], x2[:, f.par, b, 0:D], x2[:, f.par, b, D:D + 1],
                                                x2[:, f.par, b, D + 1:D + 2], ALU.mult, ALU.add)
                    last.then_inc(s_["xn2_done"], 1)
                if g.real():
                    wait(pool, xr_in[g.par], g.halved(16, 16))
                    if isinstance(g.base, int) and g.off == 0:
                        pool.wait_ge(s_["gb_done"], 1)
                    g_.tensor_tensor(xres[:, :, :], xres[:, :, :],
                                     gbias[:].unsqueeze(1).to_broadcast([P, GB, D]), ALU.add).then_inc(s_["xb_done"], 1)
                if r.real():
                    wait(pool, s_["pos_done"], r.count(1, 1))
                    carry(2 + s.par)
                    for b in range(GB):
                        g_.indirect_dma_start(out=rows[:, :], out_offset=bass.IndirectOffsetOnAxis(ap=posi[:, b:b + 1], axis=0),
                                              in_=x2[:, r.par, b, :], in_offset=None).then_inc(scat[r.par], 16)

            schedule(pool, step)

            pool.wait_ge(s_["p_rows"], 2)
            for e in range(PADS_SP, E):
                g_.indirect_dma_start(out=rows[:, :], out_offset=bass.IndirectOffsetOnAxis(ap=pidx[:, e:e + 1], axis=0),
                                      in_=pad[:, :], in_offset=None).then_inc(pads_pool, 16)

            def two_tiles(n, lap):
                wait(pool, s_["f_carry"], lap * (NG // 2) + (n // 2 + 1))
                wait(pool, s_["f_out"], lap * NG + (n + 2))
                carry(6).then_inc(s_["f_carry"], 1)
                for m in (n, n + 1):
                    g_.indirect_dma_start(out=out, out_offset=bass.IndirectOffsetOnAxis(ap=ido[:, m:m + 1], axis=0),
                                          in_=yo[m], in_offset=None, bounds_check=TOKENS - 1, oob_is_err=False
                                          ).then_inc(t_out[m], 16)

            carry(7).then_inc(s_["f_carry"], 1)
            with pool.Fori(0, TILES // NG) as it:
                for n in range(0, NG, 2):
                    two_tiles(n, it)

        @block.scalar
        def _(act):
            a_ = nc.scalar

            def scaled(raw):
                for t in range(2):
                    a_.activation(raw[:, t, :], raw[:, t, :], ACT.Copy, scale=WS).then_inc(s_["w_raw8"], 1)

            act.wait_ge(s_["g_in"], 16)
            a_.activation(tg[:], gate[:], ACT.Tanh).then_inc(s_["tanh_done"], 1)
            act.wait_ge(s_["w_in"], 32)
            scaled(wraw[:, 0:2, :])
            scaled(wraw[:, 2:4, :])
            act.wait_ge(s_["w_raw8"], 4)
            a_.copy(wq_s[:, 0, :, :], wraw[:, 0:2, :]).then_inc(s_["w_hi"], 1)
            a_.copy(wk_s[:, 0, :, :], wraw[:, 2:4, :]).then_inc(s_["w_hi"], 1)
            act.wait_ge(s_["bias_in"], 16 * 8)
            a_.activation(bqk8[:], bqk[:], ACT.Copy, scale=WS).then_inc(s_["w_hi"], 1)
            a_.activation(b2raw[:], b2raw[:], ACT.Copy, scale=WS).then_inc(s_["w_hi"], 1)
            a_.activation(rw_raw[:], rw_raw[:], ACT.Copy, scale=WS).then_inc(s_["w_hi"], 1)
            act.wait_ge(s_["w_hi"], 5)
            a_.copy(b2hl[:, 0, :], b2raw[:]).then_inc(s_["b2_hi"], 1)
            a_.copy(rw_s[:, 0, :, :], rw_raw[:]).then_inc(s_["b2_hi"], 1)
            a_.copy(bvb[:], bvc[:].unsqueeze(2).to_broadcast([P, KT, P])).then_inc(s_["bv_wide"], 1)
            act.wait_ge(s_["w_in2"], 32)
            scaled(wraw2[:, 0:2, :])
            act.wait_ge(s_["w_raw8"], 6)
            a_.copy(wv_s[:, 0, :, :], wraw2[:, 0:2, :]).then_inc(s_["w_hi"], 1)
            act.wait_ge(s_["bvwo_ready"], 1)
            act.wait_ge(s_["tanh_done"], 1)
            a_.activation(wraw2[:, 2:4, :], wraw2[:, 2:4, :], ACT.Copy, scale=WS).then_inc(s_["w_raw8"], 1)
            act.wait_ge(s_["w_raw8"], 7)
            a_.activation(wraw2[:, 2:4, :], wraw2[:, 2:4, :], ACT.Identity, scale=tg[:, 0:1]).then_inc(s_["w_raw8"], 1)
            act.wait_ge(s_["w_raw8"], 8)
            a_.copy(wo_s[:, 0, :, :], wraw2[:, 2:4, :]).then_inc(s_["w_hi"], 1)

            def exp_chunk(g, c):
                act.wait_ge(s_["st_ready"], g.count(CHUNKS, c + 1))
                wait(act, s_["av_ready"], g.count(CHUNKS, c + 1 - NPT))
                a_.activation(pt[:, c % NPT, :], ST[c % 2][:], ACT.Exp,
                              scale=0.25 / (WS * WS)).then_inc(s_["exp_done"], 1)

            def attn_out(g, b):
                act.wait_ge(s_["av_ready"], g.count(CHUNKS, 4 * b + 4))
                wait(act, s_["lg_ready"], g.count(1, -1))
                a_.copy(ot[:, b, :], AV[b % 2][:]).then_inc(s_["av_out"], 1)

            def max_row(n1, b):
                act.wait_ge(s_["mt_ready"], n1.count(4, b + 1))
                prev = n1.plus(-1)
                if prev.real():
                    wait(act, m_in[prev.par], prev.halved(32, 32))
                a_.activation(mrow[:, b * P:(b + 1) * P], (S[0] if b == 3 else M[(b + 1) % 2])[0:HEADS, 0:P], ACT.Copy,
                              scale=-1.0 / MS).then_inc(s_["m_done"], 1)

            def expert_raw(a):
                act.wait_ge(ew_in, a.count(32, 32))
                a_.activation(w1r[:], w1r[:], ACT.Copy, scale=WS).then_inc(s_["ew_r8"], 1)
                a_.activation(w2r[:], w2r[:], ACT.Copy, scale=WS).then_inc(s_["ew_r8"], 1)

            def expert_hi(a):
                act.wait_ge(s_["ew_r8"], a.count(2, 2))
                a_.copy(w1s[:, 0, bass.ds(a.index(SLICE * KT * P), SLICE * KT * P)].rearrange("p (c u n) -> p c u n", u=2, n=H),
                        w1r[:].rearrange("p (c n) -> p c n", n=H).unsqueeze(2).to_broadcast([P, SLICE * KT, 2, H])
                        ).then_inc(s_["ew_hi"], 1)
                a_.copy(w2s[:, 0, bass.ds(a.index(SLICE * D), SLICE * D)], w2r[:]).then_inc(s_["ew_hi"], 1)

            def step(s):
                a, n1, g, f = s.plus(2), s.plus(1), s, s.plus(-1)
                for c in range(CHUNKS):
                    if g.real():
                        exp_chunk(g, c)
                        if c % 4 == 2 and c > 4:
                            attn_out(g, c // 4 - 1)
                    if n1.real() and c in MAX_ROW:
                        max_row(n1, MAX_ROW[c])
                if a.real():
                    for t in range(KT):
                        act.wait_ge(s_["xt_ready"], a.count(2, t + 1))
                        wait(act, s_["y_ready"], a.count(2, -4))
                        a_.copy(xt[:, 0, t, :], M[t][:]).then_inc(s_["xt_hi"], 1)
                if g.real():
                    attn_out(g, 3)
                for t in range(KT):
                    if a.real():
                        act.wait_ge(s_["k_ready"], a.count(2, t + 1))
                        wait(act, k_out, a.count(64))
                        a_.activation(ks[:, 0, t, :], ST[t][:], ACT.Identity, bias=bqk8[:, 1, t:t + 1]).then_inc(s_["k_hi"], 1)
                    if n1.real() and t == 0:
                        max_row(n1, 3)
                if a.real():
                    for t in range(KT):
                        act.wait_ge(s_["q_ready"], a.count(2, t + 1))
                        wait(act, q_out, a.count(64))
                        a_.activation(qs[:, 0, t, :], M[t][:], ACT.Identity, bias=bqk8[:, 0, t:t + 1]).then_inc(s_["q_hi"], 1)
                if g.real():
                    for t in range(KT):
                        act.wait_ge(s_["at_ready"], g.count(2, t + 1))
                        if a.real():
                            act.wait_ge(s_["q_ready"], a.count(2, 2))
                        a_.copy(at[:, 0, t, :], S[t][:]).then_inc(s_["at_hi"], 1)
                if a.real():
                    for t in range(2):
                        act.wait_ge(s_["v_ready"], a.count(2, t + 1))
                        wait(act, s_["av_ready"], a.count(CHUNKS, -CHUNKS))
                        vv = v[:, a.par, t * 1024:t * 1024 + 1024].rearrange("p (h d) -> p h d", d=32)[:, :, 0:DH]
                        a_.activation(vv, ST[t][:].rearrange("p (h d) -> p h d", d=DH), ACT.Copy,
                                      scale=1.0 / WS).then_inc(s_["v_done"], 1)
                if f.real():
                    for t in range(KT):
                        act.wait_ge(s_["x2t_ready"], f.count(2, t + 1))
                        a_.copy(x2t[:, t, :], AV[t][:]).then_inc(s_["x2t_hi"], 1)
                if a.real():
                    expert_raw(a)
                    expert_hi(a)

            schedule(act, step)

            act.wait_ge(s_["t_rows"], 1)

            def moved_hi(t):
                j, n, lap, e = t
                act.wait_ge(s_["f_t"], j + 1)
                wait(act, s_["f_h"], j + (-1))
                a_.copy(gx[:, n % 2, 0, :, :], S[n % 2][:, 0:D].rearrange("p (k t) -> p k t", k=KT)).then_inc(s_["f_hi"], 1)

            def hidden(t):
                j, n, lap, e = t
                act.wait_ge(s_["f_h"], j + 1)
                wait(act, s_["f_y"], j + (-1))
                a_.activation(hs[:, n % 2, :], ST[n % 2][:, 0:P], ACT.Relu, bias=b1c[:, bass.ds(e, 1)],
                              scale=1.0 / WS).then_inc(s_["f_hs"], 1)
                a_.activation(hr[H:P, n % 2, :], ST[n % 2][H:P, 0:P], ACT.Relu, bias=b1c[H:P, bass.ds(e, 1)],
                              scale=1.0 / WS).then_inc(s_["f_hr"], 1)

            def relu_out(t):
                j, n, lap, e = t
                act.wait_ge(s_["f_y"], j + 1)
                wait(act, s_["f_out"], j + (-1))
                a_.activation(yr[:, n % 2, :], AV[n % 2][:, 0:D], ACT.Relu, scale=1.0 / WS).then_inc(s_["f_yr"], 1)

            def fstep(at_):
                for d, stage in ((0, moved_hi), (-2, hidden), (-4, relu_out)):
                    t = at_(d)
                    if t is not None:
                        stage(t)

            tiles_schedule(act, fstep, lead=0, experts=(-2,))

        @block.vector
        def _(dve):
            v_ = nc.vector

            def carry(site):
                v_.tensor_copy(carry_v[:, site:site + 1], tg[:, 0:1])

            dve.wait_ge(s_["w_hi"], 2)
            v_.tensor_tensor(wq_s[:, 1, :, :], wraw[:, 0:2, :], wq_s[:, 0, :, :], ALU.subtract).then_inc(s_["w_lo"], 1)
            v_.tensor_tensor(wk_s[:, 1, :, :], wraw[:, 2:4, :], wk_s[:, 0, :, :], ALU.subtract).then_inc(s_["w_lo"], 1)
            dve.wait_ge(s_["b2_hi"], 2)
            v_.tensor_tensor(b2hl[:, 1, :], b2raw[:], b2hl[:, 0, :], ALU.subtract).then_inc(s_["b2_lo"], 1)
            v_.tensor_tensor(rw_s[:, 1, :, :], rw_raw[:], rw_s[:, 0, :, :], ALU.subtract).then_inc(s_["w_lo"], 1)
            v_.memset(kstk[:, :, 0, :, :], 0.0).then_inc(s_["dve_set"], 1)
            dve.wait_ge(s_["w_hi"], 6)
            v_.tensor_tensor(wv_s[:, 1, :, :], wraw2[:, 0:2, :], wv_s[:, 0, :, :], ALU.subtract).then_inc(s_["w_lo"], 1)
            dve.wait_ge(s_["bvwo_ready"], 1)
            v_.tensor_tensor(gbias[:], AV[0][:, 0:D], bo_b[:], ALU.add).then_inc(s_["gb_a"], 1)
            dve.wait_ge(s_["gb_a"], 1)
            dve.wait_ge(s_["tanh_done"], 1)
            v_.tensor_scalar(gbias[:], gbias[:], tg[:, 0:1], None, ALU.mult).then_inc(s_["gb_done"], 1)
            dve.wait_ge(s_["w_hi"], 7)
            v_.tensor_tensor(wo_s[:, 1, :, :], wraw2[:, 2:4, :], wo_s[:, 0, :, :], ALU.subtract).then_inc(s_["w_lo"], 1)
            dve.wait_ge(s_["pool_set"], 1)

            def x_stats(b):
                v_.bn_stats(st1[:, b, :], xin[:, b, :]).then_inc(s_["ln1_st"], 1)

            def stats_2(st, mv, st_sem, mv_sem, g, k):
                wait(dve, s_[st_sem], g.count(GB, GB))
                carry(2 * k + g.par)
                for b in range(GB):
                    v_.bn_aggr(mv[:, b, :], st[:, b, :]).then_inc(s_[mv_sem], 1)

            def max_chunk(n1, c):
                dve.wait_ge(s_["s_ready"], n1.count(CHUNKS, c + 1))
                if c % 4 == 0:
                    wait(dve, s_["mt_ready"], n1.count(4, c // 4 - 3))
                b, cc = c // 4, c % 4
                v_.reduce_max(mx[:, b, CH * cc:CH * cc + CH], S[(c + 1) % 2][:].rearrange("p (h t) -> p h t", h=CH), X
                              ).then_inc(s_["s_max"], 1)

            def rank_post(r, n):
                link = s_["rk_link"]
                if n == 0:
                    dve.wait_ge(s_["rk_ready"], r.count(1, 1))
                    v_.tensor_tensor(posn[:], M[0][:, 0:GB * E].rearrange("p (b e) -> p b e", b=GB),
                                     run[:].unsqueeze(1).to_broadcast([P, GB, E]), ALU.add).then_inc(link, 1)
                    dve.wait_ge(link, r.count(3, 1))
                    v_.tensor_tensor(run[:], M[0][:, GB * E:GB * E + E], run[:], ALU.add).then_inc(s_["rk_read"], 1)
                    v_.tensor_tensor(posn[:], posn[:], hot[:], ALU.mult).then_inc(link, 1)
                if n == 1:
                    dve.wait_ge(link, r.count(3, 2))
                    v_.reduce_sum(pos[:], posn[:], X).then_inc(link, 1)
                if n == 2:
                    dve.wait_ge(link, r.count(3, 3))
                    pr = r.plus(-1)
                    if pr.real():
                        wait(dve, scat[pr.par], pr.halved(16 * GB, 16 * GB))
                    v_.tensor_copy(posi[:], pos[:]).then_inc(s_["pos_done"], 1)
                    dve.wait_ge(s_["rk_read"], r.count(1, 1))

            def lo_part(dst, src, hi, ready, n, done, bias=None):
                dve.wait_ge(s_[ready], n)
                if bias is None:
                    v_.tensor_tensor(dst, src, hi, ALU.subtract).then_inc(s_[done], 1)
                else:
                    v_.scalar_tensor_tensor(out=dst, in0=src, scalar=bias, in1=hi, op0=ALU.add,
                                            op1=ALU.subtract).then_inc(s_[done], 1)

            def logits(f):
                dve.wait_ge(s_["lg_ready"], f.count(1, 1))
                v_.scalar_tensor_tensor(out=lg[:], in0=S[0][:, 0:GB * E].rearrange("p (b e) -> p b e", b=GB), scalar=1.0 / WS,
                                        in1=rb_b[:].unsqueeze(1).to_broadcast([P, GB, E]), op0=ALU.mult, op1=ALU.add
                                        ).then_inc(s_["lg_done"], 1)

            def route(r, n):
                link = s_["route"]
                ranks_e = rank_e[:].unsqueeze(1).to_broadcast([P, GB, E])
                if n == 0:
                    dve.wait_ge(s_["lg_done"], r.count(1, 1))
                    v_.reduce_max(lmax[:], lg[:], X).then_inc(link, 1)
                if n == 1:
                    dve.wait_ge(link, r.count(5, 1))
                    v_.tensor_tensor(pick[:], lg[:], lmax[:].unsqueeze(2).to_broadcast([P, GB, E]), ALU.is_ge).then_inc(link, 1)
                if n == 2:
                    dve.wait_ge(link, r.count(5, 2))
                    v_.tensor_tensor(pick[:], pick[:], ranks_e, ALU.mult).then_inc(link, 1)
                if n == 3:
                    dve.wait_ge(link, r.count(5, 3))
                    v_.reduce_max(first[:], pick[:], X).then_inc(link, 1)
                if n == 4:
                    dve.wait_ge(link, r.count(5, 4))
                    v_.tensor_tensor(hot[:], ranks_e, first[:].unsqueeze(2).to_broadcast([P, GB, E]),
                                     ALU.is_equal).then_inc(link, 1)
                if n == 5:
                    dve.wait_ge(link, r.count(5, 5))
                    v_.tensor_tensor(hots[:], hot[:], sign_e[:].unsqueeze(1).to_broadcast([P, GB, E]), ALU.mult
                                     ).then_inc(s_["hot_done"], 1)

            def step(s):
                nxt, a, n1, g, f, r = s.plus(3), s.plus(2), s.plus(1), s, s.plus(-1), s.plus(-2)
                for c in range(CHUNKS):
                    if n1.real():
                        max_chunk(n1, c)
                    if f.real() and c < GB:
                        v_.bn_stats(st2[:, c, :], x2[:, f.par, c, 0:D]).then_inc(s_["ln2_st"], 1)
                    if f.real() and c == GB:
                        wait(dve, s_["xn2_done"], f.count(1))
                        stats_2(st2, mv2, "ln2_st", "ln2_mv", f, 1)
                    if r.real() and c < 6:
                        route(r, c)
                    if r.real() and 8 <= c < 11:
                        rank_post(r, c - 8)
                if a.real():
                    for t in range(KT):
                        lo_part(xt[:, 1, t, :], M[t][:], xt[:, 0, t, :], "xt_hi", a.count(2, t + 1), "xt_lo")
                if nxt.real():
                    dve.wait_ge(x_in[nxt.par], nxt.halved(16, 16))
                    wait(dve, s_["xn_done"], nxt.count(1))
                    x_stats(0)
                if a.real():
                    for t in range(KT):
                        lo_part(ks[:, 1, t, :], ST[t][:], ks[:, 0, t, :], "k_hi", a.count(2, t + 1), "k_lo", bqk8[:, 1, t:t + 1])
                        if nxt.real():
                            x_stats(1 + t)
                elif nxt.real():
                    x_stats(1)
                    x_stats(2)
                if nxt.real():
                    x_stats(3)
                if a.real():
                    for t in range(KT):
                        lo_part(qs[:, 1, t, :], M[t][:], qs[:, 0, t, :], "q_hi", a.count(2, t + 1), "q_lo", bqk8[:, 0, t:t + 1])
                if g.real():
                    banks = [bank[:].rearrange("p (h d) -> p h d", d=32) for bank in (S[0], S[1], AV[0], AV[1])]
                    for b in range(GB):
                        dve.wait_ge(s_["o_ready"], g.count(4, b + 1))
                        v_.reciprocal(rec[:, b, :], banks[b][:, :, DH]).then_inc(s_["nrm_r"], 1)
                    for b in range(GB):
                        dve.wait_ge(s_["nrm_r"], g.count(4, b + 1))
                        v_.tensor_tensor(an[:, b, :].rearrange("p (h d) -> p h d", d=DH), banks[b][:, :, 0:DH],
                                         rec[:, b, :].unsqueeze(2).to_broadcast([P, HEADS, DH]), ALU.mult
                                         ).then_inc(s_["nrm_done"], 1)
                if nxt.real():
                    stats_2(st1, mv1, "ln1_st", "ln1_mv", nxt, 0)
                if g.real():
                    for t in range(KT):
                        lo_part(at[:, 1, t, :], S[t][:], at[:, 0, t, :], "at_hi", g.count(2, t + 1), "at_lo")
                if f.real():
                    for t in range(KT):
                        lo_part(x2t[:, KT + t, :], AV[t][:], x2t[:, t, :], "x2t_hi", f.count(2, t + 1), "x2t_lo")
                if g.real():
                    dve.wait_ge(s_["xb_done"], g.count(1, 1))
                    pg = g.plus(-2)
                    if pg.real():
                        wait(dve, scat[pg.par], pg.halved(16 * GB, 16 * GB))
                    for t in range(2):
                        dve.wait_ge(s_["y_ready"], g.count(2, t + 1))
                        v_.scalar_tensor_tensor(out=x2[:, g.par, 2 * t:2 * t + 2, 0:D],
                                                in0=M[t][:].rearrange("p (b n) -> p b n", b=2), scalar=1.0 / WS,
                                                in1=xres[:, 2 * t:2 * t + 2, :], op0=ALU.mult, op1=ALU.add
                                                ).then_inc(s_["x2_done"], 1)
                if f.real():
                    logits(f)
                if g.real():
                    dve.wait_ge(s_["x2_done"], g.count(2, 2))

            schedule(dve, step)

            link, n = s_["t_link"], [0]

            def then(ins):
                n[0] += 1
                ins.then_inc(link, 1)
                dve.wait_ge(link, n[0])

            def floored(dst, src, add):
                then(v_.tensor_scalar(dst, src, float(add), 1.0 / P, ALU.add, ALU.mult))
                then(v_.tensor_scalar(dst, dst, -0.498, 8388608.0, ALU.add, ALU.add))
                then(v_.tensor_scalar(dst, dst, 8388608.0, None, ALU.subtract))

            dve.wait_ge(s_["rk_read"], GROUPS)
            then(v_.tensor_scalar(etmp[:, 0, :], sign_e[:], -1.0, (P - 1) / 2.0, ALU.add, ALU.mult))
            then(v_.tensor_tensor(etmp[:, 1, :], etmp[:, 0, :], run[:], ALU.add))
            v_.tensor_copy(prow[:], etmp[0:1, 1, :]).then_inc(s_["p_rows"], 1)
            v_.tensor_scalar(pidx[:], etmp[:, 1, :], jcol[:, 0:1], None, ALU.add).then_inc(s_["p_rows"], 1)
            dve.wait_ge(s_["p_rows"], 2)
            then(v_.tensor_tensor(cnt[:], run[:], base_e[:], ALU.subtract))
            then(v_.tensor_tensor(cnt[:], cnt[:], sign_e[:], ALU.mult))
            floored(til[:], cnt[:], P - 1)
            then(v_.tensor_tensor_scan(end[:], til[:], zero_e[:], 0.0, ALU.add, ALU.add))
            then(v_.tensor_scalar(ecmp[:], end[:], jcol[:, 0:1], None, ALU.is_le))
            then(v_.reduce_sum(eidx[:, 0:1], ecmp[:], X))
            then(v_.tensor_scalar(ehot[:], iota_e[:], eidx[:, 0:1], None, ALU.is_equal))
            then(v_.tensor_tensor(etmp[:, 3, :], end[:], til[:], ALU.subtract))
            then(v_.tensor_tensor(etmp[:, 0, :], etmp[:, 3, :], ehot[:], ALU.mult))
            then(v_.tensor_scalar(etmp[:, 3, :], sign_e[:], -1.0, (P - 1) / 2.0, ALU.add, ALU.mult))
            then(v_.tensor_tensor(etmp[:, 3, :], etmp[:, 3, :], base_e[:], ALU.add))
            then(v_.tensor_tensor(etmp[:, 1, :], etmp[:, 3, :], ehot[:], ALU.mult))
            then(v_.tensor_tensor(etmp[:, 2, :], sign_e[:], ehot[:], ALU.mult))
            then(v_.tensor_copy(etmp[:, 3, :], ehot[:]))
            then(v_.reduce_sum(ered[:], etmp[:], X))
            then(v_.tensor_scalar(eidx[:, 1:2], jcol[:], ered[:, 0:1], float(P), ALU.subtract, ALU.mult))
            then(v_.tensor_scalar(eidx[:, 1:2], eidx[:, 1:2], ered[:, 2:3], ered[:, 1:2], ALU.mult, ALU.add))
            then(v_.tensor_scalar(ered[:, 3:4], ered[:, 3:4], -float(PADS), float(PADS), ALU.mult, ALU.add))
            then(v_.tensor_tensor(eidx[:, 1:2], eidx[:, 1:2], ered[:, 3:4], ALU.add))
            v_.tensor_scalar(eidx[:, 0:1], eidx[:, 0:1], float(E - 1), None, ALU.min).then_inc(s_["t_cols"], 1)
            dve.wait_ge(s_["t_tr"], 1)
            then(v_.tensor_copy(trow[:, 1, :], M[0][0:1, P:2 * P]))
            packed = pick[0:1].rearrange("p b e -> p (b e)").rearrange("p (w n) -> p w n", n=PACK)
            then(v_.tensor_tensor(packed, M[0][0:1, 0:P].rearrange("p (w n) -> p w n", n=PACK), places[:], ALU.mult))
            then(v_.reduce_sum(ecmp[0:1, 0:TILES_PAD // PACK], packed, X))
            v_.tensor_copy(trow[:, 0, 0:TILES_PAD // PACK], ecmp[0:1, 0:TILES_PAD // PACK]).then_inc(s_["t_rows"], 1)

            def normed(t):
                j, n, lap, e = t
                dve.wait_ge(t_in[n], lap * 16 + 16)
                wait(dve, s_["f_t"], j + (-1))
                v_.tensor_scalar(gn[:, n % 2, :], gt[:, n, 0:D], gt[:, n, D:D + 1], gt[:, n, D + 1:D + 2],
                                 ALU.mult, ALU.add).then_inc(s_["f_norm"], 1)

            def moved_lo(t):
                j, n, lap, e = t
                dve.wait_ge(s_["f_hi"], j + 1)
                v_.tensor_tensor(gx[:, n % 2, 1, :, :], S[n % 2][:, 0:D].rearrange("p (k t) -> p k t", k=KT),
                                 gx[:, n % 2, 0, :, :], ALU.subtract).then_inc(s_["f_lo"], 1)

            def hidden_lo(t):
                j, n, lap, e = t
                dve.wait_ge(s_["f_hr"], j + 1)
                v_.tensor_tensor(hs[H:P, n % 2, :], hr[H:P, n % 2, :], hs[H:P, n % 2, :], ALU.subtract
                                 ).then_inc(s_["f_hlo"], 1)

            def finish(t):
                j, n, lap, e = t
                dve.wait_ge(s_["f_yr"], j + 1)
                wait(dve, t_out[n], lap * 16)
                v_.scalar_tensor_tensor(out=yo[n], in0=yr[:, n % 2, :], scalar=tg[:, 1:2], in1=gt[:, n, 0:D],
                                        op0=ALU.mult, op1=ALU.add)
                v_.tensor_copy(ido[:, n:n + 1], gt[:, n, D + 2:D + 3].bitcast(U32)).then_inc(s_["f_out"], 1)

            def fstep(at_):
                for d, stage in ((1, normed), (0, moved_lo), (-2, hidden_lo), (-4, finish)):
                    t = at_(d)
                    if t is not None:
                        stage(t)

            tiles_schedule(dve, fstep, lead=1)

        @block.tensor
        def _(pe):
            t_ = nc.tensor
            pe.wait_ge(s_["bv_wide"], 1)
            pe.wait_ge(s_["w_in2"], 32)
            for t in range(KT):
                last = t_.matmul(AV[0][:, 0:D], bvb[:, t, :], wraw2[:, 2 + t, :], start=(t == 0), stop=(t == KT - 1))
            last.then_inc(s_["bvwo_ready"], 1)
            pe.wait_ge(s_["pool_set"], 1)
            pe.wait_ge(s_["w_lo"], 5)

            def scores(n1, c):
                b, cc = c // 4, c % 4
                if c == 0:
                    pe.wait_ge(stk[n1.par], n1.halved(128, 128))
                    wait(pe, s_["at_lo"], n1.count(2, -2))
                if c == 1:
                    wait(pe, s_["lg_done"], n1.count(1, -2))
                if c >= 2:
                    pe.wait_ge(s_["s_max"], n1.count(CHUNKS, c - 1))
                for i in range(CH):
                    hp = CH * (cc % 2) + i
                    last = t_.matmul(S[(c + 1) % 2][:, i * P:(i + 1) * P], qstk[0:STACK, n1.par, hp, b * P:(b + 1) * P],
                                     kstk[0:STACK, n1.par, cc // 2, hp, b * P:(b + 1) * P], start=True, stop=True)
                last.then_inc(s_["s_ready"], 1)

            def scores_t(g, c):
                b, cc = c // 4, c % 4
                if c == 0:
                    pe.wait_ge(m_in[g.par], g.halved(32, 32))
                    nv = g.plus(1)
                    pe.wait_ge(s_["v_done"], nv.count(2, 2) if nv.real() else 2 * GROUPS)
                if c >= 2:
                    pe.wait_ge(s_["exp_done"], g.count(CHUNKS, c - 1))
                for i in range(CH):
                    hp = CH * (cc % 2) + i
                    last = t_.matmul(ST[c % 2][:, i * P:(i + 1) * P],
                                     kstk[0:STACK + 2, g.par, cc // 2, hp, b * P:(b + 1) * P],
                                     qstk[0:STACK + 2, g.par, hp, b * P:(b + 1) * P], start=True, stop=True)
                last.then_inc(s_["st_ready"], 1)

            def times_v(g, c):
                b, cc = c // 4, c % 4
                pe.wait_ge(s_["exp_done"], g.count(CHUNKS, c + 1))
                if cc == 0:
                    if b >= 2:
                        pe.wait_ge(s_["av_out"], g.count(4, b - 1))
                    else:
                        wait(pe, s_["x2t_lo"], g.count(2, -4 + b + 1))
                        wait(pe, s_["nrm_done"], g.count(4))
                for i in range(CH):
                    h = (b * HEADS + CH * cc + i) * 32
                    last = t_.matmul(AV[b % 2][32 * i:32 * i + 32, cc * P:(cc + 1) * P], v[:, g.par, h:h + 32],
                                     pt[:, c % NPT, i * P:(i + 1) * P], start=True, stop=True)
                last.then_inc(s_["av_ready"], 1)

            def max_t(n1, b):
                pe.wait_ge(s_["s_max"], n1.count(CHUNKS, 4 * b + 4))
                if b < 2:
                    wait(pe, s_["x2_done"], n1.count(2, -2))
                    r = n1.plus(-3)
                    if b == 1 and r.real():
                        wait(pe, s_["rk_read"], r.count(1, 1))
                elif b == 2:
                    pe.wait_ge(s_["m_done"], n1.count(4, 1))
                bank = S[0] if b == 3 else M[(b + 1) % 2]
                t_.transpose(bank[0:HEADS, 0:P], mx[:, b, :], ident[:]).then_inc(s_["mt_ready"], 1)

            def normed_t(a, n1, t):
                if t == 0:
                    pe.wait_ge(s_["xn_done"], a.count(1, 1))
                if n1.real():
                    pe.wait_ge(s_["m_done"], n1.count(4, 2 + t))
                for b in range(GB):
                    last = t_.transpose(M[t][:, b * P:(b + 1) * P], xn[:, b, t * P:(t + 1) * P], ident[:])
                last.then_inc(s_["xt_ready"], 1)

            def ranks(r):
                pe.wait_ge(s_["hot_done"], r.count(1, 1))
                pe.wait_ge(s_["x2_done"], min_groups(r.plus(1), 2))
                oh = hots[:].rearrange("p b e -> p (b e)")
                t_.matmul(M[0][:, 0:GB * E], tri[:], oh, start=True, stop=False)
                for b in range(1, GB):
                    last_b = b == GB - 1
                    t_.matmul(M[0][:, b * E:GB * E], ones[:], oh[:, 0:(GB - b) * E], start=False, stop=last_b)
                for b in range(GB):
                    last = t_.matmul(M[0][:, GB * E:GB * E + E], ones[:], oh[:, b * E:(b + 1) * E],
                                     start=(b == 0), stop=(b == GB - 1))
                last.then_inc(s_["rk_ready"], 1)

            def min_groups(g, per):
                return g.count(per, per) if g.real() else per * GROUPS

            def split_matmul(bank, pairs):
                for n, (w, m) in enumerate(pairs):
                    last = t_.matmul(bank, w, m, start=(n == 0), stop=(n == len(pairs) - 1))
                return last

            THREE = ((0, 0), (1, 0), (0, 1))

            def step(s):
                a, n1, g, f, r = s.plus(2), s.plus(1), s, s.plus(-1), s.plus(-2)
                for c in range(CHUNKS + 1):
                    if n1.real() and c < CHUNKS:
                        scores(n1, c)
                    if c == 7 and r.real():
                        ranks(r)
                    if g.real() and c < CHUNKS:
                        scores_t(g, c)
                    if g.real() and 1 <= c <= CHUNKS:
                        times_v(g, c - 1)
                    if n1.real() and c in MAX_T:
                        max_t(n1, MAX_T[c])
                    if a.real() and c in (14, 15):
                        normed_t(a, n1, c - 14)
                if a.real():
                    pe.wait_ge(s_["y_hi"], a.count(3, 3))
                    if g.real():
                        pe.wait_ge(s_["exp_done"], g.count(CHUNKS, CHUNKS))
                    elif n1.real():
                        pe.wait_ge(s_["v_done"], n1.count(2, 2))
                for m in range(2):
                    if a.real():
                        col = slice(m * P, (m + 1) * P)
                        split_matmul(ST[m][:], [(wk_s[:, i, t, col], ys[:, j, :]) for i, t, j in
                                                ((0, 0, 0), (1, 0, 0), (0, 0, 1), (0, 1, 2), (1, 1, 2))]
                                     ).then_inc(s_["k_ready"], 1)
                    if n1.real() and m == 0:
                        max_t(n1, 3)
                if a.real():
                    pe.wait_ge(s_["xt_lo"], a.count(2, 2))
                    for m in range(2):
                        split_matmul(M[m][:], [(wq_s[:, i, t, m * P:(m + 1) * P], xt[:, j, t, :])
                                               for t in range(KT) for i, j in THREE]).then_inc(s_["q_ready"], 1)
                if g.real():
                    banks = [S[0], S[1], AV[0], AV[1]]
                    wait(pe, s_["s_max"], CHUNKS * GROUPS if not n1.real() else n1.count(CHUNKS, CHUNKS))
                    pe.wait_ge(s_["av_out"], g.count(4, 4))
                    if n1.real():
                        pe.wait_ge(s_["m_done"], n1.count(4, 4))
                    for b in range(GB):
                        for cc in range(4):
                            last = t_.transpose(banks[b][:, cc * P:(cc + 1) * P], ot[:, b, cc * P:(cc + 1) * P], ident[:])
                        last.then_inc(s_["o_ready"], 1)
                if a.real():
                    pe.wait_ge(s_["k_lo"], a.count(2, 2))
                    for b in range(GB):
                        tok = slice(b * P, (b + 1) * P)
                        last = split_matmul(ST[b // 2][:, (b % 2) * D:(b % 2) * D + D],
                                            [(ys[:, j, tok], wv_s[:, i, t, :]) for i, t, j in
                                             ((0, 0, 0), (1, 0, 0), (0, 0, 1), (0, 1, 2), (1, 1, 2))])
                        if b % 2:
                            last.then_inc(s_["v_ready"], 1)
                if g.real():
                    pe.wait_ge(s_["nrm_done"], g.count(4, 4))
                    for t in range(KT):
                        for b in range(GB):
                            last = t_.transpose(S[t][:, b * P:(b + 1) * P], an[:, b, t * P:(t + 1) * P], ident[:])
                        last.then_inc(s_["at_ready"], 1)
                if f.real():
                    pe.wait_ge(s_["xn2_done"], f.count(1, 1))
                    for t in range(KT):
                        for b in range(GB):
                            last = t_.transpose(AV[t][:, b * P:(b + 1) * P], xn2[:, b, t * P:(t + 1) * P], ident[:])
                        last.then_inc(s_["x2t_ready"], 1)
                if g.real():
                    pe.wait_ge(s_["at_lo"], g.count(2, 2))
                    if a.real():
                        pe.wait_ge(s_["q_lo"], a.count(2, 2))
                    elif n1.real():
                        pe.wait_ge(s_["m_done"], n1.count(4, 4))
                    elif r.real():
                        pe.wait_ge(s_["rk_read"], r.count(1, 1))
                    for b in range(GB):
                        tok = slice(b * P, (b + 1) * P)
                        last = split_matmul(M[b // 2][:, (b % 2) * D:(b % 2) * D + D],
                                            [(at[:, i, t, tok], wo_s[:, j, t, :]) for t in range(KT) for i, j in THREE])
                        if b % 2:
                            last.then_inc(s_["y_ready"], 1)
                if f.real():
                    pe.wait_ge(s_["x2t_lo"], f.count(2, 2))
                    for b in range(GB):
                        tok = slice(b * P, (b + 1) * P)
                        last = split_matmul(S[0][:, b * E:(b + 1) * E],
                                            [(x2t[:, i * KT + t, tok], rw_s[:, j, t, :]) for t in range(KT) for i, j in THREE])
                    last.then_inc(s_["lg_ready"], 1)

            schedule(pe, step)

            pe.wait_ge(s_["t_cols"], 1)
            for n in range(2):
                last = t_.transpose(M[0][0:1, n * P:(n + 1) * P], eidx[:, n:n + 1], ident[:])
            last.then_inc(s_["t_tr"], 1)
            pe.wait_ge(s_["t_rows"], 1)
            pe.wait_ge(s_["ew_lo"], 2 * GROUPS)
            pe.wait_ge(s_["ew_hi"], 2 * GROUPS)
            pe.wait_ge(s_["b2_rows"], 32)

            def moved(t):
                j, n, lap, e = t
                pe.wait_ge(s_["f_norm"], j + 1)
                wait(pe, s_["f_lo"], j + (-1))
                for k in range(KT):
                    last = t_.transpose(S[n % 2][:, k * P:(k + 1) * P], gn[:, n % 2, k * P:(k + 1) * P], ident[:])
                last.then_inc(s_["f_t"], 1)

            def hidden(t):
                j, n, lap, e = t
                pe.wait_ge(s_["f_lo"], j + 1)
                wait(pe, s_["f_hr"], j + (-1))
                split_matmul(ST[n % 2][:, 0:P],
                             [(w1s[:, i, bass.ds(e + k * P, P)], gx[:, n % 2, m, k, :])
                              for k in range(KT) for i, m in THREE]).then_inc(s_["f_h"], 1)

            def output(t):
                j, n, lap, e = t
                pe.wait_ge(s_["f_hlo"], j + 1)
                wait(pe, s_["f_yr"], j + (-1))
                cols = bass.ds(e, D)
                bank = AV[n % 2][:, 0:D]
                t_.matmul(bank, ones16[:], b2s[:, cols], start=True, stop=False)
                t_.matmul(bank, hs[:, n % 2, :], w2s[:, 0, cols], start=False, stop=False)
                t_.matmul(bank, hs[:, n % 2, :], w2s[:, 1, cols], start=False, stop=True).then_inc(s_["f_y"], 1)

            def fstep(at_):
                t0, t1, t3 = at_(0), at_(-1), at_(-3)
                if t0 is not None:
                    moved(t0)
                if t1 is not None:
                    hidden(t1)
                if t3 is not None:
                    output(t3)

            tiles_schedule(pe, fstep, lead=0, experts=(-1, -3), scale=D)


def kernel(x, ctx_768, g_xattn, g_ffn, L0_xattn_wq, L0_xattn_bq, L0_xattn_wk, L0_xattn_bk, L0_xattn_wv, L0_xattn_bv,
           L0_xattn_wo, L0_xattn_bo, L0_ffn_router_w, L0_ffn_router_b, L0_ffn_weights1, L0_ffn_bias1,
           L0_ffn_weights2, L0_ffn_bias2):
    import numpy as np
    import concourse.bacc as bacc
    from concourse.bass_utils import run_bass_kernel_spmd

    def arr(a):
        return np.ascontiguousarray(np.asarray(a))

    def tail_twice(a):
        a = np.asarray(a)
        return np.ascontiguousarray(np.concatenate([a, a[P:DC]], axis=0))

    def twice(a):
        return np.concatenate([a, a], axis=0)

    w1 = np.asarray(L0_ffn_weights1)
    w2 = np.asarray(L0_ffn_weights2)
    arrays = {
        "x": arr(x),
        "ctx_t": tail_twice(np.asarray(ctx_768).reshape(TOKENS, DC).T),
        "g2": arr(np.concatenate([np.asarray(g_xattn), np.asarray(g_ffn)])),
        "wq": arr(L0_xattn_wq),
        "bq": arr(np.asarray(L0_xattn_bq).reshape(KT, P).T),
        "wk": tail_twice(L0_xattn_wk),
        "bk": arr(np.asarray(L0_xattn_bk).reshape(KT, P).T),
        "wv": tail_twice(L0_xattn_wv),
        "bv": arr(np.asarray(L0_xattn_bv).reshape(KT, P).T),
        "wo": arr(L0_xattn_wo),
        "bo": arr(L0_xattn_bo),
        "rw": arr(np.asarray(L0_ffn_router_w).T),
        "rb": arr(L0_ffn_router_b),
        "w1": arr(w1.reshape(E, KT, P, H).transpose(2, 0, 1, 3).reshape(P, E * KT * H)),
        "b1": arr(twice(np.asarray(L0_ffn_bias1).T)),
        "w2": arr(twice(w2.transpose(1, 0, 2).reshape(H, E * D))),
        "b2": arr(L0_ffn_bias2),
    }
    nc = bacc.Bacc("TRN2", target_bir_lowering=False, num_devices=1)
    args = [nc.dram_tensor(name, a.shape, mybir.dt.from_np(a.dtype), kind="ExternalInput").ap() for name, a in arrays.items()]
    out = nc.dram_tensor("out", (TOKENS, D), F32, kind="ExternalOutput").ap()
    build(nc, *args, out)
    r = run_bass_kernel_spmd(nc, [arrays], core_ids=[0])
    return r.results[0]["out"].reshape(BATCHES, P, D)
```
